# Optimizing a Trainium2 kernel written in Bass

```python
import numpy as np
import jax
import jax.numpy as jnp

def _softmax(x, axis=-1):
    return jax.nn.softmax(x, axis=axis)

def _gelu(x):
    return jax.nn.gelu(x, approximate=True)

def _silu(x):
    return jax.nn.silu(x)

def _sigmoid(x):
    return jax.nn.sigmoid(x)

def _layernorm(x, axis=-1, eps=1e-05):
    m = jnp.mean(x, axis=axis, keepdims=True)
    v = jnp.var(x, axis=axis, keepdims=True)
    return (x - m) / jnp.sqrt(v + eps)

def _scatter_add(tgt, idx, src, axis=0):
    return tgt.at[idx].add(src)

def _segment_sum(src, seg, n):
    return jax.ops.segment_sum(src, seg, n)
kernel_name = 'mk_xattn_ffn_d1_seqx_r2_e051e2'

def setup_inputs(seed: int=0):
    np.random.seed(seed)
    _w = jnp.asarray

    def _rec_inputs():
        import jax
        import jax.numpy as jnp
        _rk = jax.random.key(seed)
        x = -0.0003929 + 0.9999 * jax.random.normal(jax.random.fold_in(_rk, 1), (8, 224, 1024), jnp.float32)
        _lenS = 224 - jax.random.randint(jax.random.fold_in(_rk, 7), (8,), 0, max(1, 224 // 4) + 1, jnp.int32)
        _lenS2 = 750 - jax.random.randint(jax.random.fold_in(_rk, 8), (8,), 0, max(1, 750 // 4) + 1, jnp.int32)
        _ctx_2048P = jax.random.normal(jax.random.fold_in(_rk, 11), (8, 16, 1024), jnp.float32)
        _ctx_2048c = jax.random.dirichlet(jax.random.fold_in(_rk, 511), 0.3 * jnp.ones((16,), jnp.float32), (8, 750))
        _ctx_2048t = jnp.einsum('bsk,bkd->bsd', _ctx_2048c, _ctx_2048P)
        _ctx_2048t = _ctx_2048t * jax.lax.rsqrt(jnp.mean(jnp.square(_ctx_2048t)) + 1e-12) * 0.953939
        ctx_2048 = -1.39393e-06 + 0.999914 * (_ctx_2048t + 0.3 * jax.random.normal(jax.random.fold_in(_rk, 611), (8, 750, 1024), jnp.float32))
        itok_BxS_0_1023 = jax.random.randint(jax.random.fold_in(_rk, 12), (8, 224), 0, 512, jnp.int32)
        return (x, ctx_2048, itok_BxS_0_1023)
    x, ctx_2048, itok_BxS_0_1023 = _rec_inputs()

    def _L0_xattn_setup():
        import jax, jax.numpy as jnp
        import numpy as np
        B, Lq, Lk = (2, 2048, 512)
        Q_DIM, KV_DIM = (1024, 1024)
        H, HD = (16, 128)
        KVC, QC, R = (256, 384, 64)
        LOOKBACK = 8
        NEG = -1e+30

        def _rope(x, L):
            half = x.shape[-1] // 2
            inv_freq = 1.0 / 10000.0 ** (jnp.arange(half, dtype=jnp.float32) / half)
            ang = jnp.arange(L, dtype=jnp.float32)[:, None] * inv_freq
            cos, sin = (jnp.cos(ang), jnp.sin(ang))
            x1, x2 = (x[..., :half], x[..., half:])
            return jnp.concatenate([x1 * cos - x2 * sin, x1 * sin + x2 * cos], axis=-1)
        key = jax.random.key(seed)
        ks = jax.random.split(key, 11)

        def w(k, shape, fan_in):
            return jax.random.normal(k, shape, jnp.float32) / np.sqrt(fan_in).astype(np.float32)
        return {'q': jax.random.normal(ks[0], (B, Lq, Q_DIM), jnp.float32), 'kv': jax.random.normal(ks[1], (B, Lk, KV_DIM), jnp.float32), 'seg_id': jnp.sort(jax.random.randint(ks[2], (B, Lq), 0, Lk), axis=-1), 'W_kvc': w(ks[3], (KV_DIM, KVC), KV_DIM), 'W_dq': w(ks[4], (Q_DIM, QC), Q_DIM), 'W_uq': w(ks[5], (QC, H * HD), QC), 'W_qr': w(ks[6], (QC, H * R), QC), 'W_uk': w(ks[7], (KVC, H * HD), KVC), 'W_kr': w(ks[8], (KVC, R), KVC), 'W_uv': w(ks[9], (KVC, H * HD), KVC), 'W_o': w(ks[10], (H * HD, Q_DIM), H * HD)}
    _L0_xattn_all = _L0_xattn_setup()
    _L0_xattn_in = {k: v for k, v in _L0_xattn_all.items() if k in ('W_kvc', 'W_dq', 'W_uq', 'W_qr', 'W_uk', 'W_kr', 'W_uv', 'W_o')}
    del _L0_xattn_all

    def _L0_ffn_setup():
        import jax, jax.numpy as jnp
        import numpy as np

        def binarize_weight(w):
            alpha = jnp.mean(jnp.abs(w), axis=tuple(range(1, w.ndim)), keepdims=True)
            bw = jnp.where(w >= 0, 1.0, -1.0) * alpha
            return jax.lax.stop_gradient(bw - w) + w
        key = jax.random.key(seed)
        k1, k2, k3 = jax.random.split(key, 3)
        in_features, out_features = (1024, 1024)
        x = jax.random.normal(k1, (8, 1024, in_features), dtype=jnp.float32)
        std = np.sqrt(2.0 / out_features).astype(np.float32)
        weight = jax.random.normal(k2, (out_features, in_features), dtype=jnp.float32) * std
        bias = jax.random.normal(k3, (out_features,), dtype=jnp.float32) * 0.01
        return {'x': x, 'weight': weight, 'bias': bias}
    _L0_ffn_all = _L0_ffn_setup()
    _L0_ffn_in = {k: v for k, v in _L0_ffn_all.items() if k in ('weight', 'bias')}
    del _L0_ffn_all
    return {'x': x, 'ctx_2048': ctx_2048, 'itok_BxS_0_1023': itok_BxS_0_1023, 'L0_xattn_W_kvc': _L0_xattn_in['W_kvc'], 'L0_xattn_W_dq': _L0_xattn_in['W_dq'], 'L0_xattn_W_uq': _L0_xattn_in['W_uq'], 'L0_xattn_W_qr': _L0_xattn_in['W_qr'], 'L0_xattn_W_uk': _L0_xattn_in['W_uk'], 'L0_xattn_W_kr': _L0_xattn_in['W_kr'], 'L0_xattn_W_uv': _L0_xattn_in['W_uv'], 'L0_xattn_W_o': _L0_xattn_in['W_o'], 'L0_ffn_weight': _L0_ffn_in['weight'], 'L0_ffn_bias': _L0_ffn_in['bias']}

def reference(x, ctx_2048, itok_BxS_0_1023, L0_xattn_W_kvc, L0_xattn_W_dq, L0_xattn_W_uq, L0_xattn_W_qr, L0_xattn_W_uk, L0_xattn_W_kr, L0_xattn_W_uv, L0_xattn_W_o, L0_ffn_weight, L0_ffn_bias):
    import jax
    import jax.numpy as jnp

    def _L0_xattn_ref(q, kv, seg_id, W_kvc, W_dq, W_uq, W_qr, W_uk, W_kr, W_uv, W_o):
        import jax, jax.numpy as jnp
        import numpy as np
        B, Lq, Lk = (2, 2048, 512)
        Q_DIM, KV_DIM = (1024, 1024)
        H, HD = (16, 128)
        KVC, QC, R = (256, 384, 64)
        LOOKBACK = 8
        NEG = -1e+30

        def _rope(x, L):
            half = x.shape[-1] // 2
            inv_freq = 1.0 / 10000.0 ** (jnp.arange(half, dtype=jnp.float32) / half)
            ang = jnp.arange(L, dtype=jnp.float32)[:, None] * inv_freq
            cos, sin = (jnp.cos(ang), jnp.sin(ang))
            x1, x2 = (x[..., :half], x[..., half:])
            return jnp.concatenate([x1 * cos - x2 * sin, x1 * sin + x2 * cos], axis=-1)
        b, lq, _ = q.shape
        lk = kv.shape[1]
        kv_c = kv @ W_kvc
        q_c = q @ W_dq
        q_nope = (q_c @ W_uq).reshape(b, lq, H, HD).transpose(0, 2, 1, 3)
        q_rope = (q_c @ W_qr).reshape(b, lq, H, R).transpose(0, 2, 1, 3)
        k_nope = (kv_c @ W_uk).reshape(b, lk, H, HD)
        v = (kv_c @ W_uv).reshape(b, lk, H, HD)
        k_rope = kv_c @ W_kr
        q_rope = _rope(q_rope, lq)
        k_rope = _rope(k_rope, lk)
        scale = 1.0 / np.sqrt(HD + R).astype(np.float32)
        scores = (jnp.einsum('bhqd,bkhd->bhqk', q_nope, k_nope) + jnp.einsum('bhqr,bkr->bhqk', q_rope, k_rope)) * scale
        k_ids = jnp.arange(lk)[None, None, :]
        qs = seg_id[:, :, None]
        good = (k_ids <= qs) & (k_ids >= qs - LOOKBACK)
        scores = jnp.where(good[:, None, :, :], scores, NEG)
        attn = jax.nn.softmax(scores, axis=-1)
        out = jnp.einsum('bhqk,bkhd->bqhd', attn, v).reshape(b, lq, H * HD)
        return out @ W_o

    def _L0_ffn_ref(x, weight, bias):
        import jax, jax.numpy as jnp
        import numpy as np

        def binarize_weight(w):
            alpha = jnp.mean(jnp.abs(w), axis=tuple(range(1, w.ndim)), keepdims=True)
            bw = jnp.where(w >= 0, 1.0, -1.0) * alpha
            return jax.lax.stop_gradient(bw - w) + w
        bw = binarize_weight(weight)
        return jnp.einsum('bsi,oi->bso', x, bw) + bias
    x = x + _L0_xattn_ref(_layernorm(x, axis=-1), ctx_2048, itok_BxS_0_1023, L0_xattn_W_kvc, L0_xattn_W_dq, L0_xattn_W_uq, L0_xattn_W_qr, L0_xattn_W_uk, L0_xattn_W_kr, L0_xattn_W_uv, L0_xattn_W_o)
    x = x + _L0_ffn_ref(_layernorm(x, axis=-1), L0_ffn_weight, L0_ffn_bias)
    return x

_drawn_inputs = setup_inputs


def setup_inputs(seed=0):
    import zlib

    import numpy as np

    out = dict(_drawn_inputs(seed))
    spreads = {}
    factors = {'L0_ffn_bias': 8.0}
    for name, (base, spread) in spreads.items():
        noise = np.random.default_rng([zlib.crc32(name.encode()), seed]).standard_normal(out[name].shape)
        drawn = base * np.exp(spread * noise) if base else spread * noise
        out[name] = jnp.asarray(drawn.astype(out[name].dtype))
    for name, factor in factors.items():
        out[name] = (out[name] * factor).astype(out[name].dtype)
    return out
```

```python
import math

import concourse.bass as bass
from concourse import mybir
from contextlib import ExitStack

B, LQ, D = 8, 224, 1024
LK = 750
H, HD = 16, 128
KVC, QC, R = 256, 384, 64
LOOKBACK = 8
NEG = -1e30
EPS = 1e-5
SCALE = 1.0 / math.sqrt(HD + R)
HALF = R // 2

T = B * LQ
NS = 4
N = T // NS
BPS = B // NS
W = LOOKBACK + 1
QT_ = 14
TK = QT_ * W
NT = N // QT_
TPB = LQ // QT_
PAIRS = H // 2
PQ = PAIRS * QT_
HQ = H * QT_
KD, KC, KV = D // 128, QC // 128, KVC // 128
CK = 125
CPB = LK // CK
NC = BPS * CPB
ROWS = LK + 2
MEAN_ROW, MASKED_ROW = LK, LK + 1
KVR = KVC + R
TW = R + R + KVC + 1
GW = R + TW
GR = 8
PT_LAG, LAG = 4, 5

UW = 512
WR = 4
U_DQ, U_PAIR, U_WO, U_FF = 0, 8, 40, 88
UNITS = 104
SPLIT_UNITS = U_FF
G4 = 4
UPG = G4 + KD

C_ID, C_BM = 0, 128
C_QC = C_BM + TK
C_QS = C_QC + LQ
C_KCS = C_QS + LQ
C_ONE = C_KCS + CPB * R
C_W750 = C_ONE + 128
CW = C_W750 + 1
P_PERM, P_E14 = 0, 128
P_J = P_E14 + TK
P_BASE = P_J + 1
PW = P_BASE + NS * NT


def constants():
    import numpy as np
    c = np.zeros((128, CW), np.float32)
    c[:, C_ID:C_ID + 128] = np.eye(128)
    q_of_row = np.arange(PQ) % QT_
    q_of_key = np.arange(TK) // W
    c[:PQ, C_BM:C_BM + TK] = np.where(q_of_row[:, None] == q_of_key[None, :], 0.0, NEG)
    inv = (1.0 / np.float32(10000.0) ** (np.arange(HALF, dtype=np.float32) / np.float32(HALF))).astype(np.float32)
    ang = np.arange(LK, dtype=np.float32)[:, None] * inv
    cos, sin = np.cos(ang).astype(np.float32), np.sin(ang).astype(np.float32)
    c[:, C_QC:C_QC + LQ] = np.concatenate([cos[:LQ].T] * 4, 0)
    c[:, C_QS:C_QS + LQ] = np.concatenate([-sin[:LQ].T, sin[:LQ].T] * 2, 0)
    kcs = np.concatenate([cos, sin], 1).reshape(CPB, CK, R).transpose(1, 0, 2)
    c[:CK, C_KCS:C_KCS + CPB * R] = kcs.reshape(CK, -1)
    c[:, C_ONE:C_ONE + 128] = 1.0 / D
    c[:CK, C_W750] = np.float32(1.0) / np.float32(LK)
    p = np.zeros((128, PW), np.float32)
    r = np.arange(128)
    p[(r // R) * R + (r % R + HALF) % R, P_PERM + r] = 1.0
    p[q_of_key, P_E14 + np.arange(TK)] = 1.0
    p[:TK, P_J] = np.arange(TK) % W
    p[:, P_BASE:] = (np.arange(NS * NT) // TPB % BPS * ROWS)[None, :]
    return c, p


def program(nc, x, ctx, seg, kvc, kvct, kr, dq, uq, uk, qr, uv, wo, ff, ffn, bias, cst, pre, out):
    f32, f32r, i32 = mybir.dt.float32, mybir.dt.float32r, mybir.dt.int32
    ALU, ACT, AX = mybir.AluOpType, mybir.ActivationFunctionType, mybir.AxisListType
    ds = bass.ds

    table = nc.dram_tensor("key_table", (BPS * ROWS, TW), f32).ap()

    ctx_ = ExitStack()
    with ctx_:
        def sb(name, shape, dt=f32):
            return ctx_.enter_context(nc.sbuf_tensor(name, shape, dt))

        def sem(name):
            return ctx_.enter_context(nc.semaphore(name))

        BIG = sb("big", [128, KV * H * N + PAIRS * N])
        SPL = sb("split", [128, 2 * KD * N], f32r)
        X = sb("x_sb", [128, KD, N])
        QCS = sb("qc_split", [128, 2, KC, N], f32r)
        G = sb("gathered", [128, GR, GW])
        KT = sb("keys_t", [128, 2, 4 * TK])
        SOFT = sb("soft", [128, 2 * HQ + 4 * 2 * TK + 2 * HQ])
        WRAW = sb("w_raw", [128, WR, UW])
        WHI = sb("w_high", [128, WR, UW], f32r)
        WLO = sb("w_low", [128, WR, UW], f32r)
        KVW = sb("kv_weights", [128, 2, KD, KVR], f32r)
        C = sb("consts", [128, CW])
        PERM = sb("perm", [128, 128], f32r)
        ROW = sb("row", [128, 2, TW])
        RT = sb("row_rope_tmp", [128, 2, 2, R])
        IDX = sb("idx", [128, NS * NT], i32)
        IDXR = sb("idx_ring", [128, GR], i32)
        BIAS = sb("bias_sb", [128, KD])
        ALPHA, ALPHA2 = sb("alpha", [128, KD]), sb("alpha2", [128, KD])
        eps = sb("eps", [128, 1])
        PS = ctx_.enter_context(nc.psum_tensor("ps", [128, 8, 512], f32))

        QKV = BIG[:, 0:KV * H * N].rearrange("p (d h n) -> p d h n", d=KV, h=H)
        QKV2 = BIG[:, 0:KV * H * N].rearrange("p (e n) -> p e n", n=N)
        QR = BIG[:, KV * H * N:].rearrange("p (a n) -> p a n", a=PAIRS)
        CRAW = BIG[:, 0:4 * KD * CK].rearrange("p (b k n) -> p b (k n)", b=4, k=KD)
        o = 4 * KD * CK
        CEN = BIG[:, o:o + KD * N].rearrange("p (k n) -> p k n", k=KD)
        SQ = BIG[:, o + KD * N:o + 2 * KD * N].rearrange("p (k n) -> p k n", k=KD)
        CSPL = SPL[:, 0:3 * 2 * KD * CK].rearrange("p (b s n) -> p b s n", b=3, s=2)
        Y = SPL[:, :].rearrange("p (s k n) -> p s k n", s=2, k=KD)
        NOPE = SPL[:, 0:4 * N].rearrange("p (b s n) -> p b s n", b=2, s=2)
        RSP = SPL[:, 4 * N:6 * N].rearrange("p (s n) -> p s n", s=2)
        ATT = SPL[:, 0:2 * G4 * N].rearrange("p (s j n) -> p s j n", s=2, j=G4)
        CS = SPL[:, 2 * G4 * N:].rearrange("p (b s d n) -> p b s d n", b=2, s=2, d=KV)
        RSTD, VE = SOFT[:, 0:N], SOFT[:, N:2 * N]
        TMP = SOFT[:, 2 * N:4 * N].rearrange("p (b n) -> p b n", b=2)
        SSB = SOFT[:, 0:2 * HQ].rearrange("p (b n) -> p b n", b=2)
        SM = SOFT[:, 2 * HQ:2 * HQ + 8 * TK].rearrange("p (b e n) -> p b e n", b=4, e=2)
        PT = SOFT[:, 2 * HQ + 8 * TK:].rearrange("p (b n) -> p b n", b=2)
        STAT = sb("stat", [128, 2, 2, 2])
        SMAX, SSUM = STAT[:, :, 0, :], STAT[:, :, 1, :]
        IDENT, BM = C[:, C_ID:C_ID + 128], C[0:PQ, C_BM:C_BM + TK]
        ONES = C[:, C_ONE:C_ONE + 128]

        def psn(bank):
            return PS[:, bank, 0:N]

        const_dma, x_dma, out_dma = sem("const_dma"), sem("x_dma"), sem("out_dma")
        ctx_dma = [sem(f"ctx_dma{i}") for i in range(4)]
        w_dma = [sem(f"w_dma{i}") for i in range(WR)]
        g_dma = [sem(f"g_dma{i}") for i in range(GR)]
        row_dma = [sem(f"row_dma{i}") for i in range(2)]
        mean_dma, masked_dma = sem("mean_dma"), sem("masked_dma")
        credit = {}

        def csem(name, slots, owner):
            s_ = sem(name)
            credit[name] = (s_, slots, owner)
            return s_

        names = ("idx_seg idx_mm idx_chain idx_ready fold_mm w0_hi w0_lo perm_ready alpha_abs alpha_ready clear masked_set "
                 "ctx_hi ctx_lo tab_mm mean_ev mean_clear  "
                 "w_hi w_lo "
                 "ln_sum ln_mean_mm ln_sub ln_sq ln_sqsum ln_var_mm ln_ve ln_std ln_inv ln_n1 ln_n2 y_hi y_lo "
                 "qc_mm qc_f qc_hi qc_lo nope_hi nope_lo abs_mm rope_mm rp_hi rp_lo swap_mm "
                 "kt_mm sm_max sm_shift sm_exp sm_sum sm_rec sm_norm "
                 "cs_hi cs_lo att_hi ff_ab ff_add").split()
        S = {n_: sem(n_) for n_ in names}
        row_kv, row_rt, row_sum = csem("row_kv", 2, "act"), csem("row_rt", 2, "dve"), csem("row_sum", 2, "pool")
        mean_mm = csem("mean_mm", 1, "pe")
        w_used, w_sgn = csem("w_used", WR, "pe"), csem("w_sgn", WR, "dve")
        ln_rstd = csem("ln_rstd", 1, "dve")
        abs_even, abs_odd = csem("abs_even", 1, "act"), csem("abs_odd", 1, "dve")
        rope_t1, rope_t2, rope_ev = csem("rope_t1", 1, "dve"), csem("rope_t2", 1, "dve"), csem("rope_ev", 1, "pool")
        kt_ev, s_ev, sm_mask = csem("kt_ev", 1, "act"), csem("s_ev", 2, "act"), csem("sm_mask", 2, "dve")
        pt_ev, pv_ev = csem("pt_ev", 1, "act"), csem("pv_ev", 2, "dve")
        s_mm, st_mm, pt_mm, pv_mm = csem("s_mm", 2, "pe"), csem("st_mm", 2, "pe"), csem("pt_mm", 4, "pe"), csem("pv_mm", GR, "pe")
        att_lo, x_add = csem("att_lo", 2, "dve"), csem("x_add", 4, "dve")
        ff_t = csem("ff_t", 4, "dve")
        credit["out_dma"] = (out_dma, 16, "sp")

        def uv_unit(n):
            return U_WO + UPG * (n // G4) + n % G4

        def used(s, u):
            return s * UNITS + (u + 1 + WR)

        def give_credits(eng, who):
            for s_, slots, owner in credit.values():
                if owner == who:
                    eng.sem_inc(s_, slots)

        block = ctx_.enter_context(nc.Block())
        NCONST = 9

        def steps(eng, step, s, last):
            for i in range(GR):
                step(s, i, i)
            with eng.Fori(1, NT // GR) as k:
                for r in range(GR):
                    step(s, k * GR + r, r)
            for i in range(NT, last):
                step(s, i, i % GR)

        def has(i, lag):
            return not isinstance(i, int) or 0 <= i - lag < NT

        @block.sync
        def _(sp):
            give_credits(sp, "sp")
            sp.dma_start(C[:, :], cst).then_inc(const_dma, 16)
            sp.dma_start(BIG[:, 0:PW], pre).then_inc(const_dma, 16)
            sp.dma_start(BIG[0:QT_, 1024:1024 + NS * NT].bitcast(i32), seg).then_inc(const_dma, 16)
            sp.dma_start(BIG[:, 2048:2048 + KD * KVC], kvc).then_inc(const_dma, 16)
            sp.dma_start(BIG[:, 4096:4096 + KV * D], kvct).then_inc(const_dma, 16)
            sp.dma_start(BIG[:, 6144:6144 + KV * R], kr).then_inc(const_dma, 16)
            sp.dma_start(BIG[:, 8192:8192 + KD * D], ffn).then_inc(const_dma, 16)
            sp.dma_start(BIAS[:, :], bias).then_inc(const_dma, 16)
            sp.wait_ge(S["w0_lo"], 1)
            sp.wait_ge(S["idx_ready"], 1)
            sp.wait_ge(S["alpha_ready"], 1)
            sp.wait_ge(S["perm_ready"], 1)
            sp.wait_ge(masked_dma, 16)

            def unit(s, u, slot, src, width):
                if isinstance(u, int) and u < WR:
                    sp.wait_ge(w_sgn, s * 16 + u + 1)
                elif isinstance(u, int) and u >= U_FF + WR:
                    sp.wait_ge(w_sgn, s * 16 + (u - U_FF) + 1)
                else:
                    sp.wait_ge(S["w_lo"], s * SPLIT_UNITS + u - WR + 1)
                sp.dma_start(WRAW[:, slot, 0:width], src).then_inc(w_dma[slot], 16)

            with sp.Fori(0, NS) as s:
                sp.wait_ge(ln_rstd, s * 2 + 1)
                for c in range(4):
                    sp.dma_start(CRAW[:, c, :], ctx[ds(s * NC + c, 1), :, :].rearrange("a p n -> (a p) n")).then_inc(ctx_dma[c], 16)
                sp.wait_ge(out_dma, (s + 1) * 16)
                sp.dma_start(X[:, :, :].rearrange("p k n -> p (k n)"), x[ds(s, 1), :, :].rearrange("a p n -> (a p) n")).then_inc(x_dma, 16)
                for c in range(4, NC):
                    sp.wait_ge(S["ctx_lo"], s * NC + c - 3)
                    sp.dma_start(CRAW[:, c % 4, :], ctx[ds(s * NC + c, 1), :, :].rearrange("a p n -> (a p) n")).then_inc(ctx_dma[c % 4], 16)
                for u in range(U_PAIR):
                    unit(s, u, u % WR, dq[u], 3 * 128)
                with sp.Fori(0, PAIRS) as p:
                    u0 = p * 4 + U_PAIR
                    unit(s, u0, 0, uq[ds(p * 2, 1), :, :].rearrange("a p n -> (a p) n"), 3 * 128)
                    unit(s, u0 + 1, 1, uq[ds(p * 2 + 1, 1), :, :].rearrange("a p n -> (a p) n"), 3 * 128)
                    unit(s, u0 + 2, 2, uk[ds(p, 1), :, :].rearrange("a p n -> (a p) n"), 512)
                    unit(s, u0 + 3, 3, qr[ds(p, 1), :, :].rearrange("a p n -> (a p) n"), 3 * 128)
                for g in range(H // G4):
                    for v in range(UPG):
                        u = U_WO + UPG * g + v
                        unit(s, u, u % WR, *((uv[G4 * g + v], 256) if v < G4 else (wo[KD * g + v - G4], 512)))
                for v in range(2 * KD):
                    unit(s, U_FF + v, v % WR, ff[v], 512)
                sp.wait_ge(S["ff_add"], s * KD + KD)
                sp.dma_start(out[ds(s, 1), :, :].rearrange("a p n -> (a p) n"), X[:, :, :].rearrange("p k n -> p (k n)")).then_inc(out_dma, 16)
            sp.wait_ge(out_dma, 16 + 16 * NS)

        @block.gpsimd
        def _(pool):
            give_credits(pool, "pool")
            pool.memset(G[:, :, 0:R], 0.0).then_inc(S["clear"], 1)
            pool.memset(ROW[:, :, R:2 * R], 0.0).then_inc(S["clear"], 1)
            pool.memset(ROW[:, :, TW - 1:TW], 0.0).then_inc(S["clear"], 1)
            masked = BIG[0:BPS, 16800:16800 + TW]
            pool.memset(masked[:, 0:TW - 1], 0.0).then_inc(S["masked_set"], 1)
            pool.memset(masked[:, TW - 1:TW], NEG).then_inc(S["masked_set"], 1)
            pool.wait_ge(S["masked_set"], 2)
            pool.dma_start(table[MASKED_ROW:BPS * ROWS:ROWS, :], masked).then_inc(masked_dma, 16)

            def low(s, u, slot, width):
                pool.wait_ge(S["w_hi"], s * SPLIT_UNITS + u + 1)
                pool.tensor_tensor(WLO[:, slot, 0:width], WRAW[:, slot, 0:width], WHI[:, slot, 0:width].bitcast(f32),
                                   ALU.subtract).then_inc(S["w_lo"], 1)

            def gather(s, i, r):
                tile = s * NT + i
                pool.wait_ge(pv_mm, tile + 1)
                pool.tensor_copy(IDXR[0:TK, r:r + 1], IDX[0:TK, ds(tile, 1)])
                pool.drain()
                pool.indirect_dma_start(out=G[0:TK, r, R:GW], out_offset=None, in_=table,
                                        in_offset=bass.IndirectOffsetOnAxis(ap=IDXR[0:TK, r:r + 1], axis=0)).then_inc(g_dma[r], 16)

            pool.wait_ge(S["idx_ready"], 1)
            pool.wait_ge(S["clear"], 3)
            pool.wait_ge(masked_dma, 16)
            with pool.Fori(0, NS) as s:
                for c in range(NC):
                    b, t, e = c // CPB, c % CPB, c % 2
                    n = s * NC + c
                    pool.wait_ge(row_rt, n + 3)
                    pool.tensor_tensor(ROW[0:CK, e, 0:HALF], RT[0:CK, e, 0, 0:HALF], RT[0:CK, e, 1, HALF:R],
                                       ALU.subtract)
                    pool.tensor_tensor(ROW[0:CK, e, HALF:R], RT[0:CK, e, 0, HALF:R], RT[0:CK, e, 1, 0:HALF],
                                       ALU.add)
                    pool.wait_ge(row_kv, n + 3)
                    if c == 0:
                        pool.wait_ge(mean_mm, s + 1)
                        pool.wait_ge(pv_mm, s * NT + GR)
                    acc, kv = G[0:CK, b, R:R + KVC], ROW[0:CK, e, 2 * R:2 * R + KVC]
                    if t == 0:
                        pool.tensor_tensor(acc, kv, ROW[0:CK, e, R:R + 1].to_broadcast([CK, KVC]), ALU.add).then_inc(row_sum, 1)
                    else:
                        pool.wait_ge(row_sum, n + 2)
                        pool.tensor_tensor(acc, acc, kv, ALU.add).then_inc(row_sum, 1)
                    pool.drain()
                    pool.dma_start(table[b * ROWS + t * CK:b * ROWS + (t + 1) * CK, :], ROW[0:CK, e, :]).then_inc(row_dma[e], 16)
                pool.memset(G[0:1, 2:4, R:3 * R], 0.0).then_inc(S["mean_clear"], 1)
                pool.memset(G[0:1, 2:4, GW - 1:GW], 0.0).then_inc(S["mean_clear"], 1)
                for u in range(6):
                    low(s, u, u % WR, 384)
                pool.wait_ge(S["mean_clear"], s * 2 + 2)
                pool.wait_ge(S["mean_ev"], s + 1)
                low(s, 6, 6 % WR, 384)
                mean_rows = table.rearrange("(b r) w -> r b w", r=ROWS)[MEAN_ROW:MEAN_ROW + 1, :, :]
                pool.dma_start(mean_rows, G[0:1, 2:4, R:GW]).then_inc(mean_dma, 16)
                for u in range(7, 10):
                    low(s, u, u % WR, 384)

                def pair(p, widths):
                    for v, width in zip(range(2, 6), widths):
                        low(s, p * 4 + (U_PAIR + v), v % WR, width)
                    pool.wait_ge(rope_t1, s * PAIRS + p + 2)
                    pool.wait_ge(rope_t2, s * PAIRS + p + 2)
                    pool.tensor_tensor(QR[:, ds(p, 1), :], TMP[:, 0:1, :], TMP[:, 1:2, :], ALU.add).then_inc(rope_ev, 1)

                with pool.Fori(0, PAIRS - 1) as p:
                    pair(p, (512, 384, 384, 384))
                pair(PAIRS - 1, (512, 384, 256, 256))
                for e in range(2):
                    pool.wait_ge(row_dma[e], (s + 1) * (16 * NC // 2))
                pool.wait_ge(mean_dma, s * 16 + 16)
                steps(pool, gather, s, NT)
                for u in range(U_WO + 2, U_FF):
                    low(s, u, u % WR, 256 if (u - U_WO) % UPG < G4 else 512)
                for m in range(KD):
                    pool.wait_ge(S["ff_ab"], s * KD + m + 1)
                    pool.tensor_tensor(X[:, m, :], X[:, m, :], TMP[:, m % 2, :], ALU.add).then_inc(S["ff_add"], 1)

        @block.scalar
        def _(act):
            give_credits(act, "act")

            def high(s, u, slot, width):
                act.wait_ge(w_dma[slot], s * (UNITS // WR * 16) + (u // WR + 1) * 16)
                act.wait_ge(w_used, s * UNITS + u + 1)
                act.activation(WHI[:, slot, 0:width], WRAW[:, slot, 0:width], ACT.Copy).then_inc(S["w_hi"], 1)

            def high_in_pair(s, p, v, width):
                act.wait_ge(w_dma[v % WR], s * (UNITS // WR * 16) + p * 16 + (U_PAIR // WR + v // WR + 1) * 16)
                act.wait_ge(w_used, s * UNITS + p * 4 + (U_PAIR + v + 1))
                act.activation(WHI[:, v % WR, 0:width], WRAW[:, v % WR, 0:width], ACT.Copy).then_inc(S["w_hi"], 1)

            def norm_high(s, l, kp):
                act.wait_ge(S["ln_sub"], s * 8 + 4 * l + kp + 1)
                act.activation(Y[:, 0, 2 * kp:2 * kp + 2, :], CEN[:, 2 * kp:2 * kp + 2, :], ACT.Copy).then_inc(S["y_hi"], 1)

            def norm_square(s, l):
                act.wait_ge(S["ln_sub"], s * 8 + 4 * l + 4)
                act.activation(SQ[:, :, :], CEN[:, :, :], ACT.Square).then_inc(S["ln_sq"], 1)

            def norm_std(s, l):
                act.wait_ge(S["ln_var_mm"], s * 2 + l + 1)
                act.activation(VE, psn(3), ACT.Identity, bias=eps[:, :]).then_inc(S["ln_ve"], 1)
                act.wait_ge(S["ln_ve"], s * 2 + l + 1)
                act.activation(TMP[:, 0, :], VE, ACT.Sqrt).then_inc(S["ln_std"], 1)

            act.wait_ge(const_dma, 16 * 8)
            act.activation(PERM[:, :], BIG[:, P_PERM:P_PERM + 128], ACT.Copy).then_inc(S["perm_ready"], 1)
            act.activation(KVW[:, 0, :, 0:KVC], BIG[:, 2048:2048 + KD * KVC].rearrange("p (k n) -> p k n", k=KD),
                           ACT.Copy).then_inc(S["w0_hi"], 1)
            act.wait_ge(S["fold_mm"], 1)
            act.activation(KVW[:, 0, :, KVC:KVR], PS[:, 0, :].rearrange("p (k n) -> p k n", k=KD), ACT.Copy).then_inc(S["w0_hi"], 1)
            for m in range(KD):
                if m:
                    act.wait_ge(S["alpha_abs"], m)
                act.activation(BIG[:, 8192 + D * m:8192 + D * (m + 1)], BIG[:, 8192 + D * m:8192 + D * (m + 1)], ACT.Abs,
                               accum_out=ALPHA[:, m:m + 1]).then_inc(S["alpha_abs"], 1)
            act.wait_ge(S["alpha_abs"], KD)

            with act.Fori(0, NS) as s:
                def ctx_high(c):
                    n = s * NC + c
                    act.wait_ge(ctx_dma[c % 4], s * (16 * NC // 4) + (c // 4 + 1) * 16)
                    if c >= 3:
                        act.wait_ge(S["tab_mm"], n - 2)
                    elif c == 0:
                        act.wait_ge(w_used, used(s, -1))
                    act.activation(CSPL[:, c % 3, 0, :], CRAW[:, c % 4, :], ACT.Copy).then_inc(S["ctx_hi"], 1)

                ctx_high(0)
                ctx_high(1)
                for c in range(NC):
                    if c + 2 < NC:
                        ctx_high(c + 2)
                    n, e = s * NC + c, c % 2
                    act.wait_ge(S["tab_mm"], n + 1)
                    if c >= 2:
                        act.wait_ge(row_dma[e], s * (16 * NC // 2) + (c // 2) * 16)
                    act.wait_ge(row_sum, n + 1)
                    act.activation(ROW[0:CK, e, 2 * R:2 * R + KVC], PS[0:CK, e, 0:KVC], ACT.Copy).then_inc(row_kv, 1)
                    if c == 7:
                        norm_square(s, 0)
                    if c == 10:
                        norm_std(s, 0)
                for u in range(4):
                    high(s, u, u, 384)
                act.wait_ge(S["tab_mm"], s * NC + NC)
                for kp in range(4):
                    norm_high(s, 0, kp)
                for u in range(4, 6):
                    high(s, u, u % WR, 384)
                for m in range(KC):
                    act.wait_ge(S["qc_f"], s * KC + m + 1)
                    act.activation(QCS[:, 0, m, :], TMP[:, m % 2, :], ACT.Copy).then_inc(S["qc_hi"], 1)
                    if m == 0:
                        act.wait_ge(mean_mm, s + 2)
                        act.activation(G[0:1, 2:4, 3 * R:3 * R + KVC], PS[0:1, 7, :].rearrange("p (b n) -> p b n", b=BPS),
                                       ACT.Copy).then_inc(S["mean_ev"], 1)
                    for u in ((6,), (7, 8), (9,))[m]:
                        high(s, u, u % WR, 384)

                def pair(p, widths):
                    high_in_pair(s, p, 2, widths[0])
                    for h in range(2):
                        act.wait_ge(w_used, s * UNITS + p * 4 + (U_PAIR + h + 1 + WR))
                        act.activation(NOPE[:, h, 0, :], psn(h), ACT.Copy).then_inc(S["nope_hi"], 1)
                        if h == 0:
                            high_in_pair(s, p, 3, widths[1])
                    high_in_pair(s, p, 4, widths[2])
                    act.wait_ge(S["abs_mm"], s * H + p * 2 + 1)
                    act.activation(QKV[:, :, ds(p, 1), :].rearrange("p d a n -> p d (a n)"), PS[:, 2:4, 0:N], ACT.Copy).then_inc(abs_even, 1)
                    act.wait_ge(S["rope_mm"], s * PAIRS + p + 1)
                    act.activation(RSP[:, 0, :], psn(4), ACT.Copy).then_inc(S["rp_hi"], 1)
                    high_in_pair(s, p, 5, widths[3])

                with act.Fori(0, PAIRS - 1) as p:
                    pair(p, (512, 384, 384, 384))
                pair(PAIRS - 1, (512, 384, 256, 256))

                def step(s, i, r):
                    tile = s * NT + i
                    if has(i, 0):
                        act.wait_ge(S["kt_mm"], tile + 1)
                        act.wait_ge(s_mm, tile + 1)
                        act.activation(KT[:, r % 2, :], PS[:, 0, 0:4 * TK], ACT.Copy).then_inc(kt_ev, 1)
                    if has(i, 1):
                        n, q = tile - 1, (r - 1) % GR
                        act.wait_ge(s_mm, n + 3)
                        act.wait_ge(st_mm, n + 1)
                        act.activation(SSB[0:TK, q % 2, :], PS[0:TK, 1 + q % 2, 0:HQ], ACT.Identity,
                                       bias=G[0:TK, q, GW - 1:GW], scale=SCALE).then_inc(s_ev, 1)
                    if has(i, PT_LAG):
                        n, q = tile - PT_LAG, (r - PT_LAG) % GR
                        act.wait_ge(pt_mm, n + 5)
                        act.wait_ge(pv_mm, n + GR - 1)
                        act.activation(PT[0:TK, q % 2, :], PS[0:TK, 5, 0:HQ], ACT.Copy).then_inc(pt_ev, 1)
                    if has(i, 2):
                        n, q = tile - 2, (r - 2) % GR
                        act.wait_ge(S["sm_shift"], n + 1)
                        act.activation(SM[0:PQ, q % 4, :, :], SM[0:PQ, q % 4, :, :], ACT.Exp).then_inc(S["sm_exp"], 1)

                steps(act, step, s, NT + PT_LAG)

                act.wait_ge(pv_ev, s * NT + NT + 2)

                def sum_high(n):
                    if n >= 2:
                        act.wait_ge(w_used, used(s, uv_unit(n - 2)))
                    act.activation(CS[:, n % 2, 0, :, :], QKV[:, :, n, :], ACT.Copy).then_inc(S["cs_hi"], 1)

                sum_high(0)
                sum_high(1)
                high(s, U_WO + 2, 2, 256)
                high(s, U_WO + 3, 3, 256)
                for g in range(H // G4):
                    u = U_WO + UPG * g
                    for j in range(G4):
                        n = G4 * g + j
                        if j == 0:
                            act.wait_ge(w_used, used(s, u - 1))
                        act.wait_ge(w_used, used(s, u + j))
                        act.activation(ATT[:, 0, j, :], psn(n % 2), ACT.Copy).then_inc(S["att_hi"], 1)
                        if j < 2:
                            sum_high(n + 2)
                        high(s, u + G4 + j, (u + j) % WR, 512)
                    for v in range(2 * G4, UPG):
                        high(s, u + v, (u + v) % WR, 512)
                    if g + 1 < H // G4:
                        sum_high(G4 * (g + 1))
                        sum_high(G4 * (g + 1) + 1)
                        for v in range(UPG, UPG + G4):
                            high(s, u + v, (u + v) % WR, 256)
                act.wait_ge(w_used, used(s, U_FF - 1))
                for kp in range(4):
                    norm_high(s, 1, kp)
                norm_square(s, 1)
                norm_std(s, 1)
                for m in range(KD):
                    act.wait_ge(ff_t, s * KD + m + 5)
                    act.activation(TMP[:, m % 2, :], TMP[:, m % 2, :], ACT.Identity, bias=BIAS[:, m:m + 1],
                                   scale=ALPHA2[:, m:m + 1]).then_inc(S["ff_ab"], 1)

        @block.vector
        def _(dve):
            give_credits(dve, "dve")
            dve.memset(eps[:, :], EPS).then_inc(S["idx_chain"], 1)
            dve.wait_ge(const_dma, 16 * 8)
            segi = BIG[0:QT_, 1024:1024 + NS * NT].bitcast(i32)
            segf = BIG[0:QT_, 1152:1152 + NS * NT]
            k_, a_, b_, m_ = (BIG[0:TK, 1280 + 128 * i:1408 + 128 * i] for i in range(4))
            link = [1]

            def chain(ins):
                link[0] += 1
                ins.then_inc(S["idx_chain"], 1)
                dve.wait_ge(S["idx_chain"], link[0])

            chain(dve.tensor_copy(segf, segi))
            dve.tensor_scalar(segf, segf, -1.0, float(LK + LOOKBACK), ALU.max, ALU.min).then_inc(S["idx_seg"], 1)
            dve.wait_ge(S["idx_mm"], 1)
            chain(dve.tensor_scalar(a_, PS[0:TK, 1, 0:128], 0.0, None, ALU.is_ge))
            chain(dve.tensor_scalar(b_, PS[0:TK, 1, 0:128], float(LK - 1 + LOOKBACK), None, ALU.is_le))
            chain(dve.tensor_tensor(a_, a_, b_, ALU.mult))
            chain(dve.tensor_scalar(k_, PS[0:TK, 1, 0:128], BIG[0:TK, P_J:P_J + 1], None, ALU.subtract))
            chain(dve.tensor_scalar(b_, k_, 0.0, None, ALU.is_ge))
            chain(dve.tensor_scalar(m_, k_, float(LK - 1), None, ALU.is_le))
            chain(dve.tensor_tensor(b_, b_, m_, ALU.mult))
            chain(dve.scalar_tensor_tensor(out=b_, in0=k_, scalar=float(MASKED_ROW), in1=b_, op0=ALU.subtract, op1=ALU.mult))
            chain(dve.scalar_tensor_tensor(out=b_, in0=b_, scalar=float(MASKED_ROW - MEAN_ROW), in1=a_, op0=ALU.add, op1=ALU.mult))
            chain(dve.scalar_tensor_tensor(out=b_, in0=b_, scalar=float(MEAN_ROW), in1=BIG[0:TK, P_BASE:P_BASE + 128],
                                           op0=ALU.add, op1=ALU.add))
            dve.tensor_copy(IDX[0:TK, :], b_).then_inc(S["idx_ready"], 1)
            dve.wait_ge(S["w0_hi"], 2)
            chain(dve.tensor_tensor(KVW[:, 1, :, 0:KVC], BIG[:, 2048:2048 + KD * KVC].rearrange("p (k n) -> p k n", k=KD),
                                    KVW[:, 0, :, 0:KVC].bitcast(f32), ALU.subtract))
            dve.tensor_tensor(KVW[:, 1, :, KVC:KVR], PS[:, 0, :].rearrange("p (k n) -> p k n", k=KD),
                              KVW[:, 0, :, KVC:KVR].bitcast(f32), ALU.subtract).then_inc(S["w0_lo"], 1)
            dve.wait_ge(S["alpha_abs"], KD)
            dve.tensor_scalar(ALPHA2[:, :], ALPHA[:, :], 2.0 / D, None, ALU.mult).then_inc(S["alpha_ready"], 1)

            def norm_sum(s, l):
                dve.tensor_reduce(TMP[:, 0, :], X[:, :, :].rearrange("p k n -> p n k"), AX.X, ALU.add).then_inc(S["ln_sum"], 1)

            def norm_center(s, l, kp):
                if kp == 0:
                    dve.wait_ge(S["ln_mean_mm"], s * 2 + l + 1)
                dve.tensor_tensor(CEN[:, 2 * kp:2 * kp + 2, :], X[:, 2 * kp:2 * kp + 2, :],
                                  psn(2)[:, None, :].to_broadcast([128, 2, N]), ALU.subtract).then_inc(S["ln_sub"], 1)

            def norm_low(s, l, kp):
                dve.wait_ge(S["y_hi"], s * 8 + 4 * l + kp + 1)
                dve.tensor_tensor(Y[:, 1, 2 * kp:2 * kp + 2, :], CEN[:, 2 * kp:2 * kp + 2, :],
                                  Y[:, 0, 2 * kp:2 * kp + 2, :].bitcast(f32), ALU.subtract).then_inc(S["y_lo"], 1)

            def norm_sqsum(s, l):
                dve.wait_ge(S["ln_sq"], s * 2 + l + 1)
                dve.tensor_reduce(TMP[:, 1, :], SQ[:, :, :].rearrange("p k n -> p n k"), AX.X, ALU.add).then_inc(S["ln_sqsum"], 1)

            def norm_rstd(s, l):
                n = s * 2 + l
                dve.wait_ge(S["ln_std"], n + 1)
                dve.reciprocal(RSTD, TMP[:, 0, :]).then_inc(S["ln_inv"], 1)
                dve.wait_ge(S["ln_inv"], n + 1)
                dve.tensor_tensor(TMP[:, 1, :], RSTD, RSTD, ALU.mult).then_inc(S["ln_n1"], 1)
                dve.wait_ge(S["ln_n1"], n + 1)
                dve.scalar_tensor_tensor(out=TMP[:, 1, :], in0=TMP[:, 1, :], scalar=-0.5, in1=VE, op0=ALU.mult,
                                         op1=ALU.mult).then_inc(S["ln_n2"], 1)
                dve.wait_ge(S["ln_n2"], n + 1)
                dve.scalar_tensor_tensor(out=RSTD, in0=TMP[:, 1, :], scalar=1.5, in1=RSTD, op0=ALU.add,
                                         op1=ALU.mult).then_inc(ln_rstd, 1)

            with dve.Fori(0, NS) as s:
                def ctx_low(c):
                    dve.wait_ge(S["ctx_hi"], s * NC + c + 1)
                    dve.tensor_tensor(CSPL[:, c % 3, 1, :], CRAW[:, c % 4, :], CSPL[:, c % 3, 0, :].bitcast(f32),
                                      ALU.subtract).then_inc(S["ctx_lo"], 1)

                ctx_low(0)
                ctx_low(1)
                for c in range(NC):
                    n, e, t = s * NC + c, c % 2, c % CPB
                    if c + 2 < NC:
                        ctx_low(c + 2)
                    dve.wait_ge(row_kv, n + 3)
                    dve.wait_ge(row_sum, n + 1)
                    for w in range(2):
                        cs = C[0:CK, C_KCS + R * t + HALF * w:C_KCS + R * t + HALF * (w + 1)]
                        ins = dve.tensor_tensor(RT[0:CK, e, w, :].rearrange("p (a n) -> p a n", a=2),
                                                PS[0:CK, e, KVC:KVR].rearrange("p (a n) -> p a n", a=2),
                                                cs[:, None, :].to_broadcast([CK, 2, HALF]), ALU.mult)
                    ins.then_inc(row_rt, 1)
                    if c == 2:
                        dve.wait_ge(x_dma, s * 16 + 16)
                        norm_sum(s, 0)
                    if c == 5:
                        for kp in range(4):
                            norm_center(s, 0, kp)
                    if c == 9:
                        norm_sqsum(s, 0)
                for kp in range(4):
                    norm_low(s, 0, kp)
                norm_rstd(s, 0)
                dve.wait_ge(ln_rstd, s * 2 + 2)
                for m in range(KC):
                    n = s * KC + m
                    if m < KC - 1:
                        dve.wait_ge(S["qc_mm"], s * (KC - 1) + m + 1)
                    else:
                        dve.wait_ge(w_used, used(s, U_PAIR - 1))
                    dve.tensor_tensor(TMP[:, m % 2, :], psn(4 + m), RSTD, ALU.mult).then_inc(S["qc_f"], 1)
                    dve.wait_ge(S["qc_hi"], n + 1)
                    dve.tensor_tensor(QCS[:, 1, m, :], TMP[:, m % 2, :], QCS[:, 0, m, :].bitcast(f32),
                                      ALU.subtract).then_inc(S["qc_lo"], 1)

                with dve.Fori(0, PAIRS) as p:
                    for h in range(2):
                        n = s * H + p * 2 + h
                        dve.wait_ge(S["nope_hi"], n + 1)
                        dve.tensor_tensor(NOPE[:, h, 1, :], psn(h), NOPE[:, h, 0, :].bitcast(f32),
                                          ALU.subtract).then_inc(S["nope_lo"], 1)
                    n = s * PAIRS + p
                    dve.wait_ge(S["rp_hi"], n + 1)
                    dve.tensor_tensor(RSP[:, 1, :], psn(4), RSP[:, 0, :].bitcast(f32), ALU.subtract).then_inc(S["rp_lo"], 1)
                    dve.wait_ge(rope_ev, n + 1)
                    rep = [128, BPS, LQ]
                    dve.tensor_tensor(TMP[:, 0, :].rearrange("p (b n) -> p b n", b=BPS), psn(4).rearrange("p (b n) -> p b n", b=BPS),
                                      C[:, C_QC:C_QC + LQ][:, None, :].to_broadcast(rep), ALU.mult).then_inc(rope_t1, 1)
                    dve.wait_ge(S["abs_mm"], s * H + p * 2 + 2)
                    dve.tensor_scalar(QKV[:, :, ds(p + PAIRS, 1), :].rearrange("p d a n -> p d (a n)"), PS[:, 5:7, 0:N], 1.0, None, ALU.mult).then_inc(abs_odd, 1)
                    dve.wait_ge(S["swap_mm"], n + 1)
                    dve.tensor_tensor(TMP[:, 1, :].rearrange("p (b n) -> p b n", b=BPS), psn(7).rearrange("p (b n) -> p b n", b=BPS),
                                      C[:, C_QS:C_QS + LQ][:, None, :].to_broadcast(rep), ALU.mult).then_inc(rope_t2, 1)

                def step(s, i, r):
                    n, q = s * NT + i, r
                    if has(i, 0):
                        sm = SM[0:PQ, q % 4, :, :]
                        dve.wait_ge(st_mm, n + 3)
                        dve.wait_ge(pt_mm, n + 1)
                        dve.tensor_tensor(sm, PS[0:PQ, 3 + q % 2, 0:2 * TK].rearrange("p (e n) -> p e n", e=2),
                                          BM[:, None, :].to_broadcast([PQ, 2, TK]), ALU.add).then_inc(sm_mask, 1)
                        dve.wait_ge(sm_mask, n + 3)
                        dve.tensor_reduce(SMAX[0:PQ, q % 2, :], sm, AX.X, ALU.max).then_inc(S["sm_max"], 1)
                        dve.wait_ge(S["sm_max"], n + 1)
                        dve.tensor_tensor(sm, sm, SMAX[0:PQ, q % 2, :][:, :, None].to_broadcast([PQ, 2, TK]),
                                          ALU.subtract).then_inc(S["sm_shift"], 1)
                    if has(i, 3):
                        m = n - 3
                        dve.wait_ge(pv_mm, m + GR + 1)
                        dve.tensor_scalar(QKV2[:, :, ds(i * QT_ - 3 * QT_, QT_)],
                                          PS[:, 6 + (q - 3) % 2, 0:KV * HQ].rearrange("p (e n) -> p e n", n=QT_),
                                          1.0, None, ALU.mult).then_inc(pv_ev, 1)
                    if has(i, 0):
                        dve.wait_ge(S["sm_exp"], n + 1)
                        dve.tensor_reduce(SSUM[0:PQ, q % 2, :], sm, AX.X, ALU.add).then_inc(S["sm_sum"], 1)
                        dve.wait_ge(S["sm_sum"], n + 1)
                        dve.reciprocal(SSUM[0:PQ, q % 2, :], SSUM[0:PQ, q % 2, :]).then_inc(S["sm_rec"], 1)
                        dve.wait_ge(S["sm_rec"], n + 1)
                        dve.tensor_tensor(sm, sm, SSUM[0:PQ, q % 2, :][:, :, None].to_broadcast([PQ, 2, TK]),
                                          ALU.mult).then_inc(S["sm_norm"], 1)

                steps(dve, step, s, NT + 3)

                def sum_low(n):
                    dve.wait_ge(S["cs_hi"], s * H + n + 1)
                    dve.tensor_tensor(CS[:, n % 2, 1, :, :], QKV[:, :, n, :], CS[:, n % 2, 0, :, :].bitcast(f32),
                                      ALU.subtract).then_inc(S["cs_lo"], 1)

                dve.wait_ge(pv_ev, s * NT + NT + 2)
                sum_low(0)
                sum_low(1)
                for g in range(H // G4):
                    for j in range(G4):
                        n = G4 * g + j
                        dve.wait_ge(S["att_hi"], s * H + n + 1)
                        dve.tensor_tensor(ATT[:, 1, j, :], psn(n % 2), ATT[:, 0, j, :].bitcast(f32),
                                          ALU.subtract).then_inc(att_lo, 1)
                        if j < 2:
                            sum_low(n + 2)
                    for m in range(KD):
                        n = s * (KD * H // G4) + KD * g + m
                        dve.wait_ge(w_used, used(s, U_WO + UPG * g + G4 + m))
                        if g:
                            dve.wait_ge(x_add, n - KD + 5)
                        dve.tensor_tensor(X[:, m, :], X[:, m, :], psn(4 + m % 4), ALU.add).then_inc(x_add, 1)
                        if m == 4 and g + 1 < H // G4:
                            sum_low(G4 * g + G4)
                            sum_low(G4 * g + G4 + 1)

                def signs(v):
                    dve.wait_ge(w_dma[v % WR], s * (UNITS // WR * 16) + ((U_FF + v) // WR + 1) * 16)
                    dve.wait_ge(w_used, s * UNITS + U_FF + v + 1)
                    dve.tensor_scalar(WHI[:, v % WR, :], WRAW[:, v % WR, :], 0.0, 0.5, ALU.is_ge, ALU.subtract).then_inc(w_sgn, 1)

                dve.wait_ge(x_add, (s + 1) * (KD * H // G4) + 4)
                norm_sum(s, 1)
                for v in range(4):
                    signs(v)
                for kp in range(4):
                    norm_center(s, 1, kp)
                for kp in range(4):
                    norm_low(s, 1, kp)
                norm_sqsum(s, 1)
                signs(4)
                signs(5)
                norm_rstd(s, 1)
                dve.wait_ge(ln_rstd, s * 2 + 3)
                for m in range(KD):
                    n = s * KD + m
                    dve.wait_ge(w_used, used(s, U_FF + 2 * m + 1))
                    if m >= 2:
                        dve.wait_ge(S["ff_add"], n - 1)
                    dve.tensor_tensor(TMP[:, m % 2, :], psn(4 + m % 4), RSTD, ALU.mult).then_inc(ff_t, 1)
                    for v in (2 * m + 6, 2 * m + 7):
                        if v < 2 * KD:
                            signs(v)

        @block.tensor
        def _(pe):
            give_credits(pe, "pe")
            pe.wait_ge(const_dma, 16 * 8)
            for m in range(KD):
                for k in range(KV):
                    last = pe.matmul(PS[:, 0, R * m:R * (m + 1)], BIG[:, 4096 + D * k + 128 * m:4096 + D * k + 128 * (m + 1)],
                                     BIG[:, 6144 + R * k:6144 + R * (k + 1)], start=(k == 0), stop=(k == KV - 1))
            last.then_inc(S["fold_mm"], 1)
            pe.wait_ge(S["idx_seg"], 1)
            pe.matmul(PS[0:TK, 1, 0:128], BIG[0:QT_, P_E14:P_E14 + TK], BIG[0:QT_, 1152:1152 + NS * NT],
                      start=True, stop=True).then_inc(S["idx_mm"], 1)
            pe.wait_ge(S["w0_lo"], 1)
            pe.wait_ge(S["idx_ready"], 1)
            pe.wait_ge(S["perm_ready"], 1)

            def three(out_, whi, wlo, xhi, xlo, first, final):
                pe.matmul(out_, whi, xhi, start=first, stop=False)
                pe.matmul(out_, whi, xlo, start=False, stop=False)
                return pe.matmul(out_, wlo, xhi, start=False, stop=final)

            def w_tile(slot, t):
                return WHI[:, slot, 128 * t:128 * (t + 1)], WLO[:, slot, 128 * t:128 * (t + 1)]

            with pe.Fori(0, NS) as s:
                for c in range(NC):
                    n, e = s * NC + c, c % 2
                    pe.wait_ge(S["ctx_lo"], n + 1)
                    pe.wait_ge(row_rt, n + 1)
                    pe.wait_ge(row_kv, n + 1)
                    for k in range(KD):
                        hi, lo = (CSPL[:, c % 3, z, CK * k:CK * (k + 1)] for z in range(2))
                        last = three(PS[0:CK, e, 0:KVR], hi, lo, KVW[:, 0, k, :], KVW[:, 1, k, :], k == 0, k == KD - 1)
                    last.then_inc(S["tab_mm"], 1)
                    if c == 4:
                        pe.wait_ge(S["ln_sum"], s * 2 + 1)
                        pe.matmul(psn(2), ONES, TMP[:, 0, :], start=True, stop=True).then_inc(S["ln_mean_mm"], 1)
                    if c == 10:
                        pe.wait_ge(S["ln_sqsum"], s * 2 + 1)
                        pe.matmul(psn(3), ONES, TMP[:, 1, :], start=True, stop=True).then_inc(S["ln_var_mm"], 1)

                for m in range(KC):
                    for k in range(KD):
                        t = m * KD + k
                        u, v = t // 3, t % 3
                        if v == 0:
                            pe.wait_ge(S["w_lo"], s * SPLIT_UNITS + u + 1)
                        if m == 0 and k % 2 == 0:
                            pe.wait_ge(S["y_lo"], s * 8 + k // 2 + 1)
                        hi, lo = w_tile(u % WR, v)
                        last = three(psn(4 + m), hi, lo, Y[:, 0, k, :], Y[:, 1, k, :], k == 0, k == KD - 1)
                        if v == 2:
                            last.then_inc(w_used, 1)
                    if m < KC - 1:
                        last.then_inc(S["qc_mm"], 1)
                    if m == 0:
                        pe.wait_ge(row_sum, s * NC + NC + 2)
                        pe.matmul(PS[0:1, 7, :].rearrange("p (b n) -> p b n", b=BPS), C[0:CK, C_W750:C_W750 + 1],
                                  G[0:CK, 0:BPS, R:R + KVC], start=True, stop=True).then_inc(mean_mm, 1)

                with pe.Fori(0, PAIRS) as p:
                    pe.wait_ge(S["qc_lo"], s * KC + KC)

                    def unit_ready(v):
                        pe.wait_ge(S["w_lo"], s * SPLIT_UNITS + p * 4 + (U_PAIR + v + 1))

                    def up(bank, slot):
                        for k in range(KC):
                            hi, lo = w_tile(slot, k)
                            last = three(psn(bank), hi, lo, QCS[:, 0, k, :], QCS[:, 1, k, :], k == 0, k == KC - 1)
                        return last

                    def absorb(h, bank):
                        pe.wait_ge(S["nope_lo"], s * H + p * 2 + h + 1)
                        for d in range(KV):
                            hi, lo = w_tile(2, 2 * h + d)
                            last = three(psn(bank + d), hi, lo, NOPE[:, h, 0, :], NOPE[:, h, 1, :], True, True)
                        return last

                    n = s * PAIRS + p
                    for h in range(2):
                        unit_ready(h)
                        up(h, h).then_inc(w_used, 1)
                    unit_ready(2)
                    pe.wait_ge(abs_even, n + 1)
                    absorb(0, 2).then_inc(S["abs_mm"], 1)
                    unit_ready(3)
                    pe.wait_ge(rope_t1, n + 1)
                    up(4, 3).then_inc(S["rope_mm"], 1)
                    pe.wait_ge(abs_odd, n + 1)
                    absorb(1, 5).then_inc(S["abs_mm"], 1)
                    pe.wait_ge(S["rp_lo"], n + 1)
                    pe.wait_ge(rope_t2, n + 1)
                    pe.matmul(psn(7), PERM[:, :], RSP[:, 0, :], start=True, stop=False).then_inc(w_used, 2)
                    pe.matmul(psn(7), PERM[:, :], RSP[:, 1, :], start=False, stop=True).then_inc(S["swap_mm"], 1)
                pe.wait_ge(abs_even, s * PAIRS + PAIRS + 1)
                pe.wait_ge(abs_odd, s * PAIRS + PAIRS + 1)
                pe.wait_ge(rope_ev, s * PAIRS + PAIRS + 1)

                def step(s, i, r):
                    tile = s * NT + i
                    if has(i, 0):
                        pe.wait_ge(g_dma[r], s * (NT // GR * 16) + (i // GR + 1) * 16 if isinstance(i, int) else gd(s, i, r))
                        pe.wait_ge(kt_ev, tile + 1)
                        for w, col in enumerate((0, R, 3 * R, 3 * R + 128)):
                            last = pe.transpose(PS[:, 0, TK * w:TK * (w + 1)], G[0:TK, r, col:col + 128], IDENT[0:TK, 0:TK])
                        last.then_inc(S["kt_mm"], 1)
                    if has(i, 1):
                        n, q = tile - 1, (r - 1) % GR
                        pe.wait_ge(kt_ev, n + 2)
                        pe.wait_ge(s_ev, n + 1)
                        keys, ps = KT[:, q % 2, :], PS[0:TK, 1 + q % 2, 0:HQ]
                        cols = ds(i * QT_ - QT_, QT_)
                        for d in range(KV):
                            pe.matmul(ps, keys[:, TK * (2 + d):TK * (3 + d)], QKV[:, d, :, cols], start=(d == 0), stop=False)
                        for e in range(2):
                            last = pe.matmul(ps[:, PQ * e:PQ * (e + 1)], keys[:, TK * (1 - e):TK * (2 - e)], QR[:, :, cols],
                                             start=False, stop=(e == 1))
                        last.then_inc(s_mm, 1)
                    if has(i, 2):
                        n, q = tile - 2, (r - 2) % GR
                        pe.wait_ge(s_ev, n + 3)
                        pe.wait_ge(sm_mask, n + 1)
                        for e in range(2):
                            last = pe.transpose(PS[0:PQ, 3 + q % 2, TK * e:TK * (e + 1)], SSB[0:TK, q % 2, PQ * e:PQ * (e + 1)],
                                                IDENT[0:TK, 0:TK])
                        last.then_inc(st_mm, 1)
                    if has(i, PT_LAG):
                        n, q = tile - PT_LAG, (r - PT_LAG) % GR
                        pe.wait_ge(S["sm_norm"], n + 1)
                        pe.wait_ge(pt_ev, n + 1)
                        for e in range(2):
                            last = pe.transpose(PS[0:TK, 5, PQ * e:PQ * (e + 1)], SM[0:PQ, q % 4, e, :], IDENT[0:PQ, 0:PQ])
                        last.then_inc(pt_mm, 1)
                    if has(i, LAG):
                        n, q = tile - LAG, (r - LAG) % GR
                        pe.wait_ge(pt_ev, n + 2)
                        pe.wait_ge(pv_ev, n + 1)
                        for d in range(KV):
                            last = pe.matmul(PS[:, 6 + q % 2, HQ * d:HQ * (d + 1)], G[0:TK, q, 3 * R + 128 * d:3 * R + 128 * (d + 1)],
                                             PT[0:TK, q % 2, :], start=True, stop=True)
                        last.then_inc(pv_mm, 1)

                def gd(s, i, r):
                    return s * (NT // GR * 16) + (i - r) * 2 + 16

                steps(pe, step, s, NT + LAG)

                for g in range(H // G4):
                    for j in range(G4):
                        n, u = G4 * g + j, U_WO + UPG * g + j
                        pe.wait_ge(S["w_lo"], s * SPLIT_UNITS + u + 1)
                        pe.wait_ge(S["cs_lo"], s * H + n + 1)
                        pe.wait_ge(att_lo, s * H + n + 1)
                        for d in range(KV):
                            hi, lo = w_tile(u % WR, d)
                            last = three(psn(n % 2), hi, lo, CS[:, n % 2, 0, d, :], CS[:, n % 2, 1, d, :], d == 0, d == KV - 1)
                        last.then_inc(w_used, 1)
                    for m in range(KD):
                        u = U_WO + UPG * g + G4 + m
                        n = s * (KD * H // G4) + KD * g + m
                        pe.wait_ge(S["w_lo"], s * SPLIT_UNITS + u + 1)
                        pe.wait_ge(x_add, n + 1)
                        for j in range(G4):
                            if m == 0:
                                pe.wait_ge(att_lo, s * H + G4 * g + j + 3)
                            hi, lo = w_tile(u % WR, j)
                            last = three(psn(4 + m % 4), hi, lo, ATT[:, 0, j, :], ATT[:, 1, j, :], j == 0, j == G4 - 1)
                        last.then_inc(w_used, 1)

                pe.wait_ge(S["ln_sum"], s * 2 + 2)
                pe.matmul(psn(2), ONES, TMP[:, 0, :], start=True, stop=True).then_inc(S["ln_mean_mm"], 1)
                for m in range(KD):
                    n = s * KD + m
                    pe.wait_ge(ff_t, n + 1)
                    for k in range(KD):
                        v = 2 * m + k // 4
                        if k % 4 == 0:
                            pe.wait_ge(w_sgn, s * 16 + v + 5)
                        if m == 0 and k % 2 == 0:
                            pe.wait_ge(S["y_lo"], s * 8 + 4 + k // 2 + 1)
                        hi, _ = w_tile(v % WR, k % 4)
                        pe.matmul(psn(4 + m % 4), hi, Y[:, 0, k, :], start=(k == 0), stop=False)
                        last = pe.matmul(psn(4 + m % 4), hi, Y[:, 1, k, :], start=False, stop=(k == KD - 1))
                        if k % 4 == 3:
                            last.then_inc(w_used, 1)
                    if m == 0:
                        pe.wait_ge(S["ln_sqsum"], s * 2 + 2)
                        pe.matmul(psn(3), ONES, TMP[:, 1, :], start=True, stop=True).then_inc(S["ln_var_mm"], 1)


def kernel(**inputs):
    import numpy as np
    import concourse.bacc as bacc
    from concourse.bass_utils import run_bass_kernel_spmd

    a = {k.replace("L0_xattn_", "").replace("L0_ffn_", "ffn_"): np.asarray(v) for k, v in inputs.items()}

    def blocks(w, kd, nd):
        return w.reshape(kd, 128, nd, 128).transpose(2, 1, 0, 3)

    heads = [2 * (h % PAIRS) + h // PAIRS for h in range(H)]
    lay = {}
    lay["x"] = a["x"].reshape(NS, N, KD, 128).transpose(0, 3, 2, 1).reshape(NS, 128, KD * N)
    lay["ctx"] = a["ctx_2048"].reshape(B * CPB, CK, KD, 128).transpose(0, 3, 2, 1).reshape(B * CPB, 128, KD * CK)
    lay["seg"] = a["itok_BxS_0_1023"].reshape(NS * NT, QT_).T
    lay["kvc"] = a["W_kvc"].reshape(KD, 128, KVC).transpose(1, 0, 2).reshape(128, KD * KVC)
    lay["kvct"] = a["W_kvc"].T.reshape(KV, 128, D).transpose(1, 0, 2).reshape(128, KV * D)
    lay["kr"] = a["W_kr"].reshape(KV, 128, R).transpose(1, 0, 2).reshape(128, KV * R)
    dq = blocks(a["W_dq"], KD, KC)
    lay["dq"] = dq.transpose(0, 2, 1, 3).reshape(8, 3, 128, 128).transpose(0, 2, 1, 3).reshape(8, 128, 384)
    lay["uq"] = blocks(a["W_uq"], KC, H).reshape(H, 128, KC * 128)
    uk = a["W_uk"].reshape(KV, 128, PAIRS, 2, HD)
    lay["uk"] = uk.transpose(2, 4, 3, 0, 1).reshape(PAIRS, 128, 2 * KV * 128)
    lay["qr"] = blocks(a["W_qr"], KC, PAIRS).reshape(PAIRS, 128, KC * 128)
    lay["uv"] = blocks(a["W_uv"], KV, H)[heads].reshape(H, 128, KV * HD)
    wo = a["W_o"].reshape(H, HD, KD, 128)[heads].reshape(H // G4, G4, HD, KD, 128)
    lay["wo"] = wo.transpose(0, 3, 2, 1, 4).reshape(H // G4 * KD, 128, G4 * 128)
    ff = a["ffn_weight"].reshape(KD, 128, 2, KD // 2, 128)
    lay["ff"] = ff.transpose(0, 2, 4, 3, 1).reshape(2 * KD, 128, KD // 2 * 128)
    lay["ffn"] = a["ffn_weight"].reshape(KD, 128, D).transpose(1, 0, 2).reshape(128, KD * D)
    lay["bias"] = a["ffn_bias"].reshape(KD, 128).T
    lay["cst"], lay["pre"] = constants()

    nc = bacc.Bacc("TRN2", target_bir_lowering=False, num_devices=1)
    arrays, args = {}, []
    for name, v in lay.items():
        v = np.ascontiguousarray(v)
        arrays[f"in_{name}"] = v
        args.append(nc.dram_tensor(f"in_{name}", v.shape, mybir.dt.from_np(v.dtype), kind="ExternalInput").ap())
    out = nc.dram_tensor("out_t", (NS, 128, KD * N), mybir.dt.float32, kind="ExternalOutput").ap()
    program(nc, *args, out)
    r = run_bass_kernel_spmd(nc, [arrays], core_ids=[0])
    y = r.results[0]["out_t"].reshape(NS, 128, KD, N).transpose(0, 3, 2, 1)
    return np.ascontiguousarray(y.reshape(B, LQ, D))
```

```python
import math

import concourse.bass as bass
from concourse import mybir
from contextlib import ExitStack

B, LQ, D = 8, 224, 1024
LK = 750
H, HD = 16, 128
KVC, QC, R = 256, 384, 64
LOOKBACK = 8
NEG = -1e30
EPS = 1e-5
SCALE = 1.0 / math.sqrt(HD + R)
HALF = R // 2

T = B * LQ
NS = 4
N = T // NS
BPS = B // NS
W = LOOKBACK + 1
QT_ = 14
TK = QT_ * W
NT = N // QT_
TPB = LQ // QT_
PAIRS = H // 2
PQ = PAIRS * QT_
HQ = H * QT_
KD, KC, KV = D // 128, QC // 128, KVC // 128
CK = 125
CPB = LK // CK
NC = BPS * CPB
ROWS = LK + 2
MEAN_ROW, MASKED_ROW = LK, LK + 1
KVR = KVC + R
TW = R + R + KVC + 1
GW = R + TW
GR = 8
AHEAD = 6
PT_LAG, LAG = 4, 5

UW = 512
WR = 4
U_DQ, U_PAIR, U_WO, U_FF = 0, 8, 40, 88
UNITS = 104
SPLIT_UNITS = U_FF
G4 = 4
HALF_M = KD // 2
OUT_UNITS = [("value", n) for n in range(G4)]
for g_ in range(H // G4):
    for j_ in range(G4):
        if g_ + 1 < H // G4:
            OUT_UNITS.append(("value", G4 * (g_ + 1) + j_))
        OUT_UNITS += [("output", KD * g_ + 2 * j_), ("output", KD * g_ + 2 * j_ + 1)]

C_ID, C_BM = 0, 128
C_QC = C_BM + TK
C_QS = C_QC + LQ
C_KCS = C_QS + LQ
C_ONE = C_KCS + CPB * R
C_W750 = C_ONE + 128
CW = C_W750 + 1
P_PERM, P_E14 = 0, 128
P_J = P_E14 + TK
P_BASE = P_J + 1
PW = P_BASE + NS * NT


def constants():
    import numpy as np
    c = np.zeros((128, CW), np.float32)
    c[:, C_ID:C_ID + 128] = np.eye(128)
    q_of_row = np.arange(PQ) % QT_
    q_of_key = np.arange(TK) // W
    c[:PQ, C_BM:C_BM + TK] = np.where(q_of_row[:, None] == q_of_key[None, :], 0.0, -NEG)
    inv = (1.0 / np.float32(10000.0) ** (np.arange(HALF, dtype=np.float32) / np.float32(HALF))).astype(np.float32)
    ang = np.arange(LK, dtype=np.float32)[:, None] * inv
    cos, sin = np.cos(ang).astype(np.float32), np.sin(ang).astype(np.float32)
    c[:, C_QC:C_QC + LQ] = np.concatenate([cos[:LQ].T] * 4, 0)
    c[:, C_QS:C_QS + LQ] = np.concatenate([-sin[:LQ].T, sin[:LQ].T] * 2, 0)
    kcs = np.concatenate([cos, sin], 1).reshape(CPB, CK, R).transpose(1, 0, 2)
    c[:CK, C_KCS:C_KCS + CPB * R] = kcs.reshape(CK, -1)
    c[:, C_ONE:C_ONE + 128] = 1.0 / D
    c[:CK, C_W750] = np.float32(1.0) / np.float32(LK)
    p = np.zeros((128, PW), np.float32)
    r = np.arange(128)
    p[(r // R) * R + (r % R + HALF) % R, P_PERM + r] = 1.0
    p[q_of_key, P_E14 + np.arange(TK)] = 1.0
    p[:TK, P_J] = np.arange(TK) % W
    p[:, P_BASE:] = (np.arange(NS * NT) // TPB % BPS * ROWS)[None, :]
    return c, p


def program(nc, x, ctx, seg, kvc, kvct, kr, dq, uq, uk, qr, uv, wo, ff, ffn, bias, cst, pre, out):
    f32, f32r, i32 = mybir.dt.float32, mybir.dt.float32r, mybir.dt.int32
    ALU, ACT, AX = mybir.AluOpType, mybir.ActivationFunctionType, mybir.AxisListType
    ds = bass.ds

    table = nc.dram_tensor("key_table", (BPS * ROWS, TW), f32).ap()

    ctx_ = ExitStack()
    with ctx_:
        def sb(name, shape, dt=f32):
            return ctx_.enter_context(nc.sbuf_tensor(name, shape, dt))

        def sem(name):
            return ctx_.enter_context(nc.semaphore(name))

        with nc.sbuf_tensor("big_split", [128, KV * H * N + PAIRS * N], f32r) as BIG_R:
            pass
        BIG = sb("big", [128, KV * H * N + PAIRS * N])
        SPL = sb("split", [128, 2 * KD * N], f32r)
        X = sb("x_sb", [128, KD, N])
        QCS = sb("qc_split", [128, 2, KC, N], f32r)
        G = sb("gathered", [128, GR, GW])
        KT = sb("keys_t", [128, 2, 4 * TK])
        SOFT = sb("soft", [128, 2 * HQ + 4 * 2 * TK + 2 * HQ])
        WRAW = sb("w_raw", [128, WR, UW])
        WHI = sb("w_high", [128, WR, UW], f32r)
        WLO = sb("w_low", [128, WR, UW], f32r)
        KVW = sb("kv_weights", [128, 2, KD, KVR], f32r)
        C = sb("consts", [128, CW])
        PERM = sb("perm", [128, 128], f32r)
        ROW = sb("row", [128, 2, TW])
        RT = sb("row_rope_tmp", [128, 2, 2, R])
        IDX = sb("idx", [128, NS * NT], i32)
        IDXR = sb("idx_ring", [128, GR], i32)
        BIAS = sb("bias_sb", [128, KD])
        ALPHA, ALPHA2 = sb("alpha", [128, KD]), sb("alpha2", [128, KD])
        eps = sb("eps", [128, 1])
        PS = ctx_.enter_context(nc.psum_tensor("ps", [128, 8, 512], f32))

        QKV = BIG[:, 0:KV * H * N].rearrange("p (d h n) -> p d h n", d=KV, h=H)
        QKV2 = BIG[:, 0:KV * H * N].rearrange("p (e n) -> p e n", n=N)
        QR = BIG[:, KV * H * N:].rearrange("p (a n) -> p a n", a=PAIRS)
        CRAW = BIG[:, 0:4 * KD * CK].rearrange("p (b k n) -> p b (k n)", b=4, k=KD)
        o = 4 * KD * CK
        CEN = BIG[:, o:o + KD * N].rearrange("p (k n) -> p k n", k=KD)
        SQ = BIG[:, o + KD * N:o + 2 * KD * N].rearrange("p (k n) -> p k n", k=KD)
        o += 2 * KD * N
        CSPL = BIG_R[:, o:o + 3 * 2 * KD * CK].rearrange("p (b s n) -> p b s n", b=3, s=2)
        FF_ROWS = [BIG[:, o + 4 * KD * CK + D * i:o + 4 * KD * CK + D * (i + 1)] for i in range(2)]
        FF_ROWS += [X[:, :, :].rearrange("p k n -> p (k n)")[:, D * i:D * (i + 1)] for i in range(3)]
        FF_ROWS += [WRAW[:, 2 * i:2 * i + 2, :].rearrange("p b n -> p (b n)") for i in range(2)]
        Y = SPL[:, :].rearrange("p (s k n) -> p s k n", s=2, k=KD)
        NOPE = SPL[:, 0:4 * N].rearrange("p (b s n) -> p b s n", b=2, s=2)
        RSP = SPL[:, 4 * N:6 * N].rearrange("p (s n) -> p s n", s=2)
        ATT = SPL[:, :].rearrange("p (b s j n) -> p b s j n", b=2, s=2, j=G4)
        CS = BIG_R[:, KV * H * N:].rearrange("p (b s d n) -> p b s d n", b=2, s=2, d=KV)
        o = 4 * KD * CK
        PRE, SEG_I, SEG_F = BIG[:, o:o + PW], BIG[0:QT_, o + 384:o + 512].bitcast(i32), BIG[0:QT_, o + 512:o + 640]
        IDX_TMP = [BIG[0:TK, o + 640 + 128 * i:o + 768 + 128 * i] for i in range(4)]
        o += 1152
        KVC_F, KVC_T = BIG[:, o:o + KD * KVC], BIG[:, o + KD * KVC:o + KD * KVC + KV * D]
        KR_F = BIG[:, o + KD * KVC + KV * D:o + KD * KVC + KV * D + KV * R]
        o += KD * KVC + KV * D + KV * R
        FF_ROWS.append(BIG[:, o:o + D])
        RSTD, VE = SOFT[:, 0:N], SOFT[:, N:2 * N]
        TMP = SOFT[:, 2 * N:4 * N].rearrange("p (b n) -> p b n", b=2)
        SSB = SOFT[:, 0:2 * HQ].rearrange("p (b n) -> p b n", b=2)
        SM = SOFT[:, 2 * HQ:2 * HQ + 8 * TK].rearrange("p (b e n) -> p b e n", b=4, e=2)
        PT = SOFT[:, 2 * HQ + 8 * TK:].rearrange("p (b n) -> p b n", b=2)
        STAT = sb("stat", [128, 4, 2, 2])
        SMAX, SSUM = STAT[:, :, 0, :], STAT[:, :, 1, :]
        IDENT, BM = C[:, C_ID:C_ID + 128], C[0:PQ, C_BM:C_BM + TK]
        ONES = C[:, C_ONE:C_ONE + 128]

        def psn(bank):
            return PS[:, bank, 0:N]

        const_dma, x_dma, out_dma = sem("const_dma"), sem("x_dma"), sem("out_dma")
        fold_dma, seg_dma, ffn_dma = sem("fold_dma"), sem("seg_dma"), sem("ffn_dma")
        ctx_dma = [sem(f"ctx_dma{i}") for i in range(4)]
        w_dma = [sem(f"w_dma{i}") for i in range(WR)]
        g_dma = [sem(f"g_dma{i}") for i in range(GR)]
        row_dma = [sem(f"row_dma{i}") for i in range(2)]
        mean_dma, masked_dma = sem("mean_dma"), sem("masked_dma")
        credit = {}

        def csem(name, slots, owner):
            s_ = sem(name)
            credit[name] = (s_, slots, owner)
            return s_

        names = ("idx_seg idx_mm idx_chain idx_ready fold_mm w0_hi w0_lo perm_ready alpha_abs alpha_ready clear masked_set "
                 "ctx_hi ctx_lo tab_mm mean_ev mean_clear  "
                 "w_hi w_lo "
                 "ln_sum ln_part ln_mean_mm ln_sub ln_sq ln_sqsum ln_var_mm ln_ve ln_std ln_inv ln_n1 ln_n2 y_hi y_lo "
                 "qc_mm qc_f qc_hi qc_lo nope_hi nope_lo abs_mm rp_hi rp_lo swap_mm "
                 "idx_copied kt_mm sm_max sm_exp sm_rec sm_norm "
                 "cs_hi cs_lo att_hi ff_ab ff_add").split()
        S = {n_: sem(n_) for n_ in names}
        row_kv, row_rt, row_sum = csem("row_kv", 2, "act"), csem("row_rt", 2, "dve"), csem("row_sum", 2, "pool")
        mean_mm = csem("mean_mm", 1, "pe")
        w_used, w_sgn = csem("w_used", WR, "pe"), csem("w_sgn", WR, "dve")
        ln_rstd = csem("ln_rstd", 1, "dve")
        abs_even, abs_odd = csem("abs_even", 1, "act"), csem("abs_odd", 1, "dve")
        rope_t1, rope_t2, rope_ev = csem("rope_t1", 1, "dve"), csem("rope_t2", 1, "dve"), csem("rope_ev", 1, "pool")
        kt_ev, s_ev, sm_mask = csem("kt_ev", 1, "act"), csem("s_ev", 2, "act"), csem("sm_mask", 2, "dve")
        pt_ev, pv_ev = csem("pt_ev", 1, "act"), csem("pv_ev", 2, "dve")
        s_mm, st_mm, pt_mm, pv_mm = csem("s_mm", 2, "pe"), csem("st_mm", 2, "pe"), csem("pt_mm", 4, "pe"), csem("pv_mm", GR, "pe")
        att_lo, x_add = csem("att_lo", 2, "dve"), csem("x_add", 4, "dve")
        ff_t = csem("ff_t", 4, "dve")
        credit["out_dma"] = (out_dma, 16, "sp")

        def value_unit(n):
            return U_WO + OUT_UNITS.index(("value", n))

        def used(s, u):
            return s * UNITS + (u + 1 + WR)

        def give_credits(eng, who):
            for s_, slots, owner in credit.values():
                if owner == who:
                    eng.sem_inc(s_, slots)

        block = ctx_.enter_context(nc.Block())
        def steps(eng, step, s, last):
            for i in range(GR):
                step(s, i, i)
            with eng.Fori(1, NT // GR) as k:
                for r in range(GR):
                    step(s, k * GR + r, r)
            for i in range(NT, last):
                step(s, i, i % GR)

        def has(i, lag):
            return not isinstance(i, int) or 0 <= i - lag < NT

        @block.sync
        def _(sp):
            give_credits(sp, "sp")
            sp.dma_start(KVC_T, kvct).then_inc(fold_dma, 16)
            sp.dma_start(KR_F, kr).then_inc(fold_dma, 16)
            sp.dma_start(KVC_F, kvc).then_inc(fold_dma, 16)
            sp.dma_start(PRE, pre).then_inc(seg_dma, 16)
            sp.dma_start(SEG_I, seg).then_inc(seg_dma, 16)

            def ctx_load(n, slot):
                sp.dma_start(CRAW[:, slot, :], ctx[ds(n, 1), :, :].rearrange("a p n -> (a p) n")).then_inc(ctx_dma[slot], 16)

            ctx_load(0, 0)
            ctx_load(1, 1)
            sp.dma_start(C[:, :], cst).then_inc(const_dma, 16)
            sp.dma_start(BIAS[:, :], bias).then_inc(const_dma, 16)
            for m in range(KD):
                sp.dma_start(FF_ROWS[m], ffn[:, D * m:D * (m + 1)]).then_inc(ffn_dma, 16)
            ctx_load(2, 2)
            ctx_load(3, 3)

            def unit(s, u, slot, src, width):
                if isinstance(u, int) and u < WR:
                    sp.wait_ge(w_sgn, s * 16 + u + 1)
                elif isinstance(u, int) and u >= U_FF + WR:
                    sp.wait_ge(w_sgn, s * 16 + (u - U_FF) + 1)
                else:
                    sp.wait_ge(S["w_lo"], s * SPLIT_UNITS + u - WR + 1)
                sp.dma_start(WRAW[:, slot, 0:width], src).then_inc(w_dma[slot], 16)

            with sp.Fori(0, NS) as s:
                for c in range(4, NC):
                    if c == 7:
                        sp.wait_ge(S["alpha_ready"], 1)
                        sp.wait_ge(out_dma, (s + 1) * 16)
                        sp.dma_start(X[:, :, :].rearrange("p k n -> p (k n)"), x[ds(s, 1), :, :].rearrange("a p n -> (a p) n")).then_inc(x_dma, 16)
                    sp.wait_ge(S["ctx_lo"], s * NC + c - 3)
                    ctx_load(s * NC + c, c % 4)
                for u in range(U_PAIR):
                    unit(s, u, u % WR, dq[u], 3 * 128)
                with sp.Fori(0, PAIRS) as p:
                    u0 = p * 4 + U_PAIR
                    unit(s, u0, 0, uq[ds(p * 2, 1), :, :].rearrange("a p n -> (a p) n"), 3 * 128)
                    unit(s, u0 + 1, 1, uq[ds(p * 2 + 1, 1), :, :].rearrange("a p n -> (a p) n"), 3 * 128)
                    unit(s, u0 + 2, 2, qr[ds(p, 1), :, :].rearrange("a p n -> (a p) n"), 3 * 128)
                    unit(s, u0 + 3, 3, uk[ds(p, 1), :, :].rearrange("a p n -> (a p) n"), 512)
                for v, (kind, n) in enumerate(OUT_UNITS):
                    unit(s, U_WO + v, v % WR, *((uv[n], 256) if kind == "value" else (wo[n], 512)))
                for v in range(2 * KD):
                    unit(s, U_FF + v, v % WR, ff[v], 512)
                    if v == 3:
                        sp.wait_ge(S["cs_lo"], s * H + H)
                        for c in range(4):
                            ctx_load(s * NC + (NC + c), c)
                sp.wait_ge(S["ff_add"], s * KD + KD)
                sp.dma_start(out[ds(s, 1), :, :].rearrange("a p n -> (a p) n"), X[:, :, :].rearrange("p k n -> p (k n)")).then_inc(out_dma, 16)
            sp.wait_ge(out_dma, 16 + 16 * NS)
            for c in range(4):
                sp.wait_ge(ctx_dma[c], 16 * NC // 4 * NS + 16)

        @block.gpsimd
        def _(pool):
            give_credits(pool, "pool")
            pool.memset(G[:, :, 0:R], 0.0).then_inc(S["clear"], 1)
            pool.memset(ROW[:, :, R:2 * R], 0.0).then_inc(S["clear"], 1)
            pool.memset(ROW[:, :, TW - 1:TW], 0.0).then_inc(S["clear"], 1)
            masked = G[0:BPS, GR - 1, R:GW]
            pool.memset(masked[:, 0:TW - 1], 0.0).then_inc(S["masked_set"], 1)
            pool.memset(masked[:, TW - 1:TW], -NEG).then_inc(S["masked_set"], 1)
            pool.wait_ge(S["masked_set"], 2)
            pool.dma_start(table[MASKED_ROW:BPS * ROWS:ROWS, :], masked).then_inc(masked_dma, 16)

            def low(s, u, slot, width):
                pool.wait_ge(S["w_hi"], s * SPLIT_UNITS + u + 1)
                pool.tensor_tensor(WLO[:, slot, 0:width], WRAW[:, slot, 0:width], WHI[:, slot, 0:width].bitcast(f32),
                                   ALU.subtract).then_inc(S["w_lo"], 1)

            def gather(r):
                pool.indirect_dma_start(out=G[0:TK, r, R:GW], out_offset=None, in_=table,
                                        in_offset=bass.IndirectOffsetOnAxis(ap=IDXR[0:TK, r:r + 1], axis=0)).then_inc(g_dma[r], 16)

            def normalise(r, e):
                return pool.tensor_tensor(SM[0:PQ, r % 4, e, :], SM[0:PQ, r % 4, e, :],
                                          SSUM[0:PQ, r % 4, e:e + 1].to_broadcast([PQ, TK]), ALU.mult)

            def step(s, k, r):
                tile = s * NT + k * GR + r
                pool.wait_ge(pv_mm, tile + 1)
                pool.wait_ge(S["sm_rec"], tile - AHEAD + 1)
                normalise(r - AHEAD, 0)
                pool.tensor_copy(IDXR[0:TK, r:r + 1], IDX[0:TK, ds(tile, 1)]).then_inc(S["idx_copied"], 1)
                pool.wait_ge(S["idx_copied"], s * (NT - GR + 1) + k * GR + (r - GR + 2))
                normalise(r - AHEAD, 1).then_inc(S["sm_norm"], 1)
                gather(r)

            def finish(s, i):
                pool.wait_ge(S["sm_rec"], s * NT + i + 1)
                normalise(i, 0)
                normalise(i, 1).then_inc(S["sm_norm"], 1)

            pool.wait_ge(S["idx_ready"], 1)
            pool.wait_ge(S["clear"], 3)
            pool.wait_ge(masked_dma, 16)
            with pool.Fori(0, NS) as s:
                for c in range(NC):
                    b, t, e = c // CPB, c % CPB, c % 2
                    n = s * NC + c
                    pool.wait_ge(row_rt, n + 3)
                    pool.tensor_tensor(ROW[0:CK, e, 0:HALF], RT[0:CK, e, 0, 0:HALF], RT[0:CK, e, 1, HALF:R],
                                       ALU.subtract)
                    pool.tensor_tensor(ROW[0:CK, e, HALF:R], RT[0:CK, e, 0, HALF:R], RT[0:CK, e, 1, 0:HALF],
                                       ALU.add)
                    pool.wait_ge(row_kv, n + 3)
                    if c == 0:
                        pool.wait_ge(mean_mm, s + 1)
                        pool.wait_ge(pv_mm, s * NT + GR)
                    acc, kv = G[0:CK, b, R:R + KVC], ROW[0:CK, e, 2 * R:2 * R + KVC]
                    if t == 0:
                        pool.tensor_tensor(acc, kv, ROW[0:CK, e, R:R + 1].to_broadcast([CK, KVC]), ALU.add).then_inc(row_sum, 1)
                    else:
                        pool.wait_ge(row_sum, n + 2)
                        pool.tensor_tensor(acc, acc, kv, ALU.add).then_inc(row_sum, 1)
                    if c >= NC - 4:
                        low(s, c - (NC - 4), c - (NC - 4), 384)
                pool.memset(G[0:1, 2:4, R:3 * R], 0.0).then_inc(S["mean_clear"], 1)
                pool.memset(G[0:1, 2:4, GW - 1:GW], 0.0).then_inc(S["mean_clear"], 1)
                for u in range(4, 8):
                    low(s, u, u % WR, 384)
                pool.wait_ge(S["mean_clear"], s * 2 + 2)
                pool.wait_ge(S["mean_ev"], s + 1)
                low(s, 8, 0, 384)
                mean_rows = table.rearrange("(b r) w -> r b w", r=ROWS)[MEAN_ROW:MEAN_ROW + 1, :, :]
                pool.dma_start(mean_rows, G[0:1, 2:4, R:GW]).then_inc(mean_dma, 16)
                pool.tensor_copy(IDXR[0:TK, :], IDX[0:TK, ds(s * NT, GR)]).then_inc(S["idx_copied"], 1)
                for u in range(9, 11):
                    low(s, u, u % WR, 384)
                for p in range(PAIRS):
                    for v in range(3, 7):
                        u = U_PAIR + 4 * p + v
                        if p == 0 and v == 3:
                            for e in range(2):
                                pool.wait_ge(row_dma[e], (s + 1) * (16 * NC // 2))
                            pool.wait_ge(mean_dma, s * 16 + 16)
                            pool.wait_ge(S["idx_copied"], s * (NT - GR + 1) + 1)
                        low(s, u, v % WR, 512 if v == 3 else 384 if u < U_WO else 256)
                        if v == 4:
                            gather(p)
                    pool.wait_ge(rope_t1, s * PAIRS + p + 2)
                    pool.wait_ge(rope_t2, s * PAIRS + p + 2)
                    pool.tensor_tensor(QR[:, p, :], TMP[:, 0, :], TMP[:, 1, :], ALU.add).then_inc(rope_ev, 1)
                low(s, U_WO + 3, 3, 256)
                for i in range(GR - AHEAD):
                    finish(s, i)
                with pool.Fori(1, NT // GR) as k:
                    for r in range(GR):
                        step(s, k, r)
                for i in range(NT - AHEAD, NT):
                    finish(s, i)
                for v, (kind, n) in enumerate(OUT_UNITS):
                    if v >= WR:
                        low(s, U_WO + v, v % WR, 256 if kind == "value" else 512)
                for m in range(KD):
                    pool.wait_ge(S["ff_ab"], s * KD + m + 1)
                    pool.tensor_tensor(X[:, m, :], X[:, m, :], TMP[:, m % 2, :], ALU.add).then_inc(S["ff_add"], 1)

        @block.scalar
        def _(act):
            give_credits(act, "act")

            def high(s, u, slot, width):
                act.wait_ge(w_dma[slot], s * (UNITS // WR * 16) + (u // WR + 1) * 16)
                act.wait_ge(w_used, s * UNITS + u + 1)
                act.activation(WHI[:, slot, 0:width], WRAW[:, slot, 0:width], ACT.Copy).then_inc(S["w_hi"], 1)

            def high_in_pair(s, p, v, width):
                act.wait_ge(w_dma[v % WR], s * (UNITS // WR * 16) + p * 16 + (U_PAIR // WR + v // WR + 1) * 16)
                act.wait_ge(w_used, s * UNITS + p * 4 + (U_PAIR + v + 1))
                act.activation(WHI[:, v % WR, 0:width], WRAW[:, v % WR, 0:width], ACT.Copy).then_inc(S["w_hi"], 1)

            def norm_high(s, l, kp):
                act.wait_ge(S["ln_sub"], s * 8 + 4 * l + kp + 1)
                act.activation(Y[:, 0, 2 * kp:2 * kp + 2, :], CEN[:, 2 * kp:2 * kp + 2, :], ACT.Copy).then_inc(S["y_hi"], 1)

            def norm_square(s, l):
                act.wait_ge(S["ln_sub"], s * 8 + 4 * l + 4)
                act.activation(SQ[:, :, :], CEN[:, :, :], ACT.Square).then_inc(S["ln_sq"], 1)

            def norm_std(s, l):
                act.wait_ge(S["ln_var_mm"], s * 2 + l + 1)
                act.activation(VE, psn(3), ACT.Identity, bias=eps[:, :]).then_inc(S["ln_ve"], 1)
                act.wait_ge(S["ln_ve"], s * 2 + l + 1)
                act.activation(TMP[:, 0, :], VE, ACT.Sqrt).then_inc(S["ln_std"], 1)

            def ctx_high(s, c):
                act.wait_ge(ctx_dma[c % 4], s * (16 * NC // 4) + (c // 4 + 1) * 16)
                if 3 <= c < NC:
                    act.wait_ge(S["tab_mm"], s * NC + c - 2)
                act.activation(CSPL[:, c % 3, 0, :], CRAW[:, c % 4, :], ACT.Copy).then_inc(S["ctx_hi"], 1)

            def store_rows(s, c):
                b, t = c // CPB, c % CPB
                act.wait_ge(row_sum, s * NC + c + 3)
                act.dma_start(table[b * ROWS + t * CK:b * ROWS + (t + 1) * CK, :], ROW[0:CK, c % 2, :]).then_inc(row_dma[c % 2], 16)

            act.wait_ge(fold_dma, 16 * 3)
            act.activation(KVW[:, 0, :, 0:KVC], KVC_F.rearrange("p (k n) -> p k n", k=KD), ACT.Copy).then_inc(S["w0_hi"], 1)
            act.wait_ge(S["fold_mm"], 1)
            act.activation(KVW[:, 0, :, KVC:KVR], PS[:, 0, :].rearrange("p (k n) -> p k n", k=KD), ACT.Copy).then_inc(S["w0_hi"], 1)
            ctx_high(0, 0)
            ctx_high(0, 1)
            act.wait_ge(seg_dma, 16 * 2)
            act.activation(PERM[:, :], PRE[:, P_PERM:P_PERM + 128], ACT.Copy).then_inc(S["perm_ready"], 1)
            act.wait_ge(ffn_dma, 16 * KD)
            for m in range(KD):
                if m:
                    act.wait_ge(S["alpha_abs"], m)
                act.activation(FF_ROWS[m], FF_ROWS[m], ACT.Abs, accum_out=ALPHA[:, m:m + 1]).then_inc(S["alpha_abs"], 1)
            act.wait_ge(S["alpha_abs"], KD)
            act.wait_ge(const_dma, 16 * 2)

            with act.Fori(0, NS) as s:
                for c in range(NC):
                    if c + 2 < NC:
                        if c:
                            ctx_high(s, c + 2)
                        else:
                            act.wait_ge(ctx_dma[2], s * (16 * NC // 4) + 16)
                            act.activation(CSPL[:, 2, 0, :], CRAW[:, 2, :], ACT.Copy).then_inc(S["ctx_hi"], 1)
                    n, e = s * NC + c, c % 2
                    if c:
                        store_rows(s, c - 1)
                    act.wait_ge(S["tab_mm"], n + 1)
                    if c >= 2:
                        act.wait_ge(row_dma[e], s * (16 * NC // 2) + (c // 2) * 16)
                    act.wait_ge(row_sum, n + 1)
                    act.activation(ROW[0:CK, e, 2 * R:2 * R + KVC], PS[0:CK, 6 + e, 0:KVC], ACT.Copy).then_inc(row_kv, 1)
                    if c == 7:
                        act.wait_ge(w_used, used(s, -1))
                        norm_high(s, 0, 0)
                        norm_high(s, 0, 1)
                    if c == 8:
                        norm_high(s, 0, 2)
                        norm_high(s, 0, 3)
                    if c == 9:
                        norm_square(s, 0)
                    if c >= NC - 4:
                        high(s, c - (NC - 4), c - (NC - 4), 384)
                store_rows(s, NC - 1)
                norm_std(s, 0)
                for u in range(4, 8):
                    high(s, u, u % WR, 384)
                act.wait_ge(mean_mm, s + 2)
                act.activation(G[0:1, 2:4, 3 * R:3 * R + KVC], PS[0:1, 7, :].rearrange("p (b n) -> p b n", b=BPS),
                               ACT.Copy).then_inc(S["mean_ev"], 1)
                for m in range(KC):
                    act.wait_ge(S["qc_f"], s * KC + m + 1)
                    act.activation(QCS[:, 0, m, :], TMP[:, m % 2, :], ACT.Copy).then_inc(S["qc_hi"], 1)
                    high(s, 8 + m, m % WR, 384)

                def pair(p, next_width):
                    high_in_pair(s, p, 3, 512)
                    for h in range(2):
                        act.wait_ge(w_used, s * UNITS + p * 4 + (U_PAIR + h + 1 + WR))
                        act.activation(NOPE[:, h, 0, :], psn(h), ACT.Copy).then_inc(S["nope_hi"], 1)
                        high_in_pair(s, p, 4 + h, next_width)
                    act.wait_ge(w_used, s * UNITS + p * 4 + (U_PAIR + 2 + 1 + WR))
                    act.activation(RSP[:, 0, :], psn(4), ACT.Copy).then_inc(S["rp_hi"], 1)
                    high_in_pair(s, p, 6, next_width)
                    act.wait_ge(S["abs_mm"], s * H + p * 2 + 1)
                    act.activation(QKV[:, :, ds(p, 1), :].rearrange("p d a n -> p d (a n)"), PS[:, 2:4, 0:N], ACT.Copy).then_inc(abs_even, 1)

                with act.Fori(0, PAIRS - 1) as p:
                    pair(p, 384)
                pair(PAIRS - 1, 256)
                high(s, U_WO + 3, 3, 256)

                def step(s, i, r):
                    tile = s * NT + i
                    if has(i, 0):
                        act.wait_ge(S["kt_mm"], tile + 1)
                        act.wait_ge(s_mm, tile + 1)
                        act.activation(KT[:, r % 2, :], PS[:, 0, 0:4 * TK], ACT.Copy).then_inc(kt_ev, 1)
                    if has(i, 1):
                        n, q = tile - 1, (r - 1) % GR
                        act.wait_ge(s_mm, n + 3)
                        act.wait_ge(st_mm, n + 1)
                        act.activation(SSB[0:TK, q % 2, :], PS[0:TK, 1 + q % 2, 0:HQ], ACT.Identity,
                                       bias=G[0:TK, q, GW - 1:GW], scale=-SCALE).then_inc(s_ev, 1)
                    if has(i, PT_LAG):
                        n, q = tile - PT_LAG, (r - PT_LAG) % GR
                        act.wait_ge(pt_mm, n + 5)
                        act.wait_ge(pv_mm, n + GR - 1)
                        act.activation(PT[0:TK, q % 2, :], PS[0:TK, 5, 0:HQ], ACT.Copy).then_inc(pt_ev, 1)
                    if has(i, 2):
                        n, q = tile - 2, (r - 2) % GR
                        act.wait_ge(S["sm_max"], n + 1)
                        for e in range(2):
                            ins = act.activation(SM[0:PQ, q % 4, e, :], SM[0:PQ, q % 4, e, :], ACT.Exp, scale=-1.0,
                                                 bias=SMAX[0:PQ, q % 4, e:e + 1], accum_out=SSUM[0:PQ, q % 4, e:e + 1])
                        ins.then_inc(S["sm_exp"], 1)

                steps(act, step, s, NT + PT_LAG)

                act.wait_ge(pv_ev, s * NT + NT + 2)

                def sum_high(n):
                    if n >= 2:
                        act.wait_ge(w_used, used(s, value_unit(n - 2)))
                    act.activation(CS[:, n % 2, 0, :, :], QKV[:, :, n, :], ACT.Copy).then_inc(S["cs_hi"], 1)

                sum_high(0)
                sum_high(1)
                for v, (kind, n) in enumerate(OUT_UNITS):
                    if kind == "value":
                        g, j = n // G4, n % G4
                        if g >= 2:
                            act.wait_ge(w_used, used(s, U_WO + OUT_UNITS.index(("output", KD * (g - 1) - 1))))
                        act.wait_ge(w_used, used(s, U_WO + v))
                        act.activation(ATT[:, g % 2, 0, j, :], psn(n % 2), ACT.Copy).then_inc(S["att_hi"], 1)
                        if n + 2 < H:
                            sum_high(n + 2)
                    w = v + WR
                    if w < len(OUT_UNITS):
                        high(s, U_WO + w, w % WR, 256 if OUT_UNITS[w][0] == "value" else 512)
                act.wait_ge(w_used, used(s, U_FF - 1))
                for kp in range(4):
                    norm_high(s, 1, kp)
                norm_square(s, 1)
                for c in range(2):
                    act.wait_ge(ctx_dma[c], s * (16 * NC // 4) + (16 * NC // 4 + 16))
                    act.activation(CSPL[:, c, 0, :], CRAW[:, c, :], ACT.Copy).then_inc(S["ctx_hi"], 1)
                norm_std(s, 1)
                for m in range(KD):
                    act.wait_ge(ff_t, s * KD + m + 5)
                    act.activation(TMP[:, m % 2, :], TMP[:, m % 2, :], ACT.Identity, bias=BIAS[:, m:m + 1],
                                   scale=ALPHA2[:, m:m + 1]).then_inc(S["ff_ab"], 1)

        @block.vector
        def _(dve):
            give_credits(dve, "dve")
            dve.memset(eps[:, :], EPS).then_inc(S["idx_chain"], 1)
            dve.wait_ge(seg_dma, 16 * 2)
            segi, segf = SEG_I, SEG_F
            k_, a_, b_, m_ = IDX_TMP
            link = [1]

            def chain(ins):
                link[0] += 1
                ins.then_inc(S["idx_chain"], 1)
                dve.wait_ge(S["idx_chain"], link[0])

            chain(dve.tensor_copy(segf, segi))
            dve.tensor_scalar(segf, segf, -1.0, float(LK + LOOKBACK), ALU.max, ALU.min).then_inc(S["idx_seg"], 1)
            dve.wait_ge(S["idx_mm"], 1)
            chain(dve.tensor_scalar(a_, PS[0:TK, 1, 0:128], 0.0, None, ALU.is_ge))
            chain(dve.tensor_scalar(b_, PS[0:TK, 1, 0:128], float(LK - 1 + LOOKBACK), None, ALU.is_le))
            chain(dve.tensor_tensor(a_, a_, b_, ALU.mult))
            chain(dve.tensor_scalar(k_, PS[0:TK, 1, 0:128], PRE[0:TK, P_J:P_J + 1], None, ALU.subtract))
            chain(dve.tensor_scalar(b_, k_, 0.0, None, ALU.is_ge))
            chain(dve.tensor_scalar(m_, k_, float(LK - 1), None, ALU.is_le))
            chain(dve.tensor_tensor(b_, b_, m_, ALU.mult))
            chain(dve.scalar_tensor_tensor(out=b_, in0=k_, scalar=float(MASKED_ROW), in1=b_, op0=ALU.subtract, op1=ALU.mult))
            chain(dve.scalar_tensor_tensor(out=b_, in0=b_, scalar=float(MASKED_ROW - MEAN_ROW), in1=a_, op0=ALU.add, op1=ALU.mult))
            chain(dve.scalar_tensor_tensor(out=b_, in0=b_, scalar=float(MEAN_ROW), in1=PRE[0:TK, P_BASE:P_BASE + 128],
                                           op0=ALU.add, op1=ALU.add))
            dve.tensor_copy(IDX[0:TK, :], b_).then_inc(S["idx_ready"], 1)
            dve.wait_ge(S["w0_hi"], 2)
            chain(dve.tensor_tensor(KVW[:, 1, :, 0:KVC], KVC_F.rearrange("p (k n) -> p k n", k=KD),
                                    KVW[:, 0, :, 0:KVC].bitcast(f32), ALU.subtract))
            dve.tensor_tensor(KVW[:, 1, :, KVC:KVR], PS[:, 0, :].rearrange("p (k n) -> p k n", k=KD),
                              KVW[:, 0, :, KVC:KVR].bitcast(f32), ALU.subtract).then_inc(S["w0_lo"], 1)
            def ctx_low(n, c):
                dve.wait_ge(S["ctx_hi"], n + 1)
                dve.tensor_tensor(CSPL[:, c % 3, 1, :], CRAW[:, c % 4, :], CSPL[:, c % 3, 0, :].bitcast(f32),
                                  ALU.subtract).then_inc(S["ctx_lo"], 1)

            ctx_low(0, 0)
            ctx_low(1, 1)
            dve.wait_ge(const_dma, 16 * 2)
            dve.wait_ge(S["alpha_abs"], KD)
            dve.tensor_scalar(ALPHA2[:, :], ALPHA[:, :], 2.0 / D, None, ALU.mult).then_inc(S["alpha_ready"], 1)

            def norm_sum(s, l):
                dve.tensor_reduce(TMP[:, 0, :], X[:, :, :].rearrange("p k n -> p n k"), AX.X, ALU.add).then_inc(S["ln_sum"], 1)

            def norm_center(s, l, kp):
                if kp == 0:
                    dve.wait_ge(S["ln_mean_mm"], s * 2 + l + 1)
                dve.tensor_tensor(CEN[:, 2 * kp:2 * kp + 2, :], X[:, 2 * kp:2 * kp + 2, :],
                                  psn(2)[:, None, :].to_broadcast([128, 2, N]), ALU.subtract).then_inc(S["ln_sub"], 1)

            def norm_low(s, l, kp):
                dve.wait_ge(S["y_hi"], s * 8 + 4 * l + kp + 1)
                dve.tensor_tensor(Y[:, 1, 2 * kp:2 * kp + 2, :], CEN[:, 2 * kp:2 * kp + 2, :],
                                  Y[:, 0, 2 * kp:2 * kp + 2, :].bitcast(f32), ALU.subtract).then_inc(S["y_lo"], 1)

            def norm_sqsum(s, l):
                dve.wait_ge(S["ln_sq"], s * 2 + l + 1)
                dve.tensor_reduce(TMP[:, 1, :], SQ[:, :, :].rearrange("p k n -> p n k"), AX.X, ALU.add).then_inc(S["ln_sqsum"], 1)

            def norm_rstd(s, l):
                n = s * 2 + l
                dve.wait_ge(S["ln_std"], n + 1)
                dve.reciprocal(RSTD, TMP[:, 0, :]).then_inc(S["ln_inv"], 1)
                dve.wait_ge(S["ln_inv"], n + 1)
                dve.tensor_tensor(TMP[:, 1, :], RSTD, RSTD, ALU.mult).then_inc(S["ln_n1"], 1)
                dve.wait_ge(S["ln_n1"], n + 1)
                dve.scalar_tensor_tensor(out=TMP[:, 1, :], in0=TMP[:, 1, :], scalar=-0.5, in1=VE, op0=ALU.mult,
                                         op1=ALU.mult).then_inc(S["ln_n2"], 1)
                dve.wait_ge(S["ln_n2"], n + 1)
                dve.scalar_tensor_tensor(out=RSTD, in0=TMP[:, 1, :], scalar=1.5, in1=RSTD, op0=ALU.add,
                                         op1=ALU.mult).then_inc(ln_rstd, 1)

            with dve.Fori(0, NS) as s:
                for c in range(NC):
                    n, e, t = s * NC + c, c % 2, c % CPB
                    if c + 2 < NC:
                        ctx_low(n + 2, c + 2)
                    dve.wait_ge(row_kv, n + 3)
                    dve.wait_ge(row_sum, n + 1)
                    for w in range(2):
                        cs = C[0:CK, C_KCS + R * t + HALF * w:C_KCS + R * t + HALF * (w + 1)]
                        ins = dve.tensor_tensor(RT[0:CK, e, w, :].rearrange("p (a n) -> p a n", a=2),
                                                PS[0:CK, 6 + e, KVC:KVR].rearrange("p (a n) -> p a n", a=2),
                                                cs[:, None, :].to_broadcast([CK, 2, HALF]), ALU.mult)
                    ins.then_inc(row_rt, 1)
                    if c == 3:
                        dve.wait_ge(x_dma, s * 16 + 16)
                        norm_sum(s, 0)
                    if c in (6, 7):
                        norm_center(s, 0, 2 * (c - 6))
                        norm_center(s, 0, 2 * (c - 6) + 1)
                    if c in (8, 9):
                        norm_low(s, 0, 2 * (c - 8))
                        norm_low(s, 0, 2 * (c - 8) + 1)
                    if c == 10:
                        norm_sqsum(s, 0)
                norm_rstd(s, 0)
                dve.wait_ge(ln_rstd, s * 2 + 2)
                for m in range(KC):
                    n = s * KC + m
                    if m < KC - 1:
                        dve.wait_ge(S["qc_mm"], s * (KC - 1) + m + 1)
                    else:
                        dve.wait_ge(w_used, used(s, U_PAIR - 1))
                    dve.tensor_tensor(TMP[:, m % 2, :], psn(4 + m), RSTD, ALU.mult).then_inc(S["qc_f"], 1)
                    dve.wait_ge(S["qc_hi"], n + 1)
                    dve.tensor_tensor(QCS[:, 1, m, :], TMP[:, m % 2, :], QCS[:, 0, m, :].bitcast(f32),
                                      ALU.subtract).then_inc(S["qc_lo"], 1)

                with dve.Fori(0, PAIRS) as p:
                    for h in range(2):
                        n = s * H + p * 2 + h
                        dve.wait_ge(S["nope_hi"], n + 1)
                        dve.tensor_tensor(NOPE[:, h, 1, :], psn(h), NOPE[:, h, 0, :].bitcast(f32),
                                          ALU.subtract).then_inc(S["nope_lo"], 1)
                    n = s * PAIRS + p
                    dve.wait_ge(S["rp_hi"], n + 1)
                    dve.tensor_tensor(RSP[:, 1, :], psn(4), RSP[:, 0, :].bitcast(f32), ALU.subtract).then_inc(S["rp_lo"], 1)
                    dve.wait_ge(rope_ev, n + 1)
                    rep = [128, BPS, LQ]
                    dve.tensor_tensor(TMP[:, 0, :].rearrange("p (b n) -> p b n", b=BPS), psn(4).rearrange("p (b n) -> p b n", b=BPS),
                                      C[:, C_QC:C_QC + LQ][:, None, :].to_broadcast(rep), ALU.mult).then_inc(rope_t1, 1)
                    dve.wait_ge(S["abs_mm"], s * H + p * 2 + 2)
                    dve.tensor_scalar(QKV[:, :, ds(p + PAIRS, 1), :].rearrange("p d a n -> p d (a n)"), PS[:, 5:7, 0:N], 1.0, None, ALU.mult).then_inc(abs_odd, 1)
                    dve.wait_ge(S["swap_mm"], n + 1)
                    dve.tensor_tensor(TMP[:, 1, :].rearrange("p (b n) -> p b n", b=BPS), psn(7).rearrange("p (b n) -> p b n", b=BPS),
                                      C[:, C_QS:C_QS + LQ][:, None, :].to_broadcast(rep), ALU.mult).then_inc(rope_t2, 1)

                def step(s, i, r):
                    n, q = s * NT + i, r
                    if has(i, 0):
                        sm = SM[0:PQ, q % 4, :, :]
                        dve.wait_ge(st_mm, n + 3)
                        dve.wait_ge(pt_mm, n + 1)
                        dve.tensor_tensor(sm, PS[0:PQ, 3 + q % 2, 0:2 * TK].rearrange("p (e n) -> p e n", e=2),
                                          BM[:, None, :].to_broadcast([PQ, 2, TK]), ALU.add).then_inc(sm_mask, 1)
                        dve.wait_ge(sm_mask, n + 3)
                        dve.tensor_reduce(SMAX[0:PQ, q % 4, :], sm, AX.X, ALU.min).then_inc(S["sm_max"], 1)
                    if has(i, 3):
                        m = n - 3
                        dve.wait_ge(pv_mm, m + GR + 1)
                        dve.tensor_scalar(QKV2[:, :, ds(i * QT_ - 3 * QT_, QT_)],
                                          PS[:, 6 + (q - 3) % 2, 0:KV * HQ].rearrange("p (e n) -> p e n", n=QT_),
                                          1.0, None, ALU.mult).then_inc(pv_ev, 1)
                    if has(i, 0):
                        dve.wait_ge(S["sm_exp"], n + 1)
                        dve.reciprocal(SSUM[0:PQ, q % 4, :], SSUM[0:PQ, q % 4, :]).then_inc(S["sm_rec"], 1)

                steps(dve, step, s, NT + 3)

                def sum_low(n):
                    dve.wait_ge(S["cs_hi"], s * H + n + 1)
                    dve.tensor_tensor(CS[:, n % 2, 1, :, :], QKV[:, :, n, :], CS[:, n % 2, 0, :, :].bitcast(f32),
                                      ALU.subtract).then_inc(S["cs_lo"], 1)

                dve.wait_ge(pv_ev, s * NT + NT + 2)
                sum_low(0)
                sum_low(1)
                for v, (kind, i) in enumerate(OUT_UNITS):
                    if kind == "value":
                        g, j = i // G4, i % G4
                        dve.wait_ge(S["att_hi"], s * H + i + 1)
                        dve.tensor_tensor(ATT[:, g % 2, 1, j, :], psn(i % 2), ATT[:, g % 2, 0, j, :].bitcast(f32),
                                          ALU.subtract).then_inc(att_lo, 1)
                        if i + 2 < H:
                            sum_low(i + 2)
                    else:
                        g, m = i // KD, i % KD
                        n = s * (KD * H // G4) + i
                        dve.wait_ge(w_used, used(s, U_WO + v))
                        if g:
                            dve.wait_ge(x_add, n - KD + 5)
                        dve.tensor_tensor(X[:, m, :], X[:, m, :], psn(4 + m % 4), ALU.add).then_inc(x_add, 1)
                        if g == H // G4 - 1 and m:
                            dve.wait_ge(x_add, n + 5)
                            if m > 1:
                                dve.wait_ge(S["ln_part"], s * (KD - 2) + m - 1)
                            dve.tensor_tensor(TMP[:, 0, :], X[:, 0, :] if m == 1 else TMP[:, 0, :], X[:, m, :],
                                              ALU.add).then_inc(S["ln_part"] if m < KD - 1 else S["ln_sum"], 1)

                def signs(v):
                    dve.wait_ge(w_dma[v % WR], s * (UNITS // WR * 16) + ((U_FF + v) // WR + 1) * 16)
                    dve.wait_ge(w_used, s * UNITS + U_FF + v + 1)
                    dve.tensor_scalar(WHI[:, v % WR, :], WRAW[:, v % WR, :], 0.0, 0.5, ALU.is_ge, ALU.subtract).then_inc(w_sgn, 1)

                signs(0)
                norm_center(s, 1, 0)
                norm_center(s, 1, 1)
                norm_low(s, 1, 0)
                signs(1)
                norm_center(s, 1, 2)
                norm_low(s, 1, 1)
                signs(2)
                norm_center(s, 1, 3)
                norm_low(s, 1, 2)
                signs(3)
                norm_low(s, 1, 3)
                signs(4)
                norm_sqsum(s, 1)
                for v in range(5, 14):
                    signs(v)
                norm_rstd(s, 1)
                dve.wait_ge(ln_rstd, s * 2 + 3)
                for m in range(KD):
                    n = s * KD + m
                    h = m // HALF_M
                    dve.wait_ge(w_used, used(s, U_FF + KD * (h + 1) - 1))
                    if m >= 2:
                        dve.wait_ge(S["ff_add"], n - 1)
                    dve.tensor_tensor(TMP[:, m % 2, :], psn(4 * (1 - h) + m % 4), RSTD, ALU.mult).then_inc(ff_t, 1)
                    if m < 2:
                        signs(14 + m)
                    if m == HALF_M - 1:
                        ctx_low(s * NC + NC, 0)
                        ctx_low(s * NC + NC + 1, 1)

        @block.tensor
        def _(pe):
            give_credits(pe, "pe")
            pe.wait_ge(fold_dma, 16 * 3)
            for m in range(KD):
                for k in range(KV):
                    last = pe.matmul(PS[:, 0, R * m:R * (m + 1)], KVC_T[:, D * k + 128 * m:D * k + 128 * (m + 1)],
                                     KR_F[:, R * k:R * (k + 1)], start=(k == 0), stop=(k == KV - 1))
            last.then_inc(S["fold_mm"], 1)
            pe.wait_ge(S["idx_seg"], 1)
            pe.matmul(PS[0:TK, 1, 0:128], PRE[0:QT_, P_E14:P_E14 + TK], SEG_F,
                      start=True, stop=True).then_inc(S["idx_mm"], 1)
            pe.wait_ge(S["w0_lo"], 1)

            def three(out_, whi, wlo, xhi, xlo, first, final):
                pe.matmul(out_, whi, xhi, start=first, stop=False)
                pe.matmul(out_, whi, xlo, start=False, stop=False)
                return pe.matmul(out_, wlo, xhi, start=False, stop=final)

            def w_tile(slot, t):
                return WHI[:, slot, 128 * t:128 * (t + 1)], WLO[:, slot, 128 * t:128 * (t + 1)]

            with pe.Fori(0, NS) as s:
                pe.wait_ge(ff_t, s * KD + 1)
                for c in range(NC):
                    n, e = s * NC + c, c % 2
                    pe.wait_ge(S["ctx_lo"], n + 1)
                    pe.wait_ge(row_rt, n + 1)
                    pe.wait_ge(row_kv, n + 1)
                    for k in range(KD):
                        hi, lo = (CSPL[:, c % 3, z, CK * k:CK * (k + 1)] for z in range(2))
                        last = three(PS[0:CK, 6 + e, 0:KVR], hi, lo, KVW[:, 0, k, :], KVW[:, 1, k, :], k == 0, k == KD - 1)
                    last.then_inc(S["tab_mm"], 1)
                    if c == 5:
                        pe.wait_ge(S["ln_sum"], s * 2 + 1)
                        pe.matmul(psn(2), ONES, TMP[:, 0, :], start=True, stop=True).then_inc(S["ln_mean_mm"], 1)
                    if c == NC - 1:
                        pe.wait_ge(const_dma, 16 * 2)
                        pe.wait_ge(S["perm_ready"], 1)
                        pe.wait_ge(S["ln_sqsum"], s * 2 + 1)
                        pe.matmul(psn(3), ONES, TMP[:, 1, :], start=True, stop=True).then_inc(S["ln_var_mm"], 1)

                for m in range(KC):
                    for k in range(KD):
                        t = m * KD + k
                        u, v = t // 3, t % 3
                        if v == 0:
                            pe.wait_ge(S["w_lo"], s * SPLIT_UNITS + u + 1)
                        if m == 0 and k % 2 == 0:
                            pe.wait_ge(S["y_lo"], s * 8 + k // 2 + 1)
                        hi, lo = w_tile(u % WR, v)
                        last = three(psn(4 + m), hi, lo, Y[:, 0, k, :], Y[:, 1, k, :], k == 0, k == KD - 1)
                        if v == 2:
                            last.then_inc(w_used, 1)
                    if m < KC - 1:
                        last.then_inc(S["qc_mm"], 1)
                    if m == 0:
                        pe.wait_ge(row_sum, s * NC + NC + 2)
                        pe.matmul(PS[0:1, 7, :].rearrange("p (b n) -> p b n", b=BPS), C[0:CK, C_W750:C_W750 + 1],
                                  G[0:CK, 0:BPS, R:R + KVC], start=True, stop=True).then_inc(mean_mm, 1)

                with pe.Fori(0, PAIRS) as p:
                    pe.wait_ge(S["qc_lo"], s * KC + KC)

                    def unit_ready(v):
                        pe.wait_ge(S["w_lo"], s * SPLIT_UNITS + p * 4 + (U_PAIR + v + 1))

                    def up(bank, slot):
                        for k in range(KC):
                            hi, lo = w_tile(slot, k)
                            last = three(psn(bank), hi, lo, QCS[:, 0, k, :], QCS[:, 1, k, :], k == 0, k == KC - 1)
                        return last

                    def absorb(h, bank):
                        pe.wait_ge(S["nope_lo"], s * H + p * 2 + h + 1)
                        for d in range(KV):
                            hi, lo = w_tile(3, 2 * h + d)
                            last = three(psn(bank + d), hi, lo, NOPE[:, h, 0, :], NOPE[:, h, 1, :], True, True)
                        return last

                    n = s * PAIRS + p
                    for h in range(2):
                        unit_ready(h)
                        up(h, h).then_inc(w_used, 1)
                    unit_ready(2)
                    pe.wait_ge(rope_t1, n + 1)
                    up(4, 2).then_inc(w_used, 1)
                    unit_ready(3)
                    pe.wait_ge(abs_even, n + 1)
                    absorb(0, 2).then_inc(S["abs_mm"], 1)
                    pe.wait_ge(abs_odd, n + 1)
                    absorb(1, 5).then_inc(S["abs_mm"], 1)
                    pe.wait_ge(S["rp_lo"], n + 1)
                    pe.wait_ge(rope_t2, n + 1)
                    pe.matmul(psn(7), PERM[:, :], RSP[:, 0, :], start=True, stop=False).then_inc(w_used, 1)
                    pe.matmul(psn(7), PERM[:, :], RSP[:, 1, :], start=False, stop=True).then_inc(S["swap_mm"], 1)
                def step(s, i, r):
                    tile = s * NT + i
                    if has(i, 0):
                        pe.wait_ge(g_dma[r], s * (NT // GR * 16) + (i // GR + 1) * 16 if isinstance(i, int) else gd(s, i, r))
                        pe.wait_ge(kt_ev, tile + 1)
                        for w, col in enumerate((0, R, 3 * R, 3 * R + 128)):
                            last = pe.transpose(PS[:, 0, TK * w:TK * (w + 1)], G[0:TK, r, col:col + 128], IDENT[0:TK, 0:TK])
                        last.then_inc(S["kt_mm"], 1)
                    if has(i, 1):
                        n, q = tile - 1, (r - 1) % GR
                        if isinstance(i, int) and i == 1:
                            pe.wait_ge(abs_even, s * PAIRS + PAIRS + 1)
                            pe.wait_ge(abs_odd, s * PAIRS + PAIRS + 1)
                            pe.wait_ge(rope_ev, s * PAIRS + PAIRS + 1)
                        pe.wait_ge(kt_ev, n + 2)
                        pe.wait_ge(s_ev, n + 1)
                        keys, ps = KT[:, q % 2, :], PS[0:TK, 1 + q % 2, 0:HQ]
                        cols = ds(i * QT_ - QT_, QT_)
                        for d in range(KV):
                            pe.matmul(ps, keys[:, TK * (2 + d):TK * (3 + d)], QKV[:, d, :, cols], start=(d == 0), stop=False)
                        for e in range(2):
                            last = pe.matmul(ps[:, PQ * e:PQ * (e + 1)], keys[:, TK * (1 - e):TK * (2 - e)], QR[:, :, cols],
                                             start=False, stop=(e == 1))
                        last.then_inc(s_mm, 1)
                    if has(i, 2):
                        n, q = tile - 2, (r - 2) % GR
                        pe.wait_ge(s_ev, n + 3)
                        pe.wait_ge(sm_mask, n + 1)
                        for e in range(2):
                            last = pe.transpose(PS[0:PQ, 3 + q % 2, TK * e:TK * (e + 1)], SSB[0:TK, q % 2, PQ * e:PQ * (e + 1)],
                                                IDENT[0:TK, 0:TK])
                        last.then_inc(st_mm, 1)
                    if has(i, PT_LAG):
                        n, q = tile - PT_LAG, (r - PT_LAG) % GR
                        pe.wait_ge(S["sm_norm"], n + 1)
                        pe.wait_ge(pt_ev, n + 1)
                        for e in range(2):
                            last = pe.transpose(PS[0:TK, 5, PQ * e:PQ * (e + 1)], SM[0:PQ, q % 4, e, :], IDENT[0:PQ, 0:PQ])
                        last.then_inc(pt_mm, 1)
                    if has(i, LAG):
                        n, q = tile - LAG, (r - LAG) % GR
                        pe.wait_ge(pt_ev, n + 2)
                        pe.wait_ge(pv_ev, n + 1)
                        for d in range(KV):
                            last = pe.matmul(PS[:, 6 + q % 2, HQ * d:HQ * (d + 1)], G[0:TK, q, 3 * R + 128 * d:3 * R + 128 * (d + 1)],
                                             PT[0:TK, q % 2, :], start=True, stop=True)
                        last.then_inc(pv_mm, 1)

                def gd(s, i, r):
                    return s * (NT // GR * 16) + (i - r) * 2 + 16

                steps(pe, step, s, NT + LAG)

                for v, (kind, i) in enumerate(OUT_UNITS):
                    slot = v % WR
                    pe.wait_ge(S["w_lo"], s * SPLIT_UNITS + U_WO + v + 1)
                    if kind == "value":
                        pe.wait_ge(S["cs_lo"], s * H + i + 1)
                        pe.wait_ge(att_lo, s * H + i + 1)
                        for d in range(KV):
                            hi, lo = w_tile(slot, d)
                            last = three(psn(i % 2), hi, lo, CS[:, i % 2, 0, d, :], CS[:, i % 2, 1, d, :], d == 0, d == KV - 1)
                    else:
                        g, m = i // KD, i % KD
                        pe.wait_ge(x_add, s * (KD * H // G4) + i + 1)
                        for j in range(G4):
                            if m == 0:
                                pe.wait_ge(att_lo, s * H + G4 * g + j + 3)
                            hi, lo = w_tile(slot, j)
                            last = three(psn(4 + m % 4), hi, lo, ATT[:, g % 2, 0, j, :], ATT[:, g % 2, 1, j, :], j == 0, j == G4 - 1)
                    last.then_inc(w_used, 1)

                pe.wait_ge(S["ln_sum"], s * 2 + 2)
                pe.matmul(psn(2), ONES, TMP[:, 0, :], start=True, stop=True).then_inc(S["ln_mean_mm"], 1)
                for h in range(2):
                    for k in range(KD):
                        v = KD * h + k
                        if v == KD:
                            pe.wait_ge(S["ln_sqsum"], s * 2 + 2)
                            pe.matmul(psn(3), ONES, TMP[:, 1, :], start=True, stop=True).then_inc(S["ln_var_mm"], 1)
                        pe.wait_ge(w_sgn, s * 16 + v + 5)
                        if h == 0 and k % 2 == 0:
                            pe.wait_ge(S["y_lo"], s * 8 + 4 + k // 2 + 1)
                        order = [(j, part) for j in range(HALF_M) for part in range(2)] if h else [
                            (j, part) for part in range(2) for j in range(HALF_M)]
                        for j, part in order:
                            hi, _ = w_tile(v % WR, j)
                            if h and k == 0 and j == HALF_M - 1 and part == 0:
                                pe.wait_ge(S["ln_ve"], s * 2 + 2)
                            last = pe.matmul(psn(4 * (1 - h) + j), hi, Y[:, part, k, :], start=(k == 0 and part == 0),
                                             stop=(k == KD - 1 and part == 1))
                        last.then_inc(w_used, 1)


def kernel(**inputs):
    import numpy as np
    import concourse.bacc as bacc
    from concourse.bass_utils import run_bass_kernel_spmd

    a = {k.replace("L0_xattn_", "").replace("L0_ffn_", "ffn_"): np.asarray(v) for k, v in inputs.items()}

    def blocks(w, kd, nd):
        return w.reshape(kd, 128, nd, 128).transpose(2, 1, 0, 3)

    heads = [2 * (h % PAIRS) + h // PAIRS for h in range(H)]
    lay = {}
    lay["x"] = a["x"].reshape(NS, N, KD, 128).transpose(0, 3, 2, 1).reshape(NS, 128, KD * N)
    lay["ctx"] = a["ctx_2048"].reshape(B * CPB, CK, KD, 128).transpose(0, 3, 2, 1).reshape(B * CPB, 128, KD * CK)
    lay["ctx"] = np.concatenate([lay["ctx"], np.zeros((4, 128, KD * CK), np.float32)])
    lay["seg"] = a["itok_BxS_0_1023"].reshape(NS * NT, QT_).T
    lay["kvc"] = a["W_kvc"].reshape(KD, 128, KVC).transpose(1, 0, 2).reshape(128, KD * KVC)
    lay["kvct"] = a["W_kvc"].T.reshape(KV, 128, D).transpose(1, 0, 2).reshape(128, KV * D)
    lay["kr"] = a["W_kr"].reshape(KV, 128, R).transpose(1, 0, 2).reshape(128, KV * R)
    dq = blocks(a["W_dq"], KD, KC)
    lay["dq"] = dq.transpose(0, 2, 1, 3).reshape(8, 3, 128, 128).transpose(0, 2, 1, 3).reshape(8, 128, 384)
    lay["uq"] = blocks(a["W_uq"], KC, H).reshape(H, 128, KC * 128)
    uk = a["W_uk"].reshape(KV, 128, PAIRS, 2, HD)
    lay["uk"] = uk.transpose(2, 4, 3, 0, 1).reshape(PAIRS, 128, 2 * KV * 128)
    lay["qr"] = blocks(a["W_qr"], KC, PAIRS).reshape(PAIRS, 128, KC * 128)
    lay["uv"] = blocks(a["W_uv"], KV, H)[heads].reshape(H, 128, KV * HD)
    wo = a["W_o"].reshape(H, HD, KD, 128)[heads].reshape(H // G4, G4, HD, KD, 128)
    lay["wo"] = wo.transpose(0, 3, 2, 1, 4).reshape(H // G4 * KD, 128, G4 * 128)
    ff = a["ffn_weight"].reshape(2, HALF_M, 128, KD, 128)
    lay["ff"] = ff.transpose(0, 3, 4, 1, 2).reshape(2 * KD, 128, HALF_M * 128)
    lay["ffn"] = a["ffn_weight"].reshape(KD, 128, D).transpose(1, 0, 2).reshape(128, KD * D)
    lay["bias"] = a["ffn_bias"].reshape(KD, 128).T
    lay["cst"], lay["pre"] = constants()

    nc = bacc.Bacc("TRN2", target_bir_lowering=False, num_devices=1)
    arrays, args = {}, []
    for name, v in lay.items():
        v = np.ascontiguousarray(v)
        arrays[f"in_{name}"] = v
        args.append(nc.dram_tensor(f"in_{name}", v.shape, mybir.dt.from_np(v.dtype), kind="ExternalInput").ap())
    out = nc.dram_tensor("out_t", (NS, 128, KD * N), mybir.dt.float32, kind="ExternalOutput").ap()
    program(nc, *args, out)
    r = run_bass_kernel_spmd(nc, [arrays], core_ids=[0])
    y = r.results[0]["out_t"].reshape(NS, 128, KD, N).transpose(0, 3, 2, 1)
    return np.ascontiguousarray(y.reshape(B, LQ, D))
```

```python
import math

import concourse.bass as bass
from concourse import mybir
from contextlib import ExitStack

B, LQ, D = 8, 224, 1024
LK = 750
H, HD = 16, 128
KVC, QC, R = 256, 384, 64
LOOKBACK = 8
NEG = -1e30
EPS = 1e-5
SCALE = 1.0 / math.sqrt(HD + R)
HALF = R // 2

T = B * LQ
NS = 4
N = T // NS
BPS = B // NS
W = LOOKBACK + 1
QT_ = 14
TK = QT_ * W
NT = N // QT_
TPB = LQ // QT_
PAIRS = H // 2
PQ = PAIRS * QT_
HQ = H * QT_
KD, KC, KV = D // 128, QC // 128, KVC // 128
CK = 125
CPB = LK // CK
NC = BPS * CPB
PREFETCH = 7
ROWS = LK + 2
MEAN_ROW, MASKED_ROW = LK, LK + 1
KVR = KVC + R
TW = R + R + KVC + 1
GR = 8
AHEAD = 6
EARLY = 28
PT_LAG, LAG = 4, 5

UW = 512
WR = 4
U_DQ, U_PAIR, U_WO, U_FF = 0, 8, 40, 88
UNITS = 104
SPLIT_UNITS = U_FF
NORM = [(0, 1), (1, 2), (2, 4), (4, 6), (6, 8)]
NG = len(NORM)
G4 = 4
HALF_M = KD // 2
OUT_UNITS = [("value", n) for n in range(G4)]
for g_ in range(H // G4):
    for j_ in range(G4):
        OUT_UNITS.append(("output", KD * g_ + 2 * j_))
        if g_ + 1 < H // G4:
            OUT_UNITS.append(("value", G4 * (g_ + 1) + j_))
        OUT_UNITS.append(("output", KD * g_ + 2 * j_ + 1))

C_ID, C_BM = 0, 128
C_QC = C_BM + TK
C_QS = C_QC + LQ
C_KCS = C_QS + LQ
C_ONE = C_KCS + CPB * R
C_W750 = C_ONE + 128
CW = C_W750 + 1
P_PERM, P_E14 = 0, 128
P_J = P_E14 + TK
P_BASE = P_J + 1
PW = P_BASE + NS * NT


def constants():
    import numpy as np
    c = np.zeros((128, CW), np.float32)
    c[:, C_ID:C_ID + 128] = np.eye(128)
    q_of_row = np.arange(PQ) % QT_
    q_of_key = np.arange(TK) // W
    c[:PQ, C_BM:C_BM + TK] = np.where(q_of_row[:, None] == q_of_key[None, :], 0.0, -NEG)
    inv = (1.0 / np.float32(10000.0) ** (np.arange(HALF, dtype=np.float32) / np.float32(HALF))).astype(np.float32)
    ang = np.arange(LK, dtype=np.float32)[:, None] * inv
    cos, sin = np.cos(ang).astype(np.float32), np.sin(ang).astype(np.float32)
    c[:, C_QC:C_QC + LQ] = np.concatenate([cos[:LQ].T] * 4, 0)
    c[:, C_QS:C_QS + LQ] = np.concatenate([-sin[:LQ].T, sin[:LQ].T] * 2, 0)
    kcs = np.concatenate([cos, sin], 1).reshape(CPB, CK, R).transpose(1, 0, 2)
    c[:CK, C_KCS:C_KCS + CPB * R] = kcs.reshape(CK, -1)
    c[:, C_ONE:C_ONE + 128] = 1.0 / D
    c[:CK, C_W750] = np.float32(1.0) / np.float32(LK)
    p = np.zeros((128, PW), np.float32)
    r = np.arange(128)
    p[(r // R) * R + (r % R + HALF) % R, P_PERM + r] = 1.0
    p[q_of_key, P_E14 + np.arange(TK)] = 1.0
    p[:TK, P_J] = np.arange(TK) % W
    p[:, P_BASE:] = (np.arange(NS * NT) // TPB % BPS * ROWS)[None, :]
    return c, p


def program(nc, x, ctx, seg, kvc, kvct, kr, dq, uq, uk, qr, uv, wo, ff, ffn, bias, cst, pre, out):
    f32, f32r, i32 = mybir.dt.float32, mybir.dt.float32r, mybir.dt.int32
    ALU, ACT, AX = mybir.AluOpType, mybir.ActivationFunctionType, mybir.AxisListType
    ds = bass.ds

    table = nc.dram_tensor("key_table", (BPS * ROWS, TW), f32).ap()

    ctx_ = ExitStack()
    with ctx_:
        def sb(name, shape, dt=f32):
            return ctx_.enter_context(nc.sbuf_tensor(name, shape, dt))

        def sem(name):
            return ctx_.enter_context(nc.semaphore(name))

        with nc.sbuf_tensor("big_split", [128, KV * H * N + PAIRS * N], f32r) as BIG_R:
            pass
        BIG = sb("big", [128, KV * H * N + PAIRS * N])
        SPL = sb("split", [128, 2 * KD * N], f32r)
        X = sb("x_sb", [128, KD, N])
        QCS = sb("qc_split", [128, 2, KC, N], f32r)
        G = sb("gathered", [128, GR, TW])
        KT = sb("keys_t", [128, 2, 4 * TK])
        SOFT = sb("soft", [128, 2 * HQ + 4 * 2 * TK + 2 * HQ])
        WRAW = sb("w_raw", [128, WR, UW])
        WHI = sb("w_high", [128, WR, UW], f32r)
        WLO = sb("w_low", [128, WR, UW], f32r)
        KVW = sb("kv_weights", [128, 2, KD, KVR], f32r)
        C = sb("consts", [128, CW])
        PERM = sb("perm", [128, 128], f32r)
        ROW = sb("row", [128, 2, TW])
        RT = sb("row_rope_tmp", [128, 2, 2, R])
        IDX = sb("idx", [128, NS * NT], i32)
        IDXR = sb("idx_ring", [128, GR], i32)
        BIAS = sb("bias_sb", [128, KD])
        ALPHA, ALPHA2 = sb("alpha", [128, KD]), sb("alpha2", [128, KD])
        eps = sb("eps", [128, 1])
        PS = ctx_.enter_context(nc.psum_tensor("ps", [128, 8, 512], f32))

        QL = BIG[:, 0:KV * H * N].rearrange("p (d h n) -> p d h n", d=KV, h=H)
        QL_ROWS = BIG[:, 0:KV * H * N].rearrange("p (e n) -> p e n", n=N)
        QR = BIG[:, KV * H * N:].rearrange("p (a n) -> p a n", a=PAIRS)
        CRAW = BIG[:, 0:4 * KD * CK].rearrange("p (b k n) -> p b (k n)", b=4, k=KD)
        o = 4 * KD * CK
        CEN = BIG[:, o:o + KD * N].rearrange("p (k n) -> p k n", k=KD)
        SQ = BIG[:, o + KD * N:o + 2 * KD * N].rearrange("p (k n) -> p k n", k=KD)
        XN = SQ
        o += 2 * KD * N
        CSPL = BIG_R[:, o:o + 3 * 2 * KD * CK].rearrange("p (b s n) -> p b s n", b=3, s=2)
        Y = SPL[:, :].rearrange("p (s k n) -> p s k n", s=2, k=KD)
        NOPE = SPL[:, 0:4 * N].rearrange("p (b s n) -> p b s n", b=2, s=2)
        RSP = SPL[:, 4 * N:6 * N].rearrange("p (s n) -> p s n", s=2)
        ATT = SPL[:, :].rearrange("p (b s j n) -> p b s j n", b=2, s=2, j=G4)
        CS = BIG_R[:, KV * H * N:].rearrange("p (b s d n) -> p b s d n", b=2, s=2, d=KV)
        CS_FIRST = SPL[:, 2 * G4 * N:].rearrange("p (b s d n) -> p b s d n", b=2, s=2, d=KV)
        o = 4 * KD * CK
        PRE, SEG_I, SEG_F = BIG[:, o:o + PW], BIG[0:QT_, o + 384:o + 512].bitcast(i32), BIG[0:QT_, o + 512:o + 640]
        IDX_TMP = [BIG[0:TK, o + 640 + 128 * i:o + 768 + 128 * i] for i in range(4)]
        o += 1152
        KVC_T, KR_F = BIG[:, o:o + KV * D], BIG[:, o + KV * D:o + KV * D + KV * R]
        KVC_F = WRAW[:, :, :].rearrange("p b n -> p (b n)")
        FF_ROWS = [X[:, :, :].rearrange("p k n -> p (k n)")[:, D * i:D * (i + 1)] for i in range(3)] + [SOFT[:, 0:D]]
        FF_ROWS += [KVC_T[:, 0:D], KVC_T[:, D:2 * D], KVC_F[:, 0:D], KVC_F[:, D:2 * D]]
        RSTD, VE = SOFT[:, 0:N], SOFT[:, N:2 * N]
        XSUM = G[:, 4:7, :].rearrange("p b n -> p (b n)")[:, 0:2 * N].rearrange("p (b n) -> p b n", b=2)
        TMP = SOFT[:, 2 * N:4 * N].rearrange("p (b n) -> p b n", b=2)
        SSB = SOFT[:, 0:2 * HQ].rearrange("p (b n) -> p b n", b=2)
        SM = SOFT[:, 2 * HQ:2 * HQ + 8 * TK].rearrange("p (b e n) -> p b e n", b=4, e=2)
        PT = SOFT[:, 2 * HQ + 8 * TK:].rearrange("p (b n) -> p b n", b=2)
        STAT = sb("stat", [128, 4, 2, 2])
        SMAX, SSUM = STAT[:, :, 0, :], STAT[:, :, 1, :]
        IDENT, BM = C[:, C_ID:C_ID + 128], C[0:PQ, C_BM:C_BM + TK]
        ONES = C[:, C_ONE:C_ONE + 128]

        def psn(bank):
            return PS[:, bank, 0:N]

        const_dma, x_dma, xn_dma, out_dma = sem("const_dma"), sem("x_dma"), sem("xn_dma"), sem("out_dma")
        fold_dma, kvc_dma, seg_dma = sem("fold_dma"), sem("kvc_dma"), sem("seg_dma")
        ffn_dma = [sem("ffn_dma_first"), sem("ffn_dma_last")]
        ctx_dma = [sem(f"ctx_dma{i}") for i in range(4)]
        w_dma = [sem(f"w_dma{i}") for i in range(WR)]
        g_dma = [sem(f"g_dma{i}") for i in range(GR)]
        row_dma = [sem(f"row_dma{i}") for i in range(2)]
        mean_dma, masked_dma = sem("mean_dma"), sem("masked_dma")
        credit = {}

        def csem(name, slots, owner):
            s_ = sem(name)
            credit[name] = (s_, slots, owner)
            return s_

        names = (
            "idx_seg idx_mm idx_chain idx_ready fold_mm w0_hi w0_lo perm_ready alpha_abs alpha_ready clear masked_set "
            "ctx_hi ctx_lo_first ctx_lo tab_mm mean_ev mean_clear "
            "w_hi w_lo "
            "x_sum ln_sum ln_part ln_mean_mm ln_sub ln_sq ln_sq_part ln_sqsum ln_var_mm ln_ve ln_std ln_inv ln_n1 ln_n2 "
            "y_hi y_lo y_lo_pool "
            "qc_mm qc_f qc_hi qc_lo nope_hi nope_lo abs_mm rp_hi rp_lo swap_mm "
            "idx_copied kt_mm sm_max sm_exp sm_rec sm_norm "
            "cs_hi cs_lo att_hi ff_ab").split()
        S = {n_: sem(n_) for n_ in names}
        row_kv, row_rt, row_sum = csem("row_kv", 2, "act"), csem("row_rt", 2, "dve"), csem("row_sum", 2, "pool")
        mean_mm = csem("mean_mm", 1, "pe")
        w_used, w_sgn = csem("w_used", WR, "pe"), csem("w_sgn", WR, "dve")
        ln_rstd = csem("ln_rstd", 1, "dve")
        abs_even, abs_odd = csem("abs_even", 1, "act"), csem("abs_odd", 1, "dve")
        rope_t1, rope_t2, rope_ev = csem("rope_t1", 1, "dve"), csem("rope_t2", 1, "dve"), csem("rope_ev", 1, "pool")
        kt_ev, s_ev, sm_mask = csem("kt_ev", 1, "act"), csem("s_ev", 2, "act"), csem("sm_mask", 2, "dve")
        pt_ev, pv_ev = csem("pt_ev", 1, "act"), csem("pv_ev", 2, "dve")
        s_mm, st_mm, pt_mm, pv_mm = csem("s_mm", 2, "pe"), csem("st_mm", 2, "pe"), csem("pt_mm", 4, "pe"), csem("pv_mm", GR, "pe")
        att_lo, x_add = csem("att_lo", 2, "dve"), csem("x_add", 4, "dve")
        ff_t = csem("ff_t", 5, "dve")
        ff_add = csem("ff_add", 1, "dve")
        credit["out_dma"] = (out_dma, 32, "sp")

        def sums(n):
            return CS_FIRST[:, n] if n < 2 else CS[:, n % 2]

        def sums_part(n, part, late):
            t = slice(0, N) if n else slice(EARLY * QT_, N) if late else slice(0, EARLY * QT_)
            return sums(n)[:, part, :, t], QL[:, :, n, t]

        def sums_count(s, n, late=True):
            return s * (H + 1) + (n + 2 if late else 1)

        def value_unit(n):
            return U_WO + OUT_UNITS.index(("value", n))

        def wait_chunk(eng, s, c):
            if c < 3:
                eng.wait_ge(S["ctx_lo_first"], s * 3 + (c + 1))
            else:
                eng.wait_ge(S["ctx_lo"], s * (NC - 3) + (c - 2))

        pool_groups = (2, 4)
        dve_groups = (0, 1, 3)
        lows = NG + len(dve_groups)

        def used(s, u):
            return s * UNITS + (u + 1 + WR)

        def give_credits(eng, who):
            for s_, slots, owner in credit.values():
                if owner == who:
                    eng.sem_inc(s_, slots)

        block = ctx_.enter_context(nc.Block())

        def steps(eng, step, s, last):
            for i in range(GR):
                step(s, i, i)
            with eng.Fori(1, NT // GR) as k:
                for r in range(GR):
                    step(s, k * GR + r, r)
            for i in range(NT, last):
                step(s, i, i % GR)

        def has(i, lag):
            return not isinstance(i, int) or 0 <= i - lag < NT

        @block.sync
        def _(sp):
            give_credits(sp, "sp")
            sp.dma_start(KVC_T, kvct).then_inc(fold_dma, 16)
            sp.dma_start(KR_F, kr).then_inc(fold_dma, 16)
            sp.dma_start(KVC_F, kvc).then_inc(kvc_dma, 16)
            sp.dma_start(PRE, pre).then_inc(seg_dma, 16)
            sp.dma_start(SEG_I, seg).then_inc(seg_dma, 16)

            def ctx_load(n, slot):
                sp.dma_start(CRAW[:, slot, :], ctx[ds(n, 1), :, :].rearrange("a p n -> (a p) n")).then_inc(ctx_dma[slot], 16)

            ctx_load(0, 0)
            ctx_load(1, 1)
            for m in range(KD):
                if m == 4:
                    ctx_load(2, 2)
                    sp.wait_ge(S["fold_mm"], 1)
                    sp.wait_ge(S["w0_lo"], 1)
                sp.dma_start(FF_ROWS[m], ffn[:, D * m:D * (m + 1)]).then_inc(ffn_dma[m // 4], 16)

            def xn_load(n):
                for h in range(2):
                    sp.dma_start(XN[:, HALF_M * h:HALF_M * (h + 1), :].rearrange("p k n -> p (k n)"),
                                 x[ds(n, 1), :, HALF_M * N * h:HALF_M * N * (h + 1)].rearrange("a p n -> (a p) n")).then_inc(xn_dma, 16)

            xn_load(0)
            sp.dma_start(C[:, :], cst).then_inc(const_dma, 16)
            sp.dma_start(BIAS[:, :], bias).then_inc(const_dma, 16)
            ctx_load(3, 3)
            for c in range(4, PREFETCH):
                wait_chunk(sp, 0, c - 4)
                ctx_load(c, c - 4)

            def unit(s, u, slot, src, width):
                if isinstance(u, int) and u < WR:
                    sp.wait_ge(w_sgn, s * 16 + u + 1)
                elif isinstance(u, int) and u >= U_FF + WR:
                    sp.wait_ge(w_sgn, s * 16 + (u - U_FF) + 1)
                else:
                    sp.wait_ge(S["w_lo"], s * SPLIT_UNITS + u - WR + 1)
                sp.dma_start(WRAW[:, slot, 0:width], src).then_inc(w_dma[slot], 16)

            with sp.Fori(0, NS) as s:
                for c in range(PREFETCH, NC):
                    wait_chunk(sp, s, c - 4)
                    ctx_load(s * NC + c, c % 4)
                    if c == PREFETCH:
                        sp.wait_ge(S["alpha_ready"], 1)
                        sp.wait_ge(out_dma, (s + 1) * 32)
                    if c < PREFETCH + 2:
                        part = slice(HALF_M * (c - PREFETCH) * N, HALF_M * (c - PREFETCH + 1) * N)
                        sp.dma_start(X[:, :, :].rearrange("p k n -> p (k n)")[:, part],
                                     x[ds(s, 1), :, part].rearrange("a p n -> (a p) n")).then_inc(x_dma, 16)
                for u in range(U_PAIR):
                    unit(s, u, u % WR, dq[u], 3 * 128)
                with sp.Fori(0, PAIRS) as p:
                    u0 = p * 4 + U_PAIR
                    unit(s, u0, 0, uq[ds(p * 2, 1), :, :].rearrange("a p n -> (a p) n"), 3 * 128)
                    unit(s, u0 + 1, 1, uq[ds(p * 2 + 1, 1), :, :].rearrange("a p n -> (a p) n"), 3 * 128)
                    unit(s, u0 + 2, 2, qr[ds(p, 1), :, :].rearrange("a p n -> (a p) n"), 3 * 128)
                    unit(s, u0 + 3, 3, uk[ds(p, 1), :, :].rearrange("a p n -> (a p) n"), 512)
                for v, (kind, n) in enumerate(OUT_UNITS):
                    unit(s, U_WO + v, v % WR, *((uv[n], 256) if kind == "value" else (wo[n], 512)))
                for v in range(2 * KD):
                    unit(s, U_FF + v, v % WR, ff[v], 512)
                    if v == 3:
                        sp.wait_ge(S["cs_lo"], (s + 1) * (H + 1))
                        for c in range(4):
                            ctx_load(s * NC + (NC + c), c)
                sp.wait_ge(S["ln_sqsum"], s * 2 + 2)
                xn_load(s + 1)
                for c in range(4, PREFETCH):
                    wait_chunk(sp, s + 1, c - 4)
                    ctx_load(s * NC + (NC + c), c - 4)
                for h in range(2):
                    sp.wait_ge(ff_add, s * KD + (HALF_M * (h + 1) + 1))
                    part = slice(HALF_M * h * N, HALF_M * (h + 1) * N)
                    sp.dma_start(out[ds(s, 1), :, part].rearrange("a p n -> (a p) n"),
                                 X[:, :, :].rearrange("p k n -> p (k n)")[:, part]).then_inc(out_dma, 16)
            sp.wait_ge(out_dma, 32 + 32 * NS)
            sp.wait_ge(xn_dma, 32 * NS + 32)
            for c in range(4):
                sp.wait_ge(ctx_dma[c], 16 * NC // 4 * NS + (32 if c < PREFETCH - 4 else 16))

        @block.gpsimd
        def _(pool):
            give_credits(pool, "pool")
            pool.memset(ROW[:, :, TW - 1:TW], 0.0).then_inc(S["clear"], 1)
            masked = G[0:BPS, GR - 1, :]
            pool.memset(masked[:, 0:TW - 1], 0.0).then_inc(S["masked_set"], 1)
            pool.memset(masked[:, TW - 1:TW], -NEG).then_inc(S["masked_set"], 1)
            pool.wait_ge(S["masked_set"], 2)
            pool.dma_start(table[MASKED_ROW:BPS * ROWS:ROWS, :], masked).then_inc(masked_dma, 16)

            def low(s, u, slot, width):
                pool.wait_ge(S["w_hi"], s * SPLIT_UNITS + u + 1)
                pool.tensor_tensor(WLO[:, slot, 0:width], WRAW[:, slot, 0:width], WHI[:, slot, 0:width].bitcast(f32),
                                   ALU.subtract).then_inc(S["w_lo"], 1)

            def gather(r):
                pool.indirect_dma_start(out=G[0:TK, r, :], out_offset=None, in_=table,
                                        in_offset=bass.IndirectOffsetOnAxis(ap=IDXR[0:TK, r:r + 1], axis=0)).then_inc(g_dma[r], 16)

            def normalise(r, e):
                return pool.tensor_tensor(SM[0:PQ, r % 4, e, :], SM[0:PQ, r % 4, e, :],
                                          SSUM[0:PQ, r % 4, e:e + 1].to_broadcast([PQ, TK]), ALU.mult)

            def sum_x(s):
                pool.wait_ge(xn_dma, s * 32 + 32)
                pool.tensor_tensor(XSUM, XN[:, 0:2, :], XN[:, 2:4, :], ALU.add).then_inc(S["x_sum"], 1)
                for i in range(2):
                    pool.wait_ge(S["x_sum"], s * 4 + (i + 1))
                    pool.tensor_tensor(XSUM, XSUM, XN[:, 4 + 2 * i:6 + 2 * i, :], ALU.add).then_inc(S["x_sum"], 1)
                pool.wait_ge(S["x_sum"], s * 4 + 3)
                pool.tensor_tensor(XSUM[:, 0, :], XSUM[:, 0, :], XSUM[:, 1, :], ALU.add).then_inc(S["x_sum"], 1)

            def step(s, k, r):
                tile = s * NT + k * GR + r
                pool.wait_ge(pv_mm, tile + 1)
                pool.wait_ge(S["sm_rec"], tile - AHEAD + 1)
                normalise(r - AHEAD, 0)
                pool.tensor_copy(IDXR[0:TK, r:r + 1], IDX[0:TK, ds(tile, 1)]).then_inc(S["idx_copied"], 1)
                pool.wait_ge(S["idx_copied"], s * (NT - GR + 1) + k * GR + (r - GR + 2))
                normalise(r - AHEAD, 1).then_inc(S["sm_norm"], 1)
                gather(r)

            def finish(s, i):
                pool.wait_ge(S["sm_rec"], s * NT + i + 1)
                normalise(i, 0)
                normalise(i, 1).then_inc(S["sm_norm"], 1)

            pool.wait_ge(S["idx_ready"], 1)
            pool.wait_ge(S["clear"], 1)
            pool.wait_ge(masked_dma, 16)
            with pool.Fori(0, NS) as s:
                for c in range(NC):
                    b, t, e = c // CPB, c % CPB, c % 2
                    n = s * NC + c
                    pool.wait_ge(row_rt, n + 3)
                    for h, op in enumerate((ALU.subtract, ALU.add)):
                        x_cos, x_sin = (RT[0:CK, e, w, HALF * v:HALF * (v + 1)][:, None, :].to_broadcast([CK, 2, HALF])
                                        for w, v in ((0, h), (1, 1 - h)))
                        both = ROW[0:CK, e, 0:2 * R].rearrange("p (a n) -> p a n", a=2)[:, :, HALF * h:HALF * (h + 1)]
                        pool.tensor_tensor(both, x_cos, x_sin, op)
                    pool.wait_ge(row_kv, n + 3)
                    if c == 0:
                        pool.wait_ge(mean_mm, s + 1)
                        pool.wait_ge(pv_mm, s * NT + GR)
                    acc, kv = G[0:CK, b, 0:KVC], ROW[0:CK, e, 2 * R:2 * R + KVC]
                    if t == 0:
                        pool.tensor_tensor(acc, kv, ROW[0:CK, e, TW - 1:TW].to_broadcast([CK, KVC]), ALU.add).then_inc(row_sum, 1)
                    else:
                        pool.wait_ge(row_sum, n + 2)
                        pool.tensor_tensor(acc, acc, kv, ALU.add).then_inc(row_sum, 1)
                    if c >= NC - 4:
                        low(s, c - (NC - 4), c - (NC - 4), 384)
                pool.memset(G[0:1, 2:4, 0:2 * R], 0.0).then_inc(S["mean_clear"], 1)
                pool.memset(G[0:1, 2:4, TW - 1:TW], 0.0).then_inc(S["mean_clear"], 1)
                for u in range(4, 8):
                    low(s, u, u % WR, 384)
                low(s, 8, 0, 384)
                pool.wait_ge(S["mean_clear"], s * 2 + 2)
                pool.wait_ge(S["mean_ev"], s + 1)
                low(s, 9, 1, 384)
                mean_rows = table.rearrange("(b r) w -> r b w", r=ROWS)[MEAN_ROW:MEAN_ROW + 1, :, :]
                pool.dma_start(mean_rows, G[0:1, 2:4, :]).then_inc(mean_dma, 16)
                pool.tensor_copy(IDXR[0:TK, :], IDX[0:TK, ds(s * NT, GR)]).then_inc(S["idx_copied"], 1)
                low(s, 10, 2, 384)
                for p in range(PAIRS):
                    for v in range(3, 7):
                        u = U_PAIR + 4 * p + v
                        if p == 0 and v == 3:
                            for e in range(2):
                                pool.wait_ge(row_dma[e], (s + 1) * (16 * NC // 2))
                            pool.wait_ge(mean_dma, s * 16 + 16)
                            pool.wait_ge(S["idx_copied"], s * (NT - GR + 1) + 1)
                        low(s, u, v % WR, 512 if v == 3 else 384 if u < U_WO else 256)
                        if v == 4:
                            gather(p)
                    pool.wait_ge(rope_t1, s * PAIRS + p + 2)
                    pool.wait_ge(rope_t2, s * PAIRS + p + 2)
                    pool.tensor_tensor(QR[:, p, :], TMP[:, 0, :], TMP[:, 1, :], ALU.add).then_inc(rope_ev, 1)
                low(s, U_WO + 3, 3, 256)
                for i in range(GR - AHEAD):
                    finish(s, i)
                with pool.Fori(1, NT // GR) as k:
                    for r in range(GR):
                        step(s, k, r)
                for i in range(NT - AHEAD, NT):
                    finish(s, i)
                for v, (kind, n) in enumerate(OUT_UNITS):
                    if v >= WR:
                        low(s, U_WO + v, v % WR, 256 if kind == "value" else 512)
                for i in pool_groups:
                    a, b = NORM[i]
                    pool.wait_ge(S["y_hi"], s * (2 * NG) + (NG + i + 1))
                    pool.tensor_tensor(Y[:, 1, a:b, :], CEN[:, a:b, :], Y[:, 0, a:b, :].bitcast(f32),
                                       ALU.subtract).then_inc(S["y_lo_pool"], 1)
                for c in range(3):
                    pool.wait_ge(S["ctx_hi"], s * NC + (NC + c + 1))
                    pool.tensor_tensor(CSPL[:, c, 1, :], CRAW[:, c, :], CSPL[:, c, 0, :].bitcast(f32),
                                       ALU.subtract).then_inc(S["ctx_lo_first"], 1)
                sum_x(s + 1)

        @block.scalar
        def _(act):
            give_credits(act, "act")

            def high(s, u, slot, width):
                act.wait_ge(w_dma[slot], s * (UNITS // WR * 16) + (u // WR + 1) * 16)
                act.wait_ge(w_used, s * UNITS + u + 1)
                act.activation(WHI[:, slot, 0:width], WRAW[:, slot, 0:width], ACT.Copy).then_inc(S["w_hi"], 1)

            def high_in_pair(s, p, v, width):
                act.wait_ge(w_dma[v % WR], s * (UNITS // WR * 16) + p * 16 + (U_PAIR // WR + v // WR + 1) * 16)
                act.wait_ge(w_used, s * UNITS + p * 4 + (U_PAIR + v + 1))
                act.activation(WHI[:, v % WR, 0:width], WRAW[:, v % WR, 0:width], ACT.Copy).then_inc(S["w_hi"], 1)

            def norm_high(s, l, i):
                a, b = NORM[i]
                act.wait_ge(S["ln_sub"], s * (2 * NG) + NG * l + i + 1)
                act.activation(Y[:, 0, a:b, :], CEN[:, a:b, :], ACT.Copy).then_inc(S["y_hi"], 1)

            def norm_square(s, l):
                act.wait_ge(S["ln_sub"], s * (2 * NG) + NG * l + NG)
                act.activation(SQ[:, :, :], CEN[:, :, :], ACT.Square).then_inc(S["ln_sq"], 1)

            def norm_std(s, l):
                act.wait_ge(S["ln_var_mm"], s * 2 + l + 1)
                act.activation(TMP[:, 0, :], psn(3), ACT.Sqrt, bias=eps[:, :]).then_inc(S["ln_std"], 1)
                act.activation(VE, psn(3), ACT.Identity, bias=eps[:, :]).then_inc(S["ln_ve"], 1)

            def ctx_high(s, c):
                act.wait_ge(ctx_dma[c % 4], s * (16 * NC // 4) + (c // 4 + 1) * 16)
                if 3 <= c < NC:
                    act.wait_ge(S["tab_mm"], s * NC + c - 2)
                act.activation(CSPL[:, c % 3, 0, :], CRAW[:, c % 4, :], ACT.Copy).then_inc(S["ctx_hi"], 1)

            def store_rows(s, c):
                b, t = c // CPB, c % CPB
                act.wait_ge(row_sum, s * NC + c + 3)
                act.dma_start(table[b * ROWS + t * CK:b * ROWS + (t + 1) * CK, :], ROW[0:CK, c % 2, :]).then_inc(row_dma[c % 2], 16)

            act.wait_ge(kvc_dma, 16)
            act.activation(KVW[:, 0, :, 0:KVC], KVC_F.rearrange("p (k n) -> p k n", k=KD), ACT.Copy).then_inc(S["w0_hi"], 1)
            act.wait_ge(S["fold_mm"], 1)
            act.activation(KVW[:, 0, :, KVC:KVR], PS[:, 0, :].rearrange("p (k n) -> p k n", k=KD), ACT.Copy).then_inc(S["w0_hi"], 1)
            ctx_high(0, 0)
            ctx_high(0, 1)
            act.wait_ge(seg_dma, 16 * 2)
            act.activation(PERM[:, :], PRE[:, P_PERM:P_PERM + 128], ACT.Copy).then_inc(S["perm_ready"], 1)
            act.wait_ge(ffn_dma[0], 16 * 4)
            for m in range(KD):
                if m == 4:
                    ctx_high(0, 2)
                    act.wait_ge(ffn_dma[1], 16 * 4)
                if m:
                    act.wait_ge(S["alpha_abs"], m)
                act.activation(FF_ROWS[m], FF_ROWS[m], ACT.Abs, accum_out=ALPHA[:, m:m + 1]).then_inc(S["alpha_abs"], 1)
            act.wait_ge(S["alpha_abs"], KD)
            act.wait_ge(const_dma, 16 * 2)

            with act.Fori(0, NS) as s:
                for c in range(NC):
                    n, e = s * NC + c, c % 2
                    if c:
                        store_rows(s, c - 1)
                    act.wait_ge(S["tab_mm"], n + 1)
                    if c >= 2:
                        act.wait_ge(row_dma[e], s * (16 * NC // 2) + (c // 2) * 16)
                    act.wait_ge(row_sum, n + 1)
                    act.activation(ROW[0:CK, e, 2 * R:2 * R + KVC], PS[0:CK, 6 + e, 0:KVC], ACT.Copy).then_inc(row_kv, 1)
                    if c + 3 < NC:
                        ctx_high(s, c + 3)
                    if c == 3:
                        act.wait_ge(w_used, used(s, -1))
                        for i in range(3):
                            norm_high(s, 0, i)
                    if c == 4:
                        for i in range(3, NG):
                            norm_high(s, 0, i)
                    if c == 5:
                        norm_square(s, 0)
                    if c == 11:
                        norm_std(s, 0)
                    if c >= NC - 4:
                        high(s, c - (NC - 4), c - (NC - 4), 384)
                store_rows(s, NC - 1)
                high(s, 4, 0, 384)
                high(s, 5, 1, 384)
                high(s, 6, 2, 384)
                high(s, 7, 3, 384)
                for m in range(KC):
                    act.wait_ge(S["qc_f"], s * KC + m + 1)
                    act.activation(QCS[:, 0, m, :], TMP[:, m % 2, :], ACT.Copy).then_inc(S["qc_hi"], 1)
                    high(s, 8 + m, m % WR, 384)
                    if m == 0:
                        act.wait_ge(mean_mm, s + 2)
                        act.activation(G[0:1, 2:4, 2 * R:2 * R + KVC], PS[0:1, 7, :].rearrange("p (b n) -> p b n", b=BPS),
                                       ACT.Copy).then_inc(S["mean_ev"], 1)

                def pair(p, next_width):
                    high_in_pair(s, p, 3, 512)
                    for h in range(2):
                        act.wait_ge(w_used, s * UNITS + p * 4 + (U_PAIR + h + 1 + WR))
                        act.activation(NOPE[:, h, 0, :], psn(h), ACT.Copy).then_inc(S["nope_hi"], 1)
                        high_in_pair(s, p, 4 + h, next_width)
                    act.wait_ge(w_used, s * UNITS + p * 4 + (U_PAIR + 2 + 1 + WR))
                    act.activation(RSP[:, 0, :], psn(4), ACT.Copy).then_inc(S["rp_hi"], 1)
                    high_in_pair(s, p, 6, next_width)
                    act.wait_ge(S["abs_mm"], s * H + p * 2 + 1)
                    act.activation(QL[:, :, ds(p, 1), :].rearrange("p d a n -> p d (a n)"), PS[:, 2:4, 0:N], ACT.Copy).then_inc(abs_even, 1)

                with act.Fori(0, PAIRS - 1) as p:
                    pair(p, 384)
                pair(PAIRS - 1, 256)
                high(s, U_WO + 3, 3, 256)

                def step(s, i, r):
                    tile = s * NT + i
                    if has(i, 0):
                        act.wait_ge(S["kt_mm"], tile + 1)
                        act.wait_ge(s_mm, tile + 1)
                        act.activation(KT[:, r % 2, 2 * TK:4 * TK], PS[:, 0, TK:3 * TK], ACT.Copy)
                        for e in range(2):
                            half = slice(R * e, R * (e + 1))
                            ins = act.activation(KT[half, r % 2, TK * e:TK * (e + 1)], PS[half, 0, 0:TK], ACT.Copy)
                        ins.then_inc(kt_ev, 1)
                    if has(i, 1):
                        n, q = tile - 1, (r - 1) % GR
                        act.wait_ge(s_mm, n + 3)
                        act.wait_ge(st_mm, n + 1)
                        act.activation(SSB[0:TK, q % 2, :], PS[0:TK, 1 + q % 2, 0:HQ], ACT.Identity,
                                       bias=G[0:TK, q, TW - 1:TW], scale=-SCALE).then_inc(s_ev, 1)
                    if has(i, PT_LAG):
                        n, q = tile - PT_LAG, (r - PT_LAG) % GR
                        act.wait_ge(pt_mm, n + 5)
                        act.wait_ge(pv_mm, n + GR - 1)
                        act.activation(PT[0:TK, q % 2, :], PS[0:TK, 5, 0:HQ], ACT.Copy).then_inc(pt_ev, 1)
                    if has(i, 2):
                        n, q = tile - 2, (r - 2) % GR
                        act.wait_ge(S["sm_max"], n + 1)
                        for e in range(2):
                            ins = act.activation(SM[0:PQ, q % 4, e, :], SM[0:PQ, q % 4, e, :], ACT.Exp, scale=-1.0,
                                                 bias=SMAX[0:PQ, q % 4, e:e + 1], accum_out=SSUM[0:PQ, q % 4, e:e + 1])
                        ins.then_inc(S["sm_exp"], 1)

                def sum_high(n, late=True):
                    if n >= 4:
                        act.wait_ge(w_used, used(s, value_unit(n - 2)))
                    high_, whole = sums_part(n, 0, late)
                    act.activation(high_, whole, ACT.Copy).then_inc(S["cs_hi"], 1)

                def step_and_sums(s, i, r):
                    step(s, i, r)
                    if isinstance(i, int) and i == NT:
                        act.wait_ge(pv_ev, s * NT + EARLY + 2)
                        sum_high(0, late=False)

                steps(act, step_and_sums, s, NT + PT_LAG)

                act.wait_ge(pv_ev, s * NT + NT + 2)
                for n in range(3):
                    sum_high(n)
                for v, (kind, n) in enumerate(OUT_UNITS):
                    if kind == "value":
                        g, j = n // G4, n % G4
                        if g >= 2:
                            act.wait_ge(w_used, used(s, U_WO + OUT_UNITS.index(("output", KD * (g - 1) - 1))))
                        act.wait_ge(w_used, used(s, U_WO + v))
                        act.activation(ATT[:, g % 2, 0, j, :], psn(n % 2), ACT.Copy).then_inc(S["att_hi"], 1)
                        if n == 0:
                            sum_high(3)
                        elif 2 <= n < H - 2:
                            sum_high(n + 2)
                    w = v + WR
                    if w < len(OUT_UNITS):
                        high(s, U_WO + w, w % WR, 256 if OUT_UNITS[w][0] == "value" else 512)
                act.wait_ge(w_used, used(s, U_FF - 1))
                for i in range(NG):
                    norm_high(s, 1, i)
                norm_square(s, 1)
                for c in range(3):
                    act.wait_ge(ctx_dma[c], s * (16 * NC // 4) + (16 * NC // 4 + 16))
                    act.activation(CSPL[:, c, 0, :], CRAW[:, c, :], ACT.Copy).then_inc(S["ctx_hi"], 1)
                norm_std(s, 1)
                for m in range(KD):
                    act.wait_ge(ff_t, s * KD + m + 6)
                    act.activation(CEN[:, m, :], CEN[:, m, :], ACT.Identity, bias=BIAS[:, m:m + 1],
                                   scale=ALPHA2[:, m:m + 1]).then_inc(S["ff_ab"], 1)

        @block.vector
        def _(dve):
            give_credits(dve, "dve")
            dve.memset(KT[R:2 * R, :, 0:TK], 0.0)
            dve.memset(KT[0:R, :, TK:2 * TK], 0.0)
            dve.memset(eps[:, :], EPS).then_inc(S["idx_chain"], 1)
            dve.wait_ge(seg_dma, 16 * 2)
            segi, segf = SEG_I, SEG_F
            k_, a_, b_, m_ = IDX_TMP
            link = [1]

            def chain(ins):
                link[0] += 1
                ins.then_inc(S["idx_chain"], 1)
                dve.wait_ge(S["idx_chain"], link[0])

            chain(dve.tensor_copy(segf, segi))
            dve.tensor_scalar(segf, segf, -1.0, float(LK + LOOKBACK), ALU.max, ALU.min).then_inc(S["idx_seg"], 1)
            dve.wait_ge(S["w0_hi"], 1)
            chain(dve.tensor_tensor(KVW[:, 1, :, 0:KVC], KVC_F.rearrange("p (k n) -> p k n", k=KD),
                                    KVW[:, 0, :, 0:KVC].bitcast(f32), ALU.subtract))
            dve.wait_ge(S["w0_hi"], 2)
            dve.tensor_tensor(KVW[:, 1, :, KVC:KVR], PS[:, 0, :].rearrange("p (k n) -> p k n", k=KD),
                              KVW[:, 0, :, KVC:KVR].bitcast(f32), ALU.subtract).then_inc(S["w0_lo"], 1)
            def ctx_low(n, c):
                dve.wait_ge(S["ctx_hi"], n + 1)
                dve.tensor_tensor(CSPL[:, c % 3, 1, :], CRAW[:, c % 4, :], CSPL[:, c % 3, 0, :].bitcast(f32),
                                  ALU.subtract).then_inc(S["ctx_lo_first" if c < 3 else "ctx_lo"], 1)

            for c in range(3):
                ctx_low(c, c)
            dve.wait_ge(S["idx_mm"], 1)
            chain(dve.tensor_scalar(a_, PS[0:TK, 1, 0:128], 0.0, None, ALU.is_ge))
            chain(dve.tensor_scalar(b_, PS[0:TK, 1, 0:128], float(LK - 1 + LOOKBACK), None, ALU.is_le))
            chain(dve.tensor_tensor(a_, a_, b_, ALU.mult))
            chain(dve.tensor_scalar(k_, PS[0:TK, 1, 0:128], PRE[0:TK, P_J:P_J + 1], None, ALU.subtract))
            chain(dve.tensor_scalar(b_, k_, 0.0, None, ALU.is_ge))
            chain(dve.tensor_scalar(m_, k_, float(LK - 1), None, ALU.is_le))
            chain(dve.tensor_tensor(b_, b_, m_, ALU.mult))
            chain(dve.scalar_tensor_tensor(out=b_, in0=k_, scalar=float(MASKED_ROW), in1=b_, op0=ALU.subtract, op1=ALU.mult))
            chain(dve.scalar_tensor_tensor(out=b_, in0=b_, scalar=float(MASKED_ROW - MEAN_ROW), in1=a_, op0=ALU.add, op1=ALU.mult))
            chain(dve.scalar_tensor_tensor(out=b_, in0=b_, scalar=float(MEAN_ROW), in1=PRE[0:TK, P_BASE:P_BASE + 128],
                                           op0=ALU.add, op1=ALU.add))
            dve.tensor_copy(IDX[0:TK, :], b_).then_inc(S["idx_ready"], 1)
            dve.wait_ge(const_dma, 16 * 2)
            dve.wait_ge(S["alpha_abs"], KD)
            dve.tensor_scalar(ALPHA2[:, :], ALPHA[:, :], 2.0 / D, None, ALU.mult).then_inc(S["alpha_ready"], 1)

            dve.wait_ge(xn_dma, 32)
            dve.tensor_reduce(XSUM[:, 0, :], XN.rearrange("p k n -> p n k"), AX.X, ALU.add).then_inc(S["x_sum"], 4)

            def norm_center(s, l, i):
                a, b = NORM[i]
                if i == 0:
                    dve.wait_ge(S["ln_mean_mm"], s * 2 + l + 1)
                dve.tensor_tensor(CEN[:, a:b, :], (X if l else XN)[:, a:b, :], psn(2)[:, None, :].to_broadcast([128, b - a, N]),
                                  ALU.subtract).then_inc(S["ln_sub"], 1)

            def norm_low(s, l, i):
                a, b = NORM[i]
                dve.wait_ge(S["y_hi"], s * (2 * NG) + NG * l + i + 1)
                dve.tensor_tensor(Y[:, 1, a:b, :], CEN[:, a:b, :], Y[:, 0, a:b, :].bitcast(f32),
                                  ALU.subtract).then_inc(S["y_lo"], 1)

            def norm_sqsum(s):
                dve.wait_ge(S["ln_sq"], s * 2 + 2)
                dve.tensor_reduce(TMP[:, 1, :], SQ[:, :, :].rearrange("p k n -> p n k"), AX.X, ALU.add).then_inc(S["ln_sqsum"], 1)

            def norm_rstd(s, l, between=None):
                n = s * 2 + l
                dve.wait_ge(S["ln_std"], n + 1)
                dve.reciprocal(RSTD, TMP[:, 0, :]).then_inc(S["ln_inv"], 1)
                if between:
                    between(0)
                dve.wait_ge(S["ln_inv"], n + 1)
                dve.tensor_tensor(TMP[:, 1, :], RSTD, RSTD, ALU.mult).then_inc(S["ln_n1"], 1)
                if between:
                    between(1)
                dve.wait_ge(S["ln_n1"], n + 1)
                dve.wait_ge(S["ln_ve"], n + 1)
                dve.scalar_tensor_tensor(out=TMP[:, 1, :], in0=TMP[:, 1, :], scalar=-0.5, in1=VE, op0=ALU.mult,
                                         op1=ALU.mult).then_inc(S["ln_n2"], 1)
                dve.wait_ge(S["ln_n2"], n + 1)
                dve.scalar_tensor_tensor(out=RSTD, in0=TMP[:, 1, :], scalar=1.5, in1=RSTD, op0=ALU.add,
                                         op1=ALU.mult).then_inc(ln_rstd, 1)

            with dve.Fori(0, NS) as s:
                for c in range(NC):
                    n, e, t = s * NC + c, c % 2, c % CPB
                    dve.wait_ge(row_kv, n + 3)
                    dve.wait_ge(row_sum, n + 1)
                    for w in range(2):
                        cs = C[0:CK, C_KCS + R * t + HALF * w:C_KCS + R * t + HALF * (w + 1)]
                        ins = dve.tensor_tensor(RT[0:CK, e, w, :].rearrange("p (a n) -> p a n", a=2),
                                                PS[0:CK, 6 + e, KVC:KVR].rearrange("p (a n) -> p a n", a=2),
                                                cs[:, None, :].to_broadcast([CK, 2, HALF]), ALU.mult)
                    ins.then_inc(row_rt, 1)
                    if c + 3 < NC:
                        ctx_low(n + 3, c + 3)
                    if c == 1:
                        dve.wait_ge(ff_add, s * KD + 1)
                    for i in {1: (0, 1, 2), 2: (3, 4)}.get(c, ()):
                        norm_center(s, 0, i)
                    for i in {4: (0, 1, 2), 5: (3, 4)}.get(c, ()):
                        norm_low(s, 0, i)
                    if c in (7, 8):
                        h = c - 7
                        dve.wait_ge(S["ln_sq"], s * 2 + 1)
                        dve.tensor_reduce(TMP[:, h, :], SQ[:, HALF_M * h:HALF_M * (h + 1), :].rearrange("p k n -> p n k"),
                                          AX.X, ALU.add).then_inc(S["ln_sq_part"], 1)
                    if c == 9:
                        dve.wait_ge(S["ln_sq_part"], s * 2 + 2)
                        dve.tensor_tensor(TMP[:, 1, :], TMP[:, 1, :], TMP[:, 0, :], ALU.add).then_inc(S["ln_sqsum"], 1)
                    if c == 11:
                        norm_rstd(s, 0)
                dve.wait_ge(ln_rstd, s * 2 + 2)
                for m in range(KC):
                    n = s * KC + m
                    if m < KC - 1:
                        dve.wait_ge(S["qc_mm"], s * (KC - 1) + m + 1)
                    else:
                        dve.wait_ge(w_used, used(s, U_PAIR - 1))
                    dve.tensor_tensor(TMP[:, m % 2, :], psn(4 + m), RSTD, ALU.mult).then_inc(S["qc_f"], 1)
                    dve.wait_ge(S["qc_hi"], n + 1)
                    dve.tensor_tensor(QCS[:, 1, m, :], TMP[:, m % 2, :], QCS[:, 0, m, :].bitcast(f32),
                                      ALU.subtract).then_inc(S["qc_lo"], 1)

                with dve.Fori(0, PAIRS) as p:
                    for h in range(2):
                        n = s * H + p * 2 + h
                        dve.wait_ge(S["nope_hi"], n + 1)
                        dve.tensor_tensor(NOPE[:, h, 1, :], psn(h), NOPE[:, h, 0, :].bitcast(f32),
                                          ALU.subtract).then_inc(S["nope_lo"], 1)
                    n = s * PAIRS + p
                    dve.wait_ge(S["rp_hi"], n + 1)
                    dve.tensor_tensor(RSP[:, 1, :], psn(4), RSP[:, 0, :].bitcast(f32), ALU.subtract).then_inc(S["rp_lo"], 1)
                    dve.wait_ge(rope_ev, n + 1)
                    rep = [128, BPS, LQ]
                    dve.tensor_tensor(TMP[:, 0, :].rearrange("p (b n) -> p b n", b=BPS), psn(4).rearrange("p (b n) -> p b n", b=BPS),
                                      C[:, C_QC:C_QC + LQ][:, None, :].to_broadcast(rep), ALU.mult).then_inc(rope_t1, 1)
                    dve.wait_ge(S["swap_mm"], n + 1)
                    dve.tensor_tensor(TMP[:, 1, :].rearrange("p (b n) -> p b n", b=BPS), psn(7).rearrange("p (b n) -> p b n", b=BPS),
                                      C[:, C_QS:C_QS + LQ][:, None, :].to_broadcast(rep), ALU.mult).then_inc(rope_t2, 1)
                    dve.wait_ge(S["abs_mm"], s * H + p * 2 + 2)
                    dve.tensor_scalar(QL[:, :, ds(p + PAIRS, 1), :].rearrange("p d a n -> p d (a n)"), PS[:, 5:7, 0:N], 1.0, None, ALU.mult).then_inc(abs_odd, 1)

                def step(s, i, r):
                    n, q = s * NT + i, r
                    if has(i, 0):
                        sm = SM[0:PQ, q % 4, :, :]
                        dve.wait_ge(st_mm, n + 3)
                        dve.wait_ge(pt_mm, n + 1)
                        dve.tensor_tensor(sm, PS[0:PQ, 3 + q % 2, 0:2 * TK].rearrange("p (e n) -> p e n", e=2),
                                          BM[:, None, :].to_broadcast([PQ, 2, TK]), ALU.add).then_inc(sm_mask, 1)
                        dve.wait_ge(sm_mask, n + 3)
                        dve.tensor_reduce(SMAX[0:PQ, q % 4, :], sm, AX.X, ALU.min).then_inc(S["sm_max"], 1)
                    if has(i, 3):
                        m = n - 3
                        dve.wait_ge(pv_mm, m + GR + 1)
                        dve.tensor_scalar(QL_ROWS[:, :, ds(i * QT_ - 3 * QT_, QT_)],
                                          PS[:, 6 + (q - 3) % 2, 0:KV * HQ].rearrange("p (e n) -> p e n", n=QT_),
                                          1.0, None, ALU.mult).then_inc(pv_ev, 1)
                    if has(i, 0):
                        dve.wait_ge(S["sm_exp"], n + 1)
                        dve.reciprocal(SSUM[0:PQ, q % 4, :], SSUM[0:PQ, q % 4, :]).then_inc(S["sm_rec"], 1)

                def sum_low(n, late=True):
                    dve.wait_ge(S["cs_hi"], sums_count(s, n, late))
                    high_, whole = sums_part(n, 0, late)
                    low_, _ = sums_part(n, 1, late)
                    dve.tensor_tensor(low_, whole, high_.bitcast(f32), ALU.subtract).then_inc(S["cs_lo"], 1)

                def step_and_sums(s, i, r):
                    step(s, i, r)
                    if isinstance(i, int) and i == NT:
                        dve.wait_ge(pv_ev, s * NT + EARLY + 2)
                        sum_low(0, late=False)

                steps(dve, step_and_sums, s, NT + 3)

                dve.wait_ge(pv_ev, s * NT + NT + 2)
                for n in range(3):
                    sum_low(n)
                for v, (kind, i) in enumerate(OUT_UNITS):
                    if kind == "value":
                        g, j = i // G4, i % G4
                        dve.wait_ge(S["att_hi"], s * H + i + 1)
                        dve.tensor_tensor(ATT[:, g % 2, 1, j, :], psn(i % 2), ATT[:, g % 2, 0, j, :].bitcast(f32),
                                          ALU.subtract).then_inc(att_lo, 1)
                        if i == 0:
                            sum_low(3)
                        elif 2 <= i < H - 2:
                            sum_low(i + 2)
                    else:
                        g, m = i // KD, i % KD
                        n = s * (KD * H // G4) + i
                        last_group = g == H // G4 - 1
                        if last_group and m == KD - 1:
                            dve.wait_ge(S["ln_part"], s * (KD - 1) + KD - 2)
                            dve.tensor_tensor(TMP[:, 0, :], TMP[:, 0, :], X[:, m, :], ALU.add).then_inc(S["ln_part"], 1)
                        if i == 0:
                            dve.wait_ge(x_dma, s * 32 + 32)
                        dve.wait_ge(w_used, used(s, U_WO + v))
                        if g:
                            dve.wait_ge(x_add, n - KD + 5)
                        if last_group and m == KD - 1:
                            dve.wait_ge(S["ln_part"], s * (KD - 1) + KD - 1)
                            dve.tensor_tensor(TMP[:, 0, :], TMP[:, 0, :], psn(4 + m % 4), ALU.add).then_inc(S["ln_sum"], 1)
                        dve.tensor_tensor(X[:, m, :], X[:, m, :], psn(4 + m % 4), ALU.add).then_inc(x_add, 1)
                        if last_group and 0 < m < KD - 1:
                            dve.wait_ge(x_add, n + 5)
                            if m > 1:
                                dve.wait_ge(S["ln_part"], s * (KD - 1) + m - 1)
                            dve.tensor_tensor(TMP[:, 0, :], X[:, 0, :] if m == 1 else TMP[:, 0, :], X[:, m, :],
                                              ALU.add).then_inc(S["ln_part"], 1)

                dve.wait_ge(x_add, (s + 1) * (KD * H // G4) + 4)

                def signs(v):
                    dve.wait_ge(w_dma[v % WR], s * (UNITS // WR * 16) + ((U_FF + v) // WR + 1) * 16)
                    dve.wait_ge(w_used, s * UNITS + U_FF + v + 1)
                    dve.tensor_scalar(WHI[:, v % WR, :], WRAW[:, v % WR, :], 0.0, 0.5, ALU.is_ge, ALU.subtract).then_inc(w_sgn, 1)

                signs(0)
                norm_center(s, 1, 0)
                norm_center(s, 1, 1)
                norm_low(s, 1, 0)
                norm_center(s, 1, 2)
                norm_low(s, 1, 1)
                signs(1)
                norm_center(s, 1, 3)
                signs(2)
                norm_center(s, 1, 4)
                norm_low(s, 1, 3)
                for v in range(3, 9):
                    signs(v)
                norm_sqsum(s)
                for v in range(9, 14):
                    signs(v)
                norm_rstd(s, 1, lambda i: signs(14 + i))
                dve.wait_ge(ln_rstd, s * 2 + 3)

                def scale(m):
                    h = m // HALF_M
                    dve.wait_ge(w_used, used(s, U_FF + KD * (h + 1) - 1))
                    dve.tensor_tensor(CEN[:, m, :], psn(4 * (1 - h) + m % 4), RSTD, ALU.mult).then_inc(ff_t, 1)

                def add(m):
                    dve.wait_ge(S["ff_ab"], s * KD + m + 1)
                    dve.tensor_tensor(X[:, m, :], X[:, m, :], CEN[:, m, :], ALU.add).then_inc(ff_add, 1)

                for m in range(HALF_M):
                    scale(m)
                add(0)
                add(1)
                for m in range(HALF_M, KD):
                    scale(m)
                for m in range(2, KD):
                    add(m)

        @block.tensor
        def _(pe):
            give_credits(pe, "pe")
            pe.wait_ge(fold_dma, 16 * 2)
            for m in range(KD):
                for k in range(KV):
                    last = pe.matmul(PS[:, 0, R * m:R * (m + 1)], KVC_T[:, D * k + 128 * m:D * k + 128 * (m + 1)],
                                     KR_F[:, R * k:R * (k + 1)], start=(k == 0), stop=(k == KV - 1))
            last.then_inc(S["fold_mm"], 1)
            pe.wait_ge(S["idx_seg"], 1)
            pe.matmul(PS[0:TK, 1, 0:128], PRE[0:QT_, P_E14:P_E14 + TK], SEG_F,
                      start=True, stop=True).then_inc(S["idx_mm"], 1)
            pe.wait_ge(S["w0_lo"], 1)

            def three(out_, whi, wlo, xhi, xlo, first, final):
                pe.matmul(out_, whi, xhi, start=first, stop=False)
                pe.matmul(out_, whi, xlo, start=False, stop=False)
                return pe.matmul(out_, wlo, xhi, start=False, stop=final)

            def w_tile(slot, t):
                return WHI[:, slot, 128 * t:128 * (t + 1)], WLO[:, slot, 128 * t:128 * (t + 1)]

            with pe.Fori(0, NS) as s:
                pe.wait_ge(ff_t, s * KD + 1)
                for c in range(NC):
                    n, e = s * NC + c, c % 2
                    wait_chunk(pe, s, c)
                    pe.wait_ge(row_rt, n + 1)
                    pe.wait_ge(row_kv, n + 1)
                    for k in range(KD):
                        hi, lo = (CSPL[:, c % 3, z, CK * k:CK * (k + 1)] for z in range(2))
                        last = three(PS[0:CK, 6 + e, 0:KVR], hi, lo, KVW[:, 0, k, :], KVW[:, 1, k, :], k == 0, k == KD - 1)
                    last.then_inc(S["tab_mm"], 1)
                    if c == 10:
                        pe.wait_ge(S["ln_sqsum"], s * 2 + 1)
                        pe.matmul(psn(3), ONES, TMP[:, 1, :], start=True, stop=True).then_inc(S["ln_var_mm"], 1)
                    if c == 1:
                        pe.wait_ge(const_dma, 16 * 2)
                        pe.wait_ge(S["perm_ready"], 1)
                        pe.wait_ge(ff_t, s * KD + 5)
                        pe.wait_ge(S["x_sum"], s * 4 + 4)
                        pe.matmul(psn(2), ONES, XSUM[:, 0, :], start=True, stop=True).then_inc(S["ln_mean_mm"], 1)

                for m in range(KC):
                    for k in range(KD):
                        t = m * KD + k
                        u, v = t // 3, t % 3
                        if v == 0:
                            pe.wait_ge(S["w_lo"], s * SPLIT_UNITS + u + 1)
                        if t == 0:
                            pe.wait_ge(S["y_lo"], s * lows + NG)
                        hi, lo = w_tile(u % WR, v)
                        last = three(psn(4 + m), hi, lo, Y[:, 0, k, :], Y[:, 1, k, :], k == 0, k == KD - 1)
                        if v == 2:
                            last.then_inc(w_used, 1)
                    if m < KC - 1:
                        last.then_inc(S["qc_mm"], 1)
                    if m == 1:
                        pe.wait_ge(row_sum, s * NC + NC + 2)
                        pe.matmul(PS[0:1, 7, :].rearrange("p (b n) -> p b n", b=BPS), C[0:CK, C_W750:C_W750 + 1],
                                  G[0:CK, 0:BPS, 0:KVC], start=True, stop=True).then_inc(mean_mm, 1)

                with pe.Fori(0, PAIRS) as p:
                    pe.wait_ge(S["qc_lo"], s * KC + (KC - 1))

                    def unit_ready(v):
                        pe.wait_ge(S["w_lo"], s * SPLIT_UNITS + p * 4 + (U_PAIR + v + 1))

                    def up(bank, slot):
                        for k in range(KC):
                            if k == KC - 1 and slot == 0:
                                pe.wait_ge(S["qc_lo"], s * KC + KC)
                            hi, lo = w_tile(slot, k)
                            last = three(psn(bank), hi, lo, QCS[:, 0, k, :], QCS[:, 1, k, :], k == 0, k == KC - 1)
                        return last

                    def absorb(h, bank):
                        pe.wait_ge(S["nope_lo"], s * H + p * 2 + h + 1)
                        for d in range(KV):
                            hi, lo = w_tile(3, 2 * h + d)
                            last = three(psn(bank + d), hi, lo, NOPE[:, h, 0, :], NOPE[:, h, 1, :], True, True)
                        return last

                    n = s * PAIRS + p
                    for h in range(2):
                        unit_ready(h)
                        up(h, h).then_inc(w_used, 1)
                    unit_ready(2)
                    pe.wait_ge(rope_t1, n + 1)
                    up(4, 2).then_inc(w_used, 1)
                    unit_ready(3)
                    pe.wait_ge(abs_even, n + 1)
                    absorb(0, 2).then_inc(S["abs_mm"], 1)
                    pe.wait_ge(abs_odd, n + 1)
                    absorb(1, 5).then_inc(S["abs_mm"], 1)
                    pe.wait_ge(S["rp_lo"], n + 1)
                    pe.wait_ge(rope_t2, n + 1)
                    pe.matmul(psn(7), PERM[:, :], RSP[:, 0, :], start=True, stop=False).then_inc(w_used, 1)
                    pe.matmul(psn(7), PERM[:, :], RSP[:, 1, :], start=False, stop=True).then_inc(S["swap_mm"], 1)
                def step(s, i, r):
                    tile = s * NT + i
                    if has(i, 0):
                        pe.wait_ge(g_dma[r], s * (NT // GR * 16) + (i // GR + 1) * 16 if isinstance(i, int) else gd(s, i, r))
                        pe.wait_ge(kt_ev, tile + 1)
                        for w, col in enumerate((0, 2 * R, 2 * R + 128)):
                            last = pe.transpose(PS[:, 0, TK * w:TK * (w + 1)], G[0:TK, r, col:col + 128], IDENT[0:TK, 0:TK])
                        last.then_inc(S["kt_mm"], 1)
                    if has(i, 1):
                        n, q = tile - 1, (r - 1) % GR
                        if isinstance(i, int) and i == 1:
                            pe.wait_ge(abs_even, s * PAIRS + PAIRS + 1)
                            pe.wait_ge(abs_odd, s * PAIRS + PAIRS + 1)
                            pe.wait_ge(rope_ev, s * PAIRS + PAIRS + 1)
                        pe.wait_ge(kt_ev, n + 2)
                        pe.wait_ge(s_ev, n + 1)
                        keys, ps = KT[:, q % 2, :], PS[0:TK, 1 + q % 2, 0:HQ]
                        cols = ds(i * QT_ - QT_, QT_)
                        for d in range(KV):
                            pe.matmul(ps, keys[:, TK * (2 + d):TK * (3 + d)], QL[:, d, :, cols], start=(d == 0), stop=False)
                        for e in range(2):
                            last = pe.matmul(ps[:, PQ * e:PQ * (e + 1)], keys[:, TK * e:TK * (e + 1)], QR[:, :, cols],
                                             start=False, stop=(e == 1))
                        last.then_inc(s_mm, 1)
                    if has(i, 2):
                        n, q = tile - 2, (r - 2) % GR
                        pe.wait_ge(s_ev, n + 3)
                        pe.wait_ge(sm_mask, n + 1)
                        for e in range(2):
                            last = pe.transpose(PS[0:PQ, 3 + q % 2, TK * e:TK * (e + 1)], SSB[0:TK, q % 2, PQ * e:PQ * (e + 1)],
                                                IDENT[0:TK, 0:TK])
                        last.then_inc(st_mm, 1)
                    if has(i, PT_LAG):
                        n, q = tile - PT_LAG, (r - PT_LAG) % GR
                        pe.wait_ge(S["sm_norm"], n + 1)
                        pe.wait_ge(pt_ev, n + 1)
                        for e in range(2):
                            last = pe.transpose(PS[0:TK, 5, PQ * e:PQ * (e + 1)], SM[0:PQ, q % 4, e, :], IDENT[0:PQ, 0:PQ])
                        last.then_inc(pt_mm, 1)
                    if has(i, LAG):
                        n, q = tile - LAG, (r - LAG) % GR
                        pe.wait_ge(pt_ev, n + 2)
                        pe.wait_ge(pv_ev, n + 1)
                        for d in range(KV):
                            last = pe.matmul(PS[:, 6 + q % 2, HQ * d:HQ * (d + 1)], G[0:TK, q, 2 * R + 128 * d:2 * R + 128 * (d + 1)],
                                             PT[0:TK, q % 2, :], start=True, stop=True)
                        last.then_inc(pv_mm, 1)

                def gd(s, i, r):
                    return s * (NT // GR * 16) + (i - r) * 2 + 16

                steps(pe, step, s, NT + LAG)

                for v, (kind, i) in enumerate(OUT_UNITS):
                    slot = v % WR
                    pe.wait_ge(S["w_lo"], s * SPLIT_UNITS + U_WO + v + 1)
                    if kind == "value":
                        pe.wait_ge(S["cs_lo"], sums_count(s, i))
                        pe.wait_ge(att_lo, s * H + i + 1)
                        for d in range(KV):
                            hi, lo = w_tile(slot, d)
                            last = three(psn(i % 2), hi, lo, sums(i)[:, 0, d, :], sums(i)[:, 1, d, :], d == 0, d == KV - 1)
                    else:
                        g, m = i // KD, i % KD
                        pe.wait_ge(x_add, s * (KD * H // G4) + i + 1)
                        for j in range(G4):
                            if m == 0:
                                pe.wait_ge(att_lo, s * H + G4 * g + j + 3)
                            hi, lo = w_tile(slot, j)
                            last = three(psn(4 + m % 4), hi, lo, ATT[:, g % 2, 0, j, :], ATT[:, g % 2, 1, j, :], j == 0, j == G4 - 1)
                    last.then_inc(w_used, 1)

                pe.wait_ge(S["ln_sum"], s + 1)
                pe.matmul(psn(2), ONES, TMP[:, 0, :], start=True, stop=True).then_inc(S["ln_mean_mm"], 1)
                for h in range(2):
                    for k in range(KD):
                        v = KD * h + k
                        if v == KD:
                            pe.wait_ge(S["ln_sqsum"], s * 2 + 2)
                            pe.matmul(psn(3), ONES, TMP[:, 1, :], start=True, stop=True).then_inc(S["ln_var_mm"], 1)
                        pe.wait_ge(w_sgn, s * 16 + v + 5)
                        group = [i for i, (a, _) in enumerate(NORM) if a == k and h == 0]
                        for i in group:
                            pe.wait_ge(S["y_hi"], s * (2 * NG) + (NG + i + 1))
                        order = [(j, part) for j in range(HALF_M) for part in range(2)] if h else [
                            (j, part) for part in range(2) for j in range(HALF_M)]
                        for j, part in order:
                            hi, _ = w_tile(v % WR, j)
                            if group and part == 1 and j == 0:
                                if group[0] in pool_groups:
                                    pe.wait_ge(S["y_lo_pool"], s * 2 + (pool_groups.index(group[0]) + 1))
                                else:
                                    pe.wait_ge(S["y_lo"], s * lows + (NG + dve_groups.index(group[0]) + 1))
                            if h and k == 0 and j == HALF_M - 1 and part == 0:
                                pe.wait_ge(S["ln_ve"], s * 2 + 2)
                            last = pe.matmul(psn(4 * (1 - h) + j), hi, Y[:, part, k, :], start=(k == 0 and part == 0),
                                             stop=(k == KD - 1 and part == 1))
                        last.then_inc(w_used, 1)


def kernel(**inputs):
    import numpy as np
    import concourse.bacc as bacc
    from concourse.bass_utils import run_bass_kernel_spmd

    a = {k.replace("L0_xattn_", "").replace("L0_ffn_", "ffn_"): np.asarray(v) for k, v in inputs.items()}

    def blocks(w, kd, nd):
        return w.reshape(kd, 128, nd, 128).transpose(2, 1, 0, 3)

    heads = [2 * (h % PAIRS) + h // PAIRS for h in range(H)]
    lay = {}
    lay["x"] = a["x"].reshape(NS, N, KD, 128).transpose(0, 3, 2, 1).reshape(NS, 128, KD * N)
    lay["x"] = np.concatenate([lay["x"], np.zeros((1, 128, KD * N), np.float32)])
    lay["ctx"] = a["ctx_2048"].reshape(B * CPB, CK, KD, 128).transpose(0, 3, 2, 1).reshape(B * CPB, 128, KD * CK)
    lay["ctx"] = np.concatenate([lay["ctx"], np.zeros((PREFETCH, 128, KD * CK), np.float32)])
    lay["seg"] = a["itok_BxS_0_1023"].reshape(NS * NT, QT_).T
    lay["kvc"] = a["W_kvc"].reshape(KD, 128, KVC).transpose(1, 0, 2).reshape(128, KD * KVC)
    lay["kvct"] = a["W_kvc"].T.reshape(KV, 128, D).transpose(1, 0, 2).reshape(128, KV * D)
    lay["kr"] = a["W_kr"].reshape(KV, 128, R).transpose(1, 0, 2).reshape(128, KV * R)
    dq = blocks(a["W_dq"], KD, KC)
    lay["dq"] = dq.transpose(0, 2, 1, 3).reshape(8, 3, 128, 128).transpose(0, 2, 1, 3).reshape(8, 128, 384)
    lay["uq"] = blocks(a["W_uq"], KC, H).reshape(H, 128, KC * 128)
    uk = a["W_uk"].reshape(KV, 128, PAIRS, 2, HD)
    lay["uk"] = uk.transpose(2, 4, 3, 0, 1).reshape(PAIRS, 128, 2 * KV * 128)
    lay["qr"] = blocks(a["W_qr"], KC, PAIRS).reshape(PAIRS, 128, KC * 128)
    lay["uv"] = blocks(a["W_uv"], KV, H)[heads].reshape(H, 128, KV * HD)
    wo = a["W_o"].reshape(H, HD, KD, 128)[heads].reshape(H // G4, G4, HD, KD, 128)
    lay["wo"] = wo.transpose(0, 3, 2, 1, 4).reshape(H // G4 * KD, 128, G4 * 128)
    ff = a["ffn_weight"].reshape(2, HALF_M, 128, KD, 128)
    lay["ff"] = ff.transpose(0, 3, 4, 1, 2).reshape(2 * KD, 128, HALF_M * 128)
    lay["ffn"] = a["ffn_weight"].reshape(KD, 128, D).transpose(1, 0, 2).reshape(128, KD * D)
    lay["bias"] = a["ffn_bias"].reshape(KD, 128).T
    lay["cst"], lay["pre"] = constants()

    nc = bacc.Bacc("TRN2", target_bir_lowering=False, num_devices=1)
    arrays, args = {}, []
    for name, v in lay.items():
        v = np.ascontiguousarray(v)
        arrays[f"in_{name}"] = v
        args.append(nc.dram_tensor(f"in_{name}", v.shape, mybir.dt.from_np(v.dtype), kind="ExternalInput").ap())
    out = nc.dram_tensor("out_t", (NS, 128, KD * N), mybir.dt.float32, kind="ExternalOutput").ap()
    program(nc, *args, out)
    r = run_bass_kernel_spmd(nc, [arrays], core_ids=[0])
    y = r.results[0]["out_t"].reshape(NS, 128, KD, N).transpose(0, 3, 2, 1)
    return np.ascontiguousarray(y.reshape(B, LQ, D))
```
